# Optimizing a Trainium2 kernel written in Bass

```python
import numpy as np
import jax
import jax.numpy as jnp

def _softmax(x, axis=-1):
    return jax.nn.softmax(x, axis=axis)

def _gelu(x):
    return jax.nn.gelu(x, approximate=True)

def _silu(x):
    return jax.nn.silu(x)

def _sigmoid(x):
    return jax.nn.sigmoid(x)

def _layernorm(x, axis=-1, eps=1e-05):
    m = jnp.mean(x, axis=axis, keepdims=True)
    v = jnp.var(x, axis=axis, keepdims=True)
    return (x - m) / jnp.sqrt(v + eps)

def _scatter_add(tgt, idx, src, axis=0):
    return tgt.at[idx].add(src)

def _segment_sum(src, seg, n):
    return jax.ops.segment_sum(src, seg, n)
kernel_name = 'mk_vit_tower_postln_d2_tok_img768_r4_273c7a'

def setup_inputs(seed: int=0):
    np.random.seed(seed)
    _w = jnp.asarray

    def _rec_inputs():
        import jax
        import jax.numpy as jnp
        _rk = jax.random.key(seed)
        x = -4.65018e-05 + 0.999886 * jax.random.normal(jax.random.fold_in(_rk, 1), (32, 3, 64, 64), jnp.float32)
        return x
    x = _rec_inputs()

    def _L0_tok_setup():
        import jax, jax.numpy as jnp
        import numpy as np
        PATCH = 16
        EPS = 1e-05

        def _rms_norm(x, w):
            return x * jax.lax.rsqrt(jnp.mean(x * x, axis=-1, keepdims=True) + EPS) * w
        key = jax.random.key(seed)
        k1, k2 = jax.random.split(key)
        B, C, H, W = (64, 3, 128, 128)
        patch_dim = C * PATCH * PATCH
        dim = 192
        x = jax.random.normal(k1, (B, C, H, W), dtype=jnp.float32)
        bound = 1.0 / np.sqrt(patch_dim)
        W_proj = jax.random.uniform(k2, (dim, patch_dim), minval=-bound, maxval=bound, dtype=jnp.float32)
        b_proj = jnp.zeros((dim,), dtype=jnp.float32)
        g_in = jnp.ones((patch_dim,), dtype=jnp.float32)
        g_out = jnp.ones((dim,), dtype=jnp.float32)
        return {'x': x, 'W_proj': W_proj, 'b_proj': b_proj, 'g_in': g_in, 'g_out': g_out}
    _L0_tok_all = _L0_tok_setup()
    _L0_tok_in = {k: v for k, v in _L0_tok_all.items() if k in ('W_proj', 'b_proj', 'g_in', 'g_out')}
    del _L0_tok_all

    def _L0_attn_setup():
        import jax, jax.numpy as jnp
        import numpy as np
        B, T, E, H = (4, 256, 192, 12)
        HD = E // H
        R = 2
        LORA_SCALE = 1.0 / R
        NUM_BUCKETS, MAX_DIST = (80, 200)

        def _rel_bucket(rel):
            nb = NUM_BUCKETS // 2
            buckets = (rel > 0).astype(jnp.int32) * nb
            rel = jnp.abs(rel)
            max_exact = nb // 2
            is_small = rel < max_exact
            log_ratio = jnp.log(jnp.maximum(rel, 1).astype(jnp.float32) / max_exact)
            large = max_exact + (log_ratio / np.log(MAX_DIST / max_exact) * (nb - max_exact)).astype(jnp.int32)
            large = jnp.minimum(large, nb - 1)
            return buckets + jnp.where(is_small, rel, large)
        key = jax.random.key(seed)
        ks = jax.random.split(key, 22)
        s = 0.02
        w = lambda k, shape: jax.random.normal(k, shape, jnp.float32) * s
        return {'hidden_states': jax.random.normal(ks[0], (B, T, E), jnp.float32), 'Wq': w(ks[1], (E, E)), 'bq': w(ks[2], (E,)), 'Wk': w(ks[3], (E, E)), 'bk': w(ks[4], (E,)), 'Wv': w(ks[5], (E, E)), 'bv': w(ks[6], (E,)), 'Aq': w(ks[7], (R, E)), 'Bq': w(ks[8], (E, R)), 'Ak': w(ks[9], (R, E)), 'Bk': w(ks[10], (E, R)), 'Av': w(ks[11], (R, E)), 'Bv': w(ks[12], (E, R)), 'Wo': w(ks[13], (E, E)), 'bo': w(ks[14], (E,)), 'Wg': w(ks[15], (8, HD)), 'bg': w(ks[16], (8,)), 'gru_const': jnp.ones((1, H, 1, 1), jnp.float32), 'rel_embed': w(ks[17], (NUM_BUCKETS, H))}
    _L0_attn_all = _L0_attn_setup()
    _L0_attn_in = {k: v for k, v in _L0_attn_all.items() if k in ('Wq', 'bq', 'Wk', 'bk', 'Wv', 'bv', 'Aq', 'Bq', 'Ak', 'Bk', 'Av', 'Bv', 'Wo', 'bo', 'Wg', 'bg', 'gru_const', 'rel_embed')}
    del _L0_attn_all

    def _L0_ffn_setup():
        import jax, jax.numpy as jnp
        import numpy as np
        D_MODEL, D_FF, N_EXPERTS, TOP_K = (192, 768, 8, 2)
        B, S = (2, 256)
        LN_EPS = 1e-05

        def _layernorm(x, gamma, beta):
            mu = jnp.mean(x, axis=-1, keepdims=True)
            var = jnp.mean(jnp.square(x - mu), axis=-1, keepdims=True)
            return (x - mu) * jax.lax.rsqrt(var + LN_EPS) * gamma + beta
        key = jax.random.key(seed)
        k1, k2, k3, k4 = jax.random.split(key, 4)
        return {'hidden_states': jax.random.normal(k1, (B, S, D_MODEL), dtype=jnp.float32), 'ln_gamma': jnp.ones((D_MODEL,), dtype=jnp.float32), 'ln_beta': jnp.zeros((D_MODEL,), dtype=jnp.float32), 'router_w': jax.random.normal(k2, (D_MODEL, N_EXPERTS), dtype=jnp.float32) * 0.02, 'w1': jax.random.normal(k3, (N_EXPERTS, D_MODEL, D_FF), dtype=jnp.float32) * 0.02, 'w2': jax.random.normal(k4, (N_EXPERTS, D_FF, D_MODEL), dtype=jnp.float32) * 0.02}
    _L0_ffn_all = _L0_ffn_setup()
    _L0_ffn_in = {k: v for k, v in _L0_ffn_all.items() if k in ('ln_gamma', 'ln_beta', 'router_w', 'w1', 'w2')}
    del _L0_ffn_all

    def _L1_attn_setup():
        import jax, jax.numpy as jnp
        import numpy as np
        B, T, D, H, K = (4, 256, 192, 12, 64)
        DMIX, DDEC = (32, 64)
        key = jax.random.key(seed)
        ks = jax.random.split(key, 24)

        def n(k, shape, s=1.0):
            return jax.random.normal(k, shape, dtype=jnp.float32) * s
        return {'x': n(ks[0], (B, T, D)), 'time_maa_x': n(ks[1], (1, 1, D), 0.1) + 0.5, 'time_maa_w': n(ks[2], (1, 1, D), 0.1) + 0.5, 'time_maa_k': n(ks[3], (1, 1, D), 0.1) + 0.5, 'time_maa_v': n(ks[4], (1, 1, D), 0.1) + 0.5, 'time_maa_r': n(ks[5], (1, 1, D), 0.1) + 0.5, 'time_maa_g': n(ks[6], (1, 1, D), 0.1) + 0.5, 'maa_w1': n(ks[7], (D, 5 * DMIX), 0.01), 'maa_w2': n(ks[8], (5, DMIX, D), 0.01), 'time_decay': jnp.linspace(-6.0, -1.0, D).reshape(1, 1, D).astype(jnp.float32), 'decay_w1': n(ks[9], (D, DDEC), 0.01), 'decay_w2': n(ks[10], (DDEC, D), 0.01), 'lucid_temp': jnp.ones((1, H, 1, 1), jnp.float32), 'Wr': n(ks[11], (D, D), 0.02), 'Wk': n(ks[12], (D, D), 0.02), 'Wv': n(ks[13], (D, D), 0.02), 'Wg': n(ks[14], (D, D), 0.02), 'Wo': n(ks[15], (D, D), 0.02), 'ln_w': jnp.ones((D,), jnp.float32), 'ln_b': jnp.zeros((D,), jnp.float32)}
    _L1_attn_all = _L1_attn_setup()
    _L1_attn_in = {k: v for k, v in _L1_attn_all.items() if k in ('time_maa_x', 'time_maa_w', 'time_maa_k', 'time_maa_v', 'time_maa_r', 'time_maa_g', 'maa_w1', 'maa_w2', 'time_decay', 'decay_w1', 'decay_w2', 'lucid_temp', 'Wr', 'Wk', 'Wv', 'Wg', 'Wo', 'ln_w', 'ln_b')}
    del _L1_attn_all

    def _L1_ffn_setup():
        import jax, jax.numpy as jnp
        import numpy as np
        B, S, D = (2, 512, 192)
        E, TOP_K = (8, 2)
        H = 4 * D
        key = jax.random.key(seed)
        ks = jax.random.split(key, 8)
        s_in = 1.0 / np.sqrt(D)
        s_h = 1.0 / np.sqrt(H)
        return {'x': jax.random.normal(ks[0], (B, S, D), dtype=jnp.float32), 'gate_w': jax.random.uniform(ks[1], (D, E), jnp.float32, -s_in, s_in), 'gate_b': jax.random.uniform(ks[2], (E,), jnp.float32, -s_in, s_in), 'w1': jax.random.uniform(ks[3], (E, D, H), jnp.float32, -s_in, s_in), 'b1': jax.random.uniform(ks[4], (E, H), jnp.float32, -s_in, s_in), 'w2': jax.random.uniform(ks[5], (E, H, D), jnp.float32, -s_h, s_h), 'b2': jax.random.uniform(ks[6], (E, D), jnp.float32, -s_h, s_h)}
    _L1_ffn_all = _L1_ffn_setup()
    _L1_ffn_in = {k: v for k, v in _L1_ffn_all.items() if k in ('gate_w', 'gate_b', 'w1', 'b1', 'w2', 'b2')}
    del _L1_ffn_all
    return {'x': x, 'L0_tok_W_proj': _L0_tok_in['W_proj'], 'L0_tok_b_proj': _L0_tok_in['b_proj'], 'L0_tok_g_in': _L0_tok_in['g_in'], 'L0_tok_g_out': _L0_tok_in['g_out'], 'L0_attn_Wq': _L0_attn_in['Wq'], 'L0_attn_bq': _L0_attn_in['bq'], 'L0_attn_Wk': _L0_attn_in['Wk'], 'L0_attn_bk': _L0_attn_in['bk'], 'L0_attn_Wv': _L0_attn_in['Wv'], 'L0_attn_bv': _L0_attn_in['bv'], 'L0_attn_Aq': _L0_attn_in['Aq'], 'L0_attn_Bq': _L0_attn_in['Bq'], 'L0_attn_Ak': _L0_attn_in['Ak'], 'L0_attn_Bk': _L0_attn_in['Bk'], 'L0_attn_Av': _L0_attn_in['Av'], 'L0_attn_Bv': _L0_attn_in['Bv'], 'L0_attn_Wo': _L0_attn_in['Wo'], 'L0_attn_bo': _L0_attn_in['bo'], 'L0_attn_Wg': _L0_attn_in['Wg'], 'L0_attn_bg': _L0_attn_in['bg'], 'L0_attn_gru_const': _L0_attn_in['gru_const'], 'L0_attn_rel_embed': _L0_attn_in['rel_embed'], 'L0_ffn_ln_gamma': _L0_ffn_in['ln_gamma'], 'L0_ffn_ln_beta': _L0_ffn_in['ln_beta'], 'L0_ffn_router_w': _L0_ffn_in['router_w'], 'L0_ffn_w1': _L0_ffn_in['w1'], 'L0_ffn_w2': _L0_ffn_in['w2'], 'L1_attn_time_maa_x': _L1_attn_in['time_maa_x'], 'L1_attn_time_maa_w': _L1_attn_in['time_maa_w'], 'L1_attn_time_maa_k': _L1_attn_in['time_maa_k'], 'L1_attn_time_maa_v': _L1_attn_in['time_maa_v'], 'L1_attn_time_maa_r': _L1_attn_in['time_maa_r'], 'L1_attn_time_maa_g': _L1_attn_in['time_maa_g'], 'L1_attn_maa_w1': _L1_attn_in['maa_w1'], 'L1_attn_maa_w2': _L1_attn_in['maa_w2'], 'L1_attn_time_decay': _L1_attn_in['time_decay'], 'L1_attn_decay_w1': _L1_attn_in['decay_w1'], 'L1_attn_decay_w2': _L1_attn_in['decay_w2'], 'L1_attn_lucid_temp': _L1_attn_in['lucid_temp'], 'L1_attn_Wr': _L1_attn_in['Wr'], 'L1_attn_Wk': _L1_attn_in['Wk'], 'L1_attn_Wv': _L1_attn_in['Wv'], 'L1_attn_Wg': _L1_attn_in['Wg'], 'L1_attn_Wo': _L1_attn_in['Wo'], 'L1_attn_ln_w': _L1_attn_in['ln_w'], 'L1_attn_ln_b': _L1_attn_in['ln_b'], 'L1_ffn_gate_w': _L1_ffn_in['gate_w'], 'L1_ffn_gate_b': _L1_ffn_in['gate_b'], 'L1_ffn_w1': _L1_ffn_in['w1'], 'L1_ffn_b1': _L1_ffn_in['b1'], 'L1_ffn_w2': _L1_ffn_in['w2'], 'L1_ffn_b2': _L1_ffn_in['b2']}

def reference(x, L0_tok_W_proj, L0_tok_b_proj, L0_tok_g_in, L0_tok_g_out, L0_attn_Wq, L0_attn_bq, L0_attn_Wk, L0_attn_bk, L0_attn_Wv, L0_attn_bv, L0_attn_Aq, L0_attn_Bq, L0_attn_Ak, L0_attn_Bk, L0_attn_Av, L0_attn_Bv, L0_attn_Wo, L0_attn_bo, L0_attn_Wg, L0_attn_bg, L0_attn_gru_const, L0_attn_rel_embed, L0_ffn_ln_gamma, L0_ffn_ln_beta, L0_ffn_router_w, L0_ffn_w1, L0_ffn_w2, L1_attn_time_maa_x, L1_attn_time_maa_w, L1_attn_time_maa_k, L1_attn_time_maa_v, L1_attn_time_maa_r, L1_attn_time_maa_g, L1_attn_maa_w1, L1_attn_maa_w2, L1_attn_time_decay, L1_attn_decay_w1, L1_attn_decay_w2, L1_attn_lucid_temp, L1_attn_Wr, L1_attn_Wk, L1_attn_Wv, L1_attn_Wg, L1_attn_Wo, L1_attn_ln_w, L1_attn_ln_b, L1_ffn_gate_w, L1_ffn_gate_b, L1_ffn_w1, L1_ffn_b1, L1_ffn_w2, L1_ffn_b2):
    import jax
    import jax.numpy as jnp

    def _L0_tok_ref(x, W_proj, b_proj, g_in, g_out):
        import jax, jax.numpy as jnp
        import numpy as np
        PATCH = 16
        EPS = 1e-05

        def _rms_norm(x, w):
            return x * jax.lax.rsqrt(jnp.mean(x * x, axis=-1, keepdims=True) + EPS) * w
        B, C, H, W = x.shape
        p = PATCH
        h, w = (H // p, W // p)
        xr = x.reshape(B, C, h, p, w, p)
        xr = jnp.transpose(xr, (0, 2, 4, 3, 5, 1)).reshape(B, h * w, p * p * C)
        xn = _rms_norm(xr, g_in)
        y = jnp.einsum('bnd,ed->bne', xn, W_proj) + b_proj
        return _rms_norm(y, g_out)

    def _L0_attn_ref(hidden_states, Wq, bq, Wk, bk, Wv, bv, Aq, Bq, Ak, Bk, Av, Bv, Wo, bo, Wg, bg, gru_const, rel_embed):
        import jax, jax.numpy as jnp
        import numpy as np
        B, T, E, H = (4, 256, 192, 12)
        HD = E // H
        R = 2
        LORA_SCALE = 1.0 / R
        NUM_BUCKETS, MAX_DIST = (80, 200)

        def _rel_bucket(rel):
            nb = NUM_BUCKETS // 2
            buckets = (rel > 0).astype(jnp.int32) * nb
            rel = jnp.abs(rel)
            max_exact = nb // 2
            is_small = rel < max_exact
            log_ratio = jnp.log(jnp.maximum(rel, 1).astype(jnp.float32) / max_exact)
            large = max_exact + (log_ratio / np.log(MAX_DIST / max_exact) * (nb - max_exact)).astype(jnp.int32)
            large = jnp.minimum(large, nb - 1)
            return buckets + jnp.where(is_small, rel, large)
        Bsz, Tq, _ = hidden_states.shape
        pos = jnp.arange(Tq)
        bucket = _rel_bucket(pos[None, :] - pos[:, None])
        pos_bias = rel_embed[bucket].transpose(2, 0, 1)
        g = hidden_states.reshape(Bsz, Tq, H, HD).transpose(0, 2, 1, 3)
        gp = jnp.einsum('bhtd,ed->bhte', g, Wg) + bg
        gp = gp.reshape(Bsz, H, Tq, 2, 4).sum(-1)
        gates = jax.nn.sigmoid(gp)
        gate_a, gate_b = (gates[..., :1], gates[..., 1:])
        gate = gate_a * (gate_b * gru_const - 1.0) + 2.0
        gated_bias = gate * pos_bias[None]
        lin = lambda x, W, b: jnp.einsum('bte,oe->bto', x, W) + b
        lora = lambda x, A, Bm: jnp.einsum('bte,re,or->bto', x, A, Bm) * LORA_SCALE
        x = hidden_states
        q1 = lin(x, Wq, bq) + lora(x, Aq, Bq)
        k1 = lin(x, Wk, bk) + lora(x, Ak, Bk)
        v1 = lin(x, Wv, bv) + lora(x, Av, Bv)
        q = lin(q1, Wq, bq) * HD ** (-0.5)
        k = lin(k1, Wk, bk)
        v = lin(v1, Wv, bv)
        qh = q.reshape(Bsz, Tq, H, HD).transpose(0, 2, 1, 3)
        kh = k.reshape(Bsz, Tq, H, HD).transpose(0, 2, 1, 3)
        vh = v.reshape(Bsz, Tq, H, HD).transpose(0, 2, 1, 3)
        scores = jnp.einsum('bhqd,bhkd->bhqk', qh, kh) + gated_bias
        attn = jax.nn.softmax(scores, axis=-1)
        ctx = jnp.einsum('bhqk,bhkd->bhqd', attn, vh)
        out = ctx.transpose(0, 2, 1, 3).reshape(Bsz, Tq, E)
        return jnp.einsum('bte,oe->bto', out, Wo) + bo

    def _L0_ffn_ref(hidden_states, ln_gamma, ln_beta, router_w, w1, w2):
        import jax, jax.numpy as jnp
        import numpy as np
        D_MODEL, D_FF, N_EXPERTS, TOP_K = (192, 768, 8, 2)
        B, S = (2, 256)
        LN_EPS = 1e-05

        def _layernorm(x, gamma, beta):
            mu = jnp.mean(x, axis=-1, keepdims=True)
            var = jnp.mean(jnp.square(x - mu), axis=-1, keepdims=True)
            return (x - mu) * jax.lax.rsqrt(var + LN_EPS) * gamma + beta
        Bz, Sz, D = hidden_states.shape
        residual = hidden_states
        x = _layernorm(hidden_states, ln_gamma, ln_beta)
        tokens = x.reshape(-1, D)
        T = tokens.shape[0]
        logits = tokens @ router_w
        probs = jax.nn.softmax(logits, axis=-1)
        topw, topi = jax.lax.top_k(probs, TOP_K)
        topw = topw / jnp.sum(topw, axis=-1, keepdims=True)
        gates = jnp.zeros((T, N_EXPERTS), dtype=tokens.dtype)
        gates = gates.at[jnp.arange(T)[:, None], topi].set(topw)
        h = jnp.einsum('td,edf->etf', tokens, w1)
        h = jax.nn.silu(h)
        y = jnp.einsum('etf,efd->etd', h, w2)
        out = jnp.einsum('te,etd->td', gates, y)
        return residual + out.reshape(Bz, Sz, D)

    def _L1_attn_ref(x, time_maa_x, time_maa_w, time_maa_k, time_maa_v, time_maa_r, time_maa_g, maa_w1, maa_w2, time_decay, decay_w1, decay_w2, lucid_temp, Wr, Wk, Wv, Wg, Wo, ln_w, ln_b):
        import jax, jax.numpy as jnp
        import numpy as np
        B, T, D, H, K = (4, 256, 192, 12, 64)
        DMIX, DDEC = (32, 64)
        Bb, Tt, Dd = x.shape
        Hh = lucid_temp.shape[1]
        Kk = Dd // Hh
        left = jnp.pad(x[:, :-1], ((0, 0), (1, 0), (0, 0)))
        right = jnp.pad(x[:, 1:], ((0, 0), (0, 1), (0, 0)))
        dxprev = 0.5 * (left + right) - x
        xxx = x + dxprev * time_maa_x
        m = jnp.tanh(xxx @ maa_w1).reshape(Bb, Tt, 5, DMIX)
        mm = jnp.einsum('btcd,cde->cbte', m, maa_w2)
        mw, mk, mv, mr, mg = (mm[0], mm[1], mm[2], mm[3], mm[4])
        xw = x + dxprev * (time_maa_w + mw)
        xk = x + dxprev * (time_maa_k + mk)
        xv = x + dxprev * (time_maa_v + mv)
        xr = x + dxprev * (time_maa_r + mr)
        xg = x + dxprev * (time_maa_g + mg)
        r = xr @ Wr
        k = xk @ Wk
        v = xv @ Wv
        g = jax.nn.silu(xg @ Wg)
        w = time_decay + jnp.tanh(xw @ decay_w1) @ decay_w2

        def heads(t):
            return t.reshape(Bb, Tt, Hh, Kk).transpose(0, 2, 1, 3)
        r_h, k_h, v_h = (heads(r), heads(k), heads(v))
        w_h = -jnp.exp(heads(w))
        cs = jnp.cumsum(w_h, axis=2)
        cs_b = cs - w_h
        cs_f_s = jnp.clip(cs - cs[:, :, Tt // 2:Tt // 2 + 1, :], -60.0, 60.0)
        cs_b_s = jnp.clip(cs_b - cs_b[:, :, Tt // 2:Tt // 2 + 1, :], -60.0, 60.0)
        A_fwd = jnp.tril(jnp.einsum('bhtk,bhsk->bhts', r_h * jnp.exp(cs_f_s), k_h * jnp.exp(-cs_f_s)))
        A_bwd = jnp.triu(jnp.einsum('bhtk,bhsk->bhts', r_h * jnp.exp(-cs_b_s), k_h * jnp.exp(cs_b_s)), 1)
        A = A_fwd + A_bwd
        kn = k_h / jnp.maximum(jnp.linalg.norm(k_h, axis=-1, keepdims=True), 1e-12)
        gram = jnp.einsum('bhtk,bhsk->bhts', kn, kn)
        temp = jax.nn.softplus(lucid_temp)
        P = jnp.eye(Tt, dtype=jnp.float32) + jnp.exp(jnp.clip(temp * gram, -20.0, 20.0))
        Pv = jnp.linalg.solve(P, v_h)
        y = jnp.einsum('bhts,bhsk->bhtk', A, Pv)
        y = y.transpose(0, 2, 1, 3)
        eps = 1e-05 * 64.0
        mu = y.mean(axis=-1, keepdims=True)
        var = y.var(axis=-1, keepdims=True)
        yn = (y - mu) / jnp.sqrt(var + eps)
        yn = yn.reshape(Bb, Tt, Dd) * ln_w + ln_b
        return yn * g @ Wo

    def _L1_ffn_ref(x, gate_w, gate_b, w1, b1, w2, b2):
        import jax, jax.numpy as jnp
        import numpy as np
        B, S, D = (2, 512, 192)
        E, TOP_K = (8, 2)
        H = 4 * D
        logits = jnp.einsum('bsd,de->bse', x, gate_w) + gate_b
        top_vals, top_idx = jax.lax.top_k(logits, TOP_K)
        rw = jax.nn.softmax(top_vals, axis=-1)
        onehot = jax.nn.one_hot(top_idx, E, dtype=x.dtype)
        expert_w = jnp.einsum('bske,bsk->bse', onehot, rw)
        h = jax.nn.gelu(jnp.einsum('bsd,edh->bseh', x, w1) + b1, approximate=False)
        y = jnp.einsum('bseh,ehd->bsed', h, w2) + b2
        return jnp.einsum('bse,bsed->bsd', expert_w, y)
    h = _L0_tok_ref(x, L0_tok_W_proj, L0_tok_b_proj, L0_tok_g_in, L0_tok_g_out)
    h = _layernorm(h + _L0_attn_ref(h, L0_attn_Wq, L0_attn_bq, L0_attn_Wk, L0_attn_bk, L0_attn_Wv, L0_attn_bv, L0_attn_Aq, L0_attn_Bq, L0_attn_Ak, L0_attn_Bk, L0_attn_Av, L0_attn_Bv, L0_attn_Wo, L0_attn_bo, L0_attn_Wg, L0_attn_bg, L0_attn_gru_const, L0_attn_rel_embed), axis=-1)
    h = _layernorm(h + _L0_ffn_ref(h, L0_ffn_ln_gamma, L0_ffn_ln_beta, L0_ffn_router_w, L0_ffn_w1, L0_ffn_w2), axis=-1)
    h = _layernorm(h + _L1_attn_ref(h, L1_attn_time_maa_x, L1_attn_time_maa_w, L1_attn_time_maa_k, L1_attn_time_maa_v, L1_attn_time_maa_r, L1_attn_time_maa_g, L1_attn_maa_w1, L1_attn_maa_w2, L1_attn_time_decay, L1_attn_decay_w1, L1_attn_decay_w2, L1_attn_lucid_temp, L1_attn_Wr, L1_attn_Wk, L1_attn_Wv, L1_attn_Wg, L1_attn_Wo, L1_attn_ln_w, L1_attn_ln_b), axis=-1)
    h = _layernorm(h + _L1_ffn_ref(h, L1_ffn_gate_w, L1_ffn_gate_b, L1_ffn_w1, L1_ffn_b1, L1_ffn_w2, L1_ffn_b2), axis=-1)
    return h

_drawn_inputs = setup_inputs


def setup_inputs(seed=0):
    import zlib

    import numpy as np

    out = dict(_drawn_inputs(seed))
    spreads = {'L0_tok_b_proj': (0.0, 0.1),
     'L0_tok_g_in': (1.0, 0.2),
     'L0_tok_g_out': (1.0, 0.2),
     'L0_attn_gru_const': (1.0, 0.6),
     'L0_ffn_ln_gamma': (1.0, 0.6),
     'L0_ffn_ln_beta': (0.0, 0.689),
     'L1_attn_lucid_temp': (1.0, 0.6),
     'L1_attn_ln_w': (1.0, 0.6),
     'L1_attn_ln_b': (0.0, 0.8)}
    factors = {'L0_attn_Wq': 8.0,
     'L0_attn_bq': 8.0,
     'L0_attn_Wk': 8.0,
     'L0_attn_bk': 200.0,
     'L0_attn_Wv': 5.816,
     'L0_attn_bv': 6.864,
     'L0_attn_Aq': 8.0,
     'L0_attn_Bq': 8.0,
     'L0_attn_Ak': 8.0,
     'L0_attn_Bk': 8.0,
     'L0_attn_Av': 8.0,
     'L0_attn_Bv': 8.0,
     'L0_attn_Wo': 4.336,
     'L0_attn_Wg': 67.511,
     'L0_attn_bg': 103.225,
     'L0_attn_rel_embed': 8.0,
     'L1_attn_time_maa_x': 8.0,
     'L1_attn_time_maa_w': 64.0,
     'L1_attn_time_maa_k': 8.0,
     'L1_attn_time_maa_v': 8.0,
     'L1_attn_time_maa_r': 8.0,
     'L1_attn_time_maa_g': 8.0,
     'L1_attn_maa_w1': 8.0,
     'L1_attn_maa_w2': 8.0,
     'L1_attn_time_decay': 52.448,
     'L1_attn_decay_w1': 64.0,
     'L1_attn_decay_w2': 64.0,
     'L1_attn_Wr': 3.014,
     'L1_attn_Wk': 3.066,
     'L1_attn_Wv': 2.954,
     'L1_attn_Wg': 2.892,
     'L1_attn_Wo': 2.76,
     'L1_ffn_b1': 5.222,
     'L1_ffn_b2': 3.77,
     'L0_attn_bo': 5.652}
    for name, (base, spread) in spreads.items():
        noise = np.random.default_rng([zlib.crc32(name.encode()), seed]).standard_normal(out[name].shape)
        drawn = base * np.exp(spread * noise) if base else spread * noise
        out[name] = jnp.asarray(drawn.astype(out[name].dtype))
    for name, factor in factors.items():
        out[name] = (out[name] * factor).astype(out[name].dtype)
    return out
```

```python
from contextlib import ExitStack

import numpy as np
import concourse.bass as bass
from concourse import mybir

F32 = mybir.dt.float32
I32 = mybir.dt.int32
U32 = mybir.dt.uint32
ALU = mybir.AluOpType
ACT = mybir.ActivationFunctionType
AX = mybir.AxisListType

BATCH, T, D, HEADS, HD = 32, 16, 192, 12, 16
TOK = BATCH * T
TILES, HALVES = TOK // 128, 2
HT = TOK // HALVES
BLK = HT // 32
PATCH_DIM, PCH = 768, 6
NEXP, DFF, FCH = 8, 768, 6
D1 = D - 128
SYS = 96
WCOLS = DFF + DFF // 2 + FCH * D
MIX = 5
RMS_EPS, LN_EPS, GN_EPS = 1e-5, 1e-5, 64e-5
MASKED = -1e30
ARENA = 6610

def _columns(*spec):
    at, out = 0, {}
    for name, width in spec:
        out[name] = (at, width)
        at += width
    return out, at


CONST, NCONST = _columns(
    ("ident", 128), ("shift", 128), ("cums", 256), ("headsum", 128), ("head8", 8), ("quad4", 4),
    ("head12", 24), ("off_pair", 32), ("even", 1), ("odd", 1), ("lower", 32), ("upper", 32),
    ("anti16", 128), ("iota8", 8), ("one", 1), ("neghalf", 1), ("eye16", 16))
ROW, NROW = _columns(
    ("b_proj", D), ("g_out", D), ("ln_gamma", D), ("ln_beta", D), ("ln_w", D), ("ln_b", D),
    ("gru", HEADS), ("lucid", HEADS), ("gate_b", NEXP), ("bg", 8))
TOKP, NTOKP = _columns(("w", PCH * D), ("gin", PCH))
ATT0, NATT0 = _columns(("wn", 2 * 3 * (D + 1)), ("wt", 2 * 3 * D), ("wo", 2 * D), ("wg", 16),
                       ("b64", 3 * D), ("rel", T * HEADS))
ATT1, NATT1 = _columns(("maa_w1", 2 * 160), ("maa_w2", 2 * D), ("maa", 12), ("w4", 2 * 4 * D),
                       ("dw1", 2 * 64), ("dw2", D), ("wo", 2 * D), ("router", 16), ("gate", 16), ("b1", NEXP * FCH),
                       ("b2", D))


def vit_tower_kernel(nc, consts, rows, x_t, tok_pack, att0_pack, lora_pack, att1_pack, w_l0, w_l1,
                     p_dram, v_dram, s_dram, out):
    ctx = ExitStack()
    with ctx:
        def sb(name, shape, dt=F32):
            return ctx.enter_context(nc.sbuf_tensor(name, shape, dt))

        def sem(name):
            return ctx.enter_context(nc.semaphore(name))

        bank = [ctx.enter_context(nc.psum_tensor(f"bank{i}", [128, 512], F32)) for i in range(8)]

        arena = sb("arena", [128, ARENA])
        used = [0, 0]

        def shared(layer, shape):
            n = int(np.prod(shape[1:]))
            at = used[layer]
            used[layer] += n
            assert used[layer] <= ARENA, (layer, used)
            names = " ".join(f"a{i}" for i in range(len(shape) - 1))
            ap = arena[0:shape[0], at:at + n]
            if len(shape) == 2:
                return ap
            return ap.rearrange(f"p ({names}) -> p {names}", **{f"a{i}": k for i, k in enumerate(shape[1:])})

        scratch = sb("scratch", [128, 3, BLK * HEADS * 32])
        xt = scratch[:, 0, :].rearrange("p (c n) -> p c n", c=PCH)
        xsq = scratch[:, 1, :].rearrange("p (c n) -> p c n", c=PCH)
        tokp = scratch[:, 2, 0:NTOKP]
        lora = scratch[0:2, 2, NTOKP:NTOKP + 3 * 2 * D]

        con = sb("con", [128, NCONST])
        row = sb("row", [128, NROW])
        att0 = shared(0, [128, NATT0])
        att1 = sb("att1", [128, NATT1])
        wexp = sb("wexp", [128, NEXP, WCOLS])

        def c(name, p=128):
            a, n = CONST[name]
            return con[0:p, a:a + n]

        def r(name):
            a, n = ROW[name]
            return row[:, a:a + n]

        def col(tile_, table, name, p=128):
            a, n = table[name]
            return tile_[0:p, a:a + n]

        wtok = col(tokp, TOKP, "w").rearrange("p (c n) -> p c n", c=PCH)
        gin = col(tokp, TOKP, "gin")
        wn = col(att0, ATT0, "wn").rearrange("p (c j n) -> p c j n", c=2, j=3)
        wt = col(att0, ATT0, "wt").rearrange("p (c j n) -> p c j n", c=2, j=3)
        wo0 = col(att0, ATT0, "wo").rearrange("p (c n) -> p c n", c=2)
        wg = col(att0, ATT0, "wg").rearrange("p (c a b) -> p c a b", c=2, a=2)
        b64 = col(att0, ATT0, "b64").rearrange("p (j n) -> p j n", j=3)
        rel = col(att0, ATT0, "rel")
        router = [col(att1, ATT1, "router").rearrange("p (c n) -> p c n", c=2),
                  col(att1, ATT1, "gate").rearrange("p (c n) -> p c n", c=2)]
        lora_w = lora[:, :].rearrange("p (j a n) -> p j a n", j=3, a=2)
        maa_w1 = col(att1, ATT1, "maa_w1").rearrange("p (c n) -> p c n", c=2)
        maa_w2 = col(att1, ATT1, "maa_w2").rearrange("p (c n) -> p c n", c=2)
        maa = col(att1, ATT1, "maa").rearrange("p (c n) -> p c n", c=2)
        w4 = col(att1, ATT1, "w4").rearrange("p (c j n) -> p c j n", c=2, j=4)
        dw1 = col(att1, ATT1, "dw1").rearrange("p (c n) -> p c n", c=2)
        dw2 = col(att1, ATT1, "dw2")
        wo1 = col(att1, ATT1, "wo").rearrange("p (c n) -> p c n", c=2)
        b1 = col(att1, ATT1, "b1")
        b2 = col(att1, ATT1, "b2", 8)

        h0 = sb("h0", [128, TILES, D])
        h1 = sb("h1", [128, TILES, D])
        h2 = sb("h2", [128, TILES, D])
        h3 = h0
        acc = sb("acc", [128, TILES, D])
        pre = sb("pre", [128, TILES, D])
        xffn = pre
        stats = sb("stats", [128, TILES, 6])
        mv = sb("mv", [128, TILES, 2])
        var_in = sb("var_in", [128, 2, 24])
        rstd = sb("rstd", [128, 2, 24])
        f0 = [sb(f"f0_{n}", [128, HALVES, HT]) for n in ("att", "ffn")] * 2
        f1 = [sb(f"f1_{n}", [128, HALVES, HT]) for n in ("att", "ffn")] * 2
        def expanded(n):
            a = scratch[:, n, 0:BLK * 8 * 32].rearrange("p (b h k) -> p b h k", b=BLK, h=8)
            b = scratch[0:D1, n, BLK * 8 * 32:].rearrange("p (b h k) -> p b h k", b=BLK, h=4)
            return a, b

        fr0 = scratch[:, 1, 0:4 * HT].rearrange("p (b j k) -> p b j k", b=BLK, j=4)
        fr1 = scratch[0:D1 + 1, 1, 4 * HT:8 * HT].rearrange("p (b j k) -> p b j k", b=BLK, j=4)
        ss = sb("ss", [128, 2, 4])
        cw0 = shared(0, [128, 3, D])
        cw1 = shared(0, [128, 3, D])
        wgsum = sb("wgsum", [128, 2, 2])
        wgx = shared(0, [128, 2, HEADS, 2])
        bgs = sb("bgs", [128, 2])
        posb = shared(0, [128, T, HEADS])
        q0 = shared(0, [128, HT])
        q1 = shared(0, [D1, HT])
        vx1 = sb("vx1", [128, BLK, 3, 4, HD])
        gates0 = shared(0, [128, 2, HEADS, 2])
        gate = shared(0, [128, 2, HEADS])
        gbias = shared(0, [128, 2, HEADS, T])
        prob = shared(0, [128, 2, HEADS, 32])
        smax = sb("smax", [128, 2, HEADS])
        atr = sb("atr", [128, HALVES, 2, 3, 128])
        vx, ptr = vx1, atr[:, 0]
        ct0 = sb("ct0", [128, HT])
        ct1 = sb("ct1", [128, HT])
        lg = sb("lg", [128, 2, NEXP])
        top = sb("top", [128, 2, 8])
        topi = sb("topi", [128, 2, 8], U32)
        topf = sb("topf", [128, 2, 2])
        topd = sb("topd", [128, 2, 3])
        hot = sb("hot", [128, 2, 2, NEXP])
        gts = sb("gts", [128, TILES, NEXP])
        gts_t = sb("gts_t", [8, 2, 128])
        hid = scratch[:, 0, :].rearrange("p (a j n) -> p a j n", a=2, j=FCH)
        ysc = sb("ysc", [128, 2, 2, D])
        dx0 = shared(1, [128, HT])
        dx1 = shared(1, [D1, HT])
        xx0 = shared(1, [128, HT])
        xx1 = shared(1, [D1, HT])
        mt0 = shared(1, [128, HT])
        mt1 = shared(1, [32, HT])
        xc0 = shared(1, [128, MIX, HT])
        xc1 = shared(1, [D1, MIX, HT])
        t1 = shared(1, [128, HT])
        ew = shared(1, [128, 2, D])
        sysm_all = sb("sysm", [128, 2, T, T + HD])
        cs0 = sysm_all[:, 0].rearrange("p t k -> p (t k)").rearrange("p (i d k) -> p i d k", i=2, d=2)
        cs1 = sysm_all[0:D1, 1].rearrange("p t k -> p (t k)").rearrange("p (i d k) -> p i d k", i=2, d=2)
        xc_all = xc0.rearrange("p m n -> p (m n)")
        ex0 = xc_all[:, 0:4 * HT].rearrange("p (a i k) -> p a i k", a=4, i=2)
        ex1 = xc1.rearrange("p m n -> p (m n)")[:, 0:4 * HT].rearrange("p (a i k) -> p a i k", a=4, i=2)
        rt0 = shared(1, [128, HT])
        rt1 = shared(1, [D1, HT])
        kt0 = shared(1, [128, HT])
        kt1 = shared(1, [D1, HT])
        ksq0 = xx0
        ksq1 = xx1
        kn0 = dx0
        kn1 = dx1
        vs = shared(1, [128, 2, D])
        sg = sb("sg", [128, HALVES, 2, D])
        amix = sb("amix", [128, 2, HEADS, 32])
        gram = acc[:].rearrange("p a n -> p (a n)").rearrange("p (i h k) -> p i h k", i=2, h=HEADS)
        pmat = shared(1, [128, 2, HEADS, T])
        temp = sb("temp", [128, 3, HEADS])
        sysm = sysm_all[0:SYS]
        prod = scratch[0:SYS, 2, 0:2 * T * (T + HD)].rearrange("p (i t k) -> p i t k", i=2, t=T)
        piv = sb("piv", [SYS, 2])
        gsum = sb("gsum", [128, 24])
        gsq = ysc[:, 0]

        names = """ld_const ld_row ld_tok ld_att0 ld_att1 st_out
            wtok_scaled xsq_ready tok_y tok_ss y_ready y_sq2 h0_ready wo_read wo1_read g_raw
            lora_mm wn_ready comp_mm posb_mm comp_ready ones_set
            a0_tr a0_ft a0_q a0_k a0_v a0_gate q_ready kx_ready vx_ready gate_in gate_exp
            a0_s s_shift s_exp p_ready a0_pt pt_ready a0_ctx ct_ready a0_wo
            x_ready ff_tr ff_ft ff_lg top_in top_exp gts_ready gt_tr gt_ev b2_mm acc_init
            h_mm h_act y_mm y_act acc_add
            h2_ready a1_tr a1_ft a1_dx a1_xx a1_mt mt_ready a1_mm a1_xd xc_ready
            a1_t1 t1_ready a1_w ew_ready a1_cs cs_ready ex_ready a1_rk rk_ready a1_vg v_ready g_ready
            ksq_ready a1_n2 n2_ready kn_ready a1_gram a1_af a1_ab decay_ops gram_in gram_exp p_mat
            a_mix a1_at at_ready st_p st_v ld_g st_s ld_s solved vx1_zero
            a1_y y_in y_sq gn_ready a1_ytr yt_ready a1_wo h3_ready out_ready
            var_ready rstd_ready temp_in temp_out t1_ones amix_zero fr_ready dve_chain act_chain pool_chain""".split()
        S = {n: sem(n) for n in names}
        ld_x = [sem(f"ld_x{ch}") for ch in range(PCH)]
        ld_w = [[sem(f"ld_w{l}_{e}") for e in range(NEXP)] for l in range(2)]
        order = ["tok1", "tok2", "a0_0", "f0_0", "a0_1", "f0_1", "h2_0", "h2_1", "gn_0", "h3_0",
                 "out_0", "gn_1", "h3_1", "out_1"]
        width = {"tok1": 4, "tok2": 4, "gn_0": 24, "gn_1": 24}

        block = ctx.enter_context(nc.Block())

        def units(m):
            return (3 * (m + 1) + 1) // 2

        def bc(ap, axis, n):
            a = ap.unsqueeze(axis)
            shape = list(a.shape)
            shape[axis] = n
            return a.broadcast_to(shape)

        @block.sync
        def _(sp):
            sp.dma_start(tokp[:], tok_pack).then_inc(S["ld_tok"], 16)
            for ch in range(PCH):
                sp.dma_start(xt[:, ch, :], x_t[:, ch * TOK:(ch + 1) * TOK]).then_inc(ld_x[ch], 16)
            for e in range(NEXP):
                sp.dma_start(wexp[:, e, :], w_l0[e]).then_inc(ld_w[0][e], 16)
            for s in range(HALVES):
                for i in range(2):
                    t = 2 * s + i
                    if i == 0:
                        sp.wait_ge(S["v_ready"], s + 1)
                        for j in range(2):
                            sp.dma_start(v_dram[2 * s + j], vs[:, j, :]).then_inc(S["st_v"], 16)
                    sp.wait_ge(S["p_mat"], t + 1)
                    sp.dma_start(p_dram[t], pmat[:, i, :, :].rearrange("p h k -> p (h k)")).then_inc(S["st_p"], 16)
                sp.wait_ge(S["st_v"], 32 * (s + 1))
                sp.wait_ge(S["st_p"], 32 * (s + 1))
                if s:
                    sp.wait_ge(S["st_s"], 32 * s)
                for i in range(2):
                    t = 2 * s + i
                    for b in range(8):
                        src = p_dram[t, b * T:(b + 1) * T, :].rearrange("t (h k) -> h t k", h=HEADS)
                        sp.dma_start(sysm[b * HEADS:(b + 1) * HEADS, i, :, 0:T], src).then_inc(S["ld_g"], 16)
                        src = v_dram[t, b * T:(b + 1) * T, :].rearrange("t (h k) -> h t k", h=HEADS)
                        sp.dma_start(sysm[b * HEADS:(b + 1) * HEADS, i, :, T:], src).then_inc(S["ld_g"], 16)
                sp.wait_ge(S["solved"], s + 1)
                for i in range(2):
                    t = 2 * s + i
                    sp.dma_start(s_dram[t].rearrange("q (t k) -> q t k", t=T), sysm[:, i, :, T:]).then_inc(S["st_s"], 16)
                sp.wait_ge(S["st_s"], 32 * (s + 1))
                if s:
                    sp.wait_ge(S["a1_y"], s)
                else:
                    sp.wait_ge(S["vx1_zero"], 1)
                for i in range(2):
                    t = 2 * s + i
                    sol = s_dram[t].rearrange("(a b g j) (t k) -> j b t a g k", a=4, b=2, g=3, j=4, t=T)
                    for j in range(4):
                        for b in range(2):
                            for g in range(3):
                                sp.dma_start(vx1[32 * j + T * b:32 * j + T * (b + 1), 4 * i:4 * i + 4, g, j, :],
                                             sol[j, b, :, :, g, :]).then_inc(S["ld_s"], 16)
            for s in range(HALVES):
                sp.wait_ge(S["out_ready"], s + 1)
                for i in range(2):
                    t = 2 * s + i
                    sp.dma_start(out[t], pre[:, t, :]).then_inc(S["st_out"], 16)
            sp.wait_ge(S["st_out"], 16 * TILES)

        @block.tensor
        def _(pe):
            mm = nc.tensor.matmul

            def tokens():
                pe.wait_ge(S["ld_const"], 16)
                pe.wait_ge(S["wtok_scaled"], 1)
                for ch in range(PCH):
                    pe.wait_ge(ld_x[ch], 16)
                for t in range(TILES):
                    for ch in range(PCH):
                        last = mm(bank[t // 2][:, (t % 2) * D:(t % 2 + 1) * D], xt[:, ch, t * 128:(t + 1) * 128],
                                  wtok[:, ch, :], start=ch == 0, stop=ch == PCH - 1)
                last.then_inc(S["tok_y"], 1)
                pe.wait_ge(S["xsq_ready"], PCH)
                for t in range(TILES):
                    for ch in range(PCH):
                        last = mm(bank[2][:, t:t + 1], xsq[:, ch, t * 128:(t + 1) * 128], c("one"),
                                  start=ch == 0, stop=ch == PCH - 1)
                last.then_inc(S["tok_ss"], 1)

            def composites():
                pe.wait_ge(S["ld_att0"], 32)
                for j in range(3):
                    mm(bank[3 + j][:, 0:D], lora_w[:, j, 0, 0:128], lora_w[:, j, 1, :], start=True, stop=True)
                    last = mm(bank[3 + j][0:D1, D:2 * D], lora_w[:, j, 0, 128:D], lora_w[:, j, 1, :],
                              start=True, stop=True)
                last.then_inc(S["lora_mm"], 1)
                pe.wait_ge(S["wn_ready"], 1)
                for j in range(3):
                    for e0, e1, o in ((0, 128, 0), (128, D + 1, D)):
                        mm(bank[3 + j][0:e1 - e0, o:o + D], wn[:, 0, j, e0:e1], wt[:, 0, j, :],
                           start=True, stop=False)
                        last = mm(bank[3 + j][0:e1 - e0, o:o + D], wn[0:D1, 1, j, e0:e1], wt[0:D1, 1, j, :],
                                  start=False, stop=True)
                last.then_inc(S["comp_mm"], 1)
                mm(bank[6][:, 0:T * HEADS], c("anti16", T), rel[0:T, :], start=True, stop=True).then_inc(S["posb_mm"], 1)

            def transpose_half(src, s, dst):
                for i in range(2):
                    t = 2 * s + i
                    nc.tensor.transpose(dst[:, i * 128:(i + 1) * 128], src[:, t, 0:128], c("ident"))
                    tail = src[:, t, 128:D]
                    last = nc.tensor.transpose(dst[0:D1, HT + i * 128:HT + (i + 1) * 128], tail, c("ident"))
                return last

            def attention0(s):
                pe.wait_ge(S["h0_ready"], s + 1)
                if s:
                    pe.wait_ge(S["wo_read"], s)
                transpose_half(h0, s, bank[0]).then_inc(S["a0_tr"], 1)
                pe.wait_ge(S["a0_ft"], 2 * (s + 1))
                pe.wait_ge(S["comp_ready"], 1)
                pe.wait_ge(S["ones_set"], 2)
                fa, fb = f0[0][:, s, :], f1[0][0:D1 + 1, s, :]
                for j in range(2):
                    for lo, hi, o in ((0, 128, 0), (128, D, HT)):
                        mm(bank[1 + j][0:hi - lo, o:o + HT], cw0[:, j, lo:hi], fa, start=True, stop=False)
                        last = mm(bank[1 + j][0:hi - lo, o:o + HT], cw1[0:D1 + 1, j, lo:hi], fb,
                                  start=False, stop=True)
                    last.then_inc(S["a0_q" if j == 0 else "a0_k"], 1)
                for i in range(2):
                    mm(bank[7][:, i * 24:(i + 1) * 24], fa[:, i * 128:(i + 1) * 128],
                       wgx[:, 0, :, :].rearrange("p h a -> p (h a)"), start=True, stop=False)
                    last = mm(bank[7][:, i * 24:(i + 1) * 24], fb[0:D1, i * 128:(i + 1) * 128],
                              wgx[0:D1, 1, :, :].rearrange("p h a -> p (h a)"), start=False, stop=True)
                last.then_inc(S["a0_gate"], 1)
                pe.wait_ge(S["fr_ready"], s + 1)
                for b in range(BLK):
                    o = bank[3 + b // 2][:, (b % 2) * D:(b % 2 + 1) * D]
                    mm(o, fr0[:, b].rearrange("p j k -> p (j k)"), cw0[:, 2, :], start=True, stop=False)
                    last = mm(o, fr1[:, b].rearrange("p j k -> p (j k)"), cw1[0:D1 + 1, 2, :], start=False, stop=True)
                last.then_inc(S["a0_v"], 1)
                pe.wait_ge(S["q_ready"], 2 * (s + 1))
                pe.wait_ge(S["kx_ready"], 2 * (s + 1))
                kxa, kxb = expanded(0)
                for i in range(2):
                    for b in range(4):
                        o, n = bank[i][32 * b:32 * b + 32, :], 4 * i + b
                        mm(o[:, 0:256], q0[:, 32 * n:32 * n + 32], kxa[:, n].rearrange("p h k -> p (h k)"),
                           start=True, stop=True)
                        last = mm(o[:, 256:384], q1[:, 32 * n:32 * n + 32], kxb[:, n].rearrange("p h k -> p (h k)"),
                                  start=True, stop=True)
                    last.then_inc(S["a0_s"], 1)
                for i in range(2):
                    pe.wait_ge(S["p_ready"], 2 * s + i + 1)
                    p = prob[:, i].rearrange("p h k -> p (h k)")
                    for g in range(3):
                        last = nc.tensor.transpose(bank[2 + 5 * i][:, g * 128:(g + 1) * 128],
                                                   p[:, g * 128:(g + 1) * 128], c("ident"))
                    last.then_inc(S["a0_pt"], 1)
                pe.wait_ge(S["vx_ready"], 4 * (s + 1))
                for i in range(2):
                    pe.wait_ge(S["pt_ready"], 2 * s + i + 1)
                    for b in range(4):
                        n = 4 * i + b
                        for g in range(3):
                            o = bank[3][64 * (g % 2):64 * (g % 2) + 64, HT * (g // 2) + 32 * n:HT * (g // 2) + 32 * n + 32]
                            last = mm(o, vx[:, n, g].rearrange("p h k -> p (h k)"), ptr[:, i, g, 32 * b:32 * b + 32],
                                      start=True, stop=True)
                last.then_inc(S["a0_ctx"], 1)
                pe.wait_ge(S["ct_ready"], 2 * (s + 1))
                for i in range(2):
                    o = bank[4][:, i * D:(i + 1) * D]
                    mm(o, ct0[:, i * 128:(i + 1) * 128], wo0[:, 0, :], start=True, stop=False)
                    last = mm(o, ct1[0:D1 + 1, i * 128:(i + 1) * 128], wo0[0:D1 + 1, 1, :], start=False, stop=True)
                last.then_inc(S["a0_wo"], 1)

            def route(l, s):
                n = 2 * l + s
                if l == 0:
                    pe.wait_ge(S["x_ready"], s + 1)
                else:
                    pe.wait_ge(S["h3_ready"], s + 1)
                if n == 0:
                    pe.wait_ge(S["ld_att1"], 16)
                transpose_half(xffn if l == 0 else h3, s, bank[5]).then_inc(S["ff_tr"], 1)
                pe.wait_ge(S["ff_ft"], 3 * (n + 1))
                for i in range(2):
                    o = bank[6][:, i * NEXP:(i + 1) * NEXP]
                    mm(o, f0[1 + 2 * l][:, s, i * 128:(i + 1) * 128], router[l][:, 0, :], start=True, stop=False)
                    last = mm(o, f1[1 + 2 * l][0:D1, s, i * 128:(i + 1) * 128], router[l][0:D1, 1, :],
                              start=False, stop=True)
                last.then_inc(S["ff_lg"], 1)
                if l:
                    pe.wait_ge(S["gts_ready"], n + 1)
                    for i in range(2):
                        last = nc.tensor.transpose(bank[7][0:NEXP, i * 128:(i + 1) * 128], gts[:, 2 * s + i, :], c("ident"))
                    last.then_inc(S["gt_tr"], 1)
                    pe.wait_ge(S["gt_ev"], s + 1)
                    for i in range(2):
                        last = mm(bank[6][:, i * D:(i + 1) * D], gts_t[:, i, :], b2, start=True, stop=True)
                    last.then_inc(S["b2_mm"], 1)

            def up(l, s, e):
                ph = 2 * l + s
                pe.wait_ge(ld_w[l][e], 16)
                fa, fb = f0[1 + 2 * l][:, s, :], f1[1 + 2 * l][:, s, :]
                for jp in range(3):
                    n = (ph * NEXP + e) * 3 + jp
                    if n >= 6 and n % 2 == 0:
                        pe.wait_ge(S["h_act"], 2 * (n // 2 - 2))
                    outs = [bank[2 * (n // 2 % 3) + a][:, (n % 2) * HT:(n % 2 + 1) * HT] for a in range(2)]
                    for a in range(2):
                        j = 2 * jp + a
                        mm(outs[a], wexp[:, e, j * 128:(j + 1) * 128], fa, start=True, stop=False)
                    for a in range(2):
                        o = DFF + jp * 128
                        last = mm(outs[a], wexp[64 * a:64 * a + 64, e, o:o + 128], fb[64 * a:64 * a + 64, :],
                                  start=False, stop=True)
                    if n % 2:
                        last.then_inc(S["h_mm"], 1)

            def down(l, s, e):
                n = (2 * l + s) * NEXP + e
                pe.wait_ge(S["h_act"], 2 * units(n))
                if n >= 2:
                    pe.wait_ge(S["y_act"], n - 1)
                w2 = wexp[:, e, DFF + DFF // 2:].rearrange("p (j n) -> p j n", j=FCH)
                for i in range(2):
                    for j in range(FCH):
                        last = mm(bank[6 + n % 2][:, i * D:(i + 1) * D], hid[:, n % 2, j, i * 128:(i + 1) * 128],
                                  w2[:, j, :], start=j == 0, stop=j == FCH - 1)
                last.then_inc(S["y_mm"], 1)

            def experts(l, s):
                n = 2 * l + s
                pe.wait_ge(S["acc_init"], n + 1)
                if n == 0:
                    pe.wait_ge(S["wo_read"], HALVES)
                for e in range(NEXP):
                    up(l, s, e)
                    if e:
                        down(l, s, e - 1)
                down(l, s, NEXP - 1)

            def pre1(s):
                pe.wait_ge(S["h2_ready"], s + 1)
                transpose_half(h2, s, bank[0]).then_inc(S["a1_tr"], 1)
                for i in range(2):
                    t = 2 * s + i
                    mm(bank[1][:, i * 128:(i + 1) * 128], h2[:, t, 0:128], c("shift"), start=True, stop=True)
                    last = mm(bank[1][0:D1, HT + i * 128:HT + (i + 1) * 128], h2[:, t, 128:D], c("shift"),
                              start=True, stop=True)
                last.then_inc(S["a1_dx"], 1)
                pe.wait_ge(S["a1_xx"], s + 1)
                if s:
                    pe.wait_ge(S["wo1_read"], s)
                for lo, hi, o in ((0, 128, 0), (128, 160, HT)):
                    mm(bank[2][0:hi - lo, o:o + HT], maa_w1[:, 0, lo:hi], xx0[:], start=True, stop=False)
                    last = mm(bank[2][0:hi - lo, o:o + HT], maa_w1[0:D1, 1, lo:hi], xx1[:], start=False, stop=True)
                last.then_inc(S["a1_mt"], 1)
                pe.wait_ge(S["mt_ready"], 2 * (s + 1))
                for m in range(MIX):
                    p = 32 * (m % 4)
                    w = maa_w2[p:p + 32, m // 4, :]
                    x = mt0[p:p + 32, :] if m < 4 else mt1[:]
                    mm(bank[3 + m][:, 0:HT], w[:, 0:128], x, start=True, stop=True)
                    mm(bank[3 + m][0:D1, HT:], w[:, 128:D], x, start=True, stop=True).then_inc(S["a1_mm"], 1)
                pe.wait_ge(S["xc_ready"], MIX * s + 1)
                mm(bank[0][0:64, 0:HT], dw1[:, 0, :], xc0[:, 0, :], start=True, stop=False)
                mm(bank[0][0:64, 0:HT], dw1[0:D1, 1, :], xc1[:, 0, :], start=False, stop=True).then_inc(S["a1_t1"], 1)
                pe.wait_ge(S["xc_ready"], MIX * s + 2)
                for m, w, bk in ((1, 1, 2), (3, 0, 3)):
                    if m == 3:
                        pe.wait_ge(S["xc_ready"], MIX * s + 4)
                    for lo, hi, o in ((0, 128, 0), (128, D, HT)):
                        mm(bank[bk][0:hi - lo, o:o + HT], w4[:, 0, w, lo:hi], xc0[:, m, :], start=True, stop=False)
                        last = mm(bank[bk][0:hi - lo, o:o + HT], w4[0:D1, 1, w, lo:hi], xc1[:, m, :],
                                  start=False, stop=True)
                    last.then_inc(S["a1_rk"], 1)
                pe.wait_ge(S["xc_ready"], MIX * s + 5)
                for m, w, bk in ((2, 2, 4), (4, 3, 5)):
                    for i in range(2):
                        o = bank[bk][:, i * D:(i + 1) * D]
                        mm(o, xc0[:, m, i * 128:(i + 1) * 128], w4[:, 0, w, :], start=True, stop=False)
                        last = mm(o, xc1[:, m, i * 128:(i + 1) * 128], w4[0:D1, 1, w, :], start=False, stop=True)
                    last.then_inc(S["a1_vg"], 1)
                pe.wait_ge(S["t1_ready"], s + 1)
                pe.wait_ge(S["t1_ones"], 1)
                for i in range(2):
                    last = mm(bank[1][:, i * D:(i + 1) * D], t1[0:65, i * 128:(i + 1) * 128], dw2[0:65, :],
                              start=True, stop=True)
                last.then_inc(S["a1_w"], 1)
                pe.wait_ge(S["ksq_ready"], s + 1)
                mm(bank[6][:, 0:HT], c("headsum"), ksq0[:], start=True, stop=True)
                mm(bank[6][0:D1, HT:], c("headsum", D1)[:, 0:D1], ksq1[:], start=True, stop=True).then_inc(S["a1_n2"], 1)
                pe.wait_ge(S["ew_ready"], s + 1)
                for i in range(2):
                    mm(bank[7][:, i * 256:(i + 1) * 256], ew[:, i, 0:128], c("cums"), start=True, stop=True)
                    last = mm(bank[0][0:D1, i * 256:(i + 1) * 256], ew[:, i, 128:D], c("cums"), start=True, stop=True)
                last.then_inc(S["a1_cs"], 1)
                for m, (l0, l1, ready, bk) in enumerate(((kn0, kn1, "kn_ready", 1), (ex0, ex1, "decay_ops", 3),
                                                         (ex0, ex1, "decay_ops", 5))):
                    pe.wait_ge(S[ready], s + 1)
                    if m == 1:
                        pe.wait_ge(S["v_ready"], s + 1)
                        pe.wait_ge(S["g_raw"], s + 1)
                    xa, xb = expanded(m)
                    for i in range(2):
                        for b in range(4):
                            n = 4 * i + b
                            o = bank[bk + i][32 * b:32 * b + 32, :]
                            if m == 0:
                                a, d = l0[:, 32 * n:32 * n + 32], l1[:, 32 * n:32 * n + 32]
                            else:
                                a, d = l0[:, m - 1, i, 32 * b:32 * b + 32], l1[:, m - 1, i, 32 * b:32 * b + 32]
                            mm(o[:, 0:256], a, xa[:, n].rearrange("p h k -> p (h k)"), start=True, stop=True)
                            last = mm(o[:, 256:384], d, xb[:, n].rearrange("p h k -> p (h k)"), start=True, stop=True)
                        last.then_inc(S[("a1_gram", "a1_af", "a1_ab")[m]], 1)
                for i in range(2):
                    pe.wait_ge(S["a_mix"], 2 * s + i + 1)
                    a = amix[:, i].rearrange("p h k -> p (h k)")
                    for g in range(3):
                        last = nc.tensor.transpose(bank[1 + i][:, g * 128:(g + 1) * 128], a[:, g * 128:(g + 1) * 128],
                                                   c("ident"))
                    last.then_inc(S["a1_at"], 1)
                pe.wait_ge(S["at_ready"], 2 * (s + 1))

            def post1(s):
                pe.wait_ge(S["ld_s"], 16 * 48 * (s + 1))
                pe.wait_ge(S["h_act"], 3 * NEXP * (2 + s))
                for i in range(2):
                    for b in range(4):
                        n = 4 * i + b
                        for g in range(3):
                            last = mm(bank[0][32 * b:32 * b + 32, i * D + g * 64:i * D + (g + 1) * 64],
                                      atr[:, s, i, g, 32 * b:32 * b + 32], vx1[:, n, g].rearrange("p h k -> p (h k)"),
                                      start=True, stop=True)
                last.then_inc(S["a1_y"], 1)
                pe.wait_ge(S["gn_ready"], s + 1)
                transpose_half(gsq, 0, bank[1]).then_inc(S["a1_ytr"], 1)
                pe.wait_ge(S["yt_ready"], 2 * (s + 1))
                for i in range(2):
                    o = bank[2][:, i * D:(i + 1) * D]
                    mm(o, ct0[:, i * 128:(i + 1) * 128], wo1[:, 0, :], start=True, stop=False)
                    last = mm(o, ct1[0:D1, i * 128:(i + 1) * 128], wo1[0:D1, 1, :], start=False, stop=True)
                last.then_inc(S["a1_wo"], 1)

            tokens()
            composites()
            attention0(0)
            attention0(1)
            route(0, 0)
            experts(0, 0)
            pre1(0)
            route(0, 1)
            experts(0, 1)
            post1(0)
            pre1(1)
            route(1, 0)
            experts(1, 0)
            post1(1)
            route(1, 1)
            experts(1, 1)

        @block.scalar
        def _(act):
            chain = [0]

            def link(ins):
                chain[0] += 1
                ins.then_inc(S["act_chain"], 1)
                act.wait_ge(S["act_chain"], chain[0])

            f = nc.scalar.activation

            def loads():
                act.dma_start(con[:], consts).then_inc(S["ld_const"], 16)
                act.dma_start(row[:], rows.partition_broadcast(128)).then_inc(S["ld_row"], 16)
                act.dma_start(att0[:], att0_pack).then_inc(S["ld_att0"], 16)
                act.dma_start(lora[:], lora_pack).then_inc(S["ld_att0"], 16)
                act.dma_start(att1[:], att1_pack).then_inc(S["ld_att1"], 16)

            def tokens():
                for ch in range(PCH):
                    act.wait_ge(ld_x[ch], 16)
                    f(xsq[:, ch, :], xt[:, ch, :], ACT.Square).then_inc(S["xsq_ready"], 1)
                for t in range(TILES):
                    act.wait_ge(S["y_ready"], t + 1)
                    f(pre[:, t, :], h0[:, t, :], ACT.Square, accum_out=ss[:, 1, t:t + 1]).then_inc(S["y_sq2"], 1)

            def copy_ft(n, s, src, ready, got, inc, full=False):
                act.wait_ge(S[ready], got)
                f(f0[n][:, s, :], src[:, 0:HT], ACT.Copy).then_inc(S[inc], 1)
                f(f1[n][0:D1, s, :], src[0:D1, HT:2 * HT], ACT.Copy).then_inc(S[inc], 1)
                if full:
                    f(f1[n][D1:128, s, :], src[0:D1, HT:2 * HT], ACT.Copy).then_inc(S[inc], 1)

            def attention0(s):
                copy_ft(0, s, bank[0], "a0_tr", s + 1, "a0_ft")
                act.wait_ge(S["a0_q"], s + 1)
                f(q0[:], bank[1][:, 0:HT], ACT.Copy).then_inc(S["q_ready"], 1)
                f(q1[:], bank[1][0:D1, HT:], ACT.Copy).then_inc(S["q_ready"], 1)
                act.wait_ge(S["gate_in"], s + 1)
                g = gates0[:].rearrange("p i h a -> p (i h a)")
                f(g, g, ACT.Exp, scale=-1.0).then_inc(S["gate_exp"], 1)
                for i in range(2):
                    act.wait_ge(S["s_shift"], 2 * s + i + 1)
                    p = prob[:, i].rearrange("p h k -> p (h k)")
                    f(p, p, ACT.Exp).then_inc(S["s_exp"], 1)
                for i in range(2):
                    act.wait_ge(S["a0_pt"], 2 * s + i + 1)
                    f(ptr[:, i].rearrange("p g k -> p (g k)"), bank[2 + 5 * i][:, 0:384], ACT.Copy)\
                        .then_inc(S["pt_ready"], 1)
                act.wait_ge(S["a0_ctx"], s + 1)
                f(ct0[:], bank[3][:, 0:HT], ACT.Copy).then_inc(S["ct_ready"], 1)
                f(ct1[0:D1, :], bank[3][0:D1, HT:], ACT.Copy).then_inc(S["ct_ready"], 1)

            def route(l, s):
                n = 2 * l + s
                copy_ft(1 + 2 * l, s, bank[5], "ff_tr", n + 1, "ff_ft", full=True)
                act.wait_ge(S["top_in"], n + 1)
                f(topd[:, :, 1:2], topd[:, :, 0:1], ACT.Exp).then_inc(S["top_exp"], 1)
                if l:
                    act.wait_ge(S["gt_tr"], s + 1)
                    f(gts_t[:].rearrange("p i k -> p (i k)"), bank[7][0:NEXP, 0:256], ACT.Copy).then_inc(S["gt_ev"], 1)

            def up(l, s, u):
                u += (2 * l + s) * 12
                m = (2 * u + 1) // 3
                if m >= 2:
                    act.wait_ge(S["y_mm"], m - 1)
                act.wait_ge(S["h_mm"], u + 1)
                chunks = hid.rearrange("p a j n -> p (a j) n")
                for a in range(2):
                    src = bank[2 * (u % 3) + a]
                    if l == 0:
                        at = 4 * (u % 3) + a
                        f(chunks[:, at:at + 3:2, :], src[:].rearrange("p (j n) -> p j n", j=2), ACT.Silu)\
                            .then_inc(S["h_act"], 1)
                    else:
                        for j in range(2):
                            ch = 4 * u + a + 2 * j
                            ins = f(chunks[:, ch % 12, :], src[:, j * HT:(j + 1) * HT], ACT.Gelu,
                                    bias=b1[:, ch % (NEXP * FCH):ch % (NEXP * FCH) + 1])
                        ins.then_inc(S["h_act"], 1)

            def down(l, s, e):
                m = (2 * l + s) * NEXP + e
                act.wait_ge(S["y_mm"], m + 1)
                if m >= 2:
                    act.wait_ge(S["acc_add"], m - 1)
                for i in range(2):
                    ins = f(ysc[:, m % 2, i, :], bank[6 + m % 2][:, i * D:(i + 1) * D], ACT.Copy,
                            scale=gts[:, 2 * s + i, e:e + 1])
                ins.then_inc(S["y_act"], 1)
                if l == 0 and s == 1:
                    act.dma_start(wexp[:, e, :], w_l1[e]).then_inc(ld_w[1][e], 16)

            def experts(l, s):
                act.wait_ge(S["gts_ready"], 2 * l + s + 1)
                done = 0
                for e in range(NEXP):
                    while done < 3 * (e + 1) // 2:
                        up(l, s, done)
                        done += 1
                    if e:
                        down(l, s, e - 1)
                down(l, s, NEXP - 1)

            def temperature():
                act.wait_ge(S["temp_in"], 1)
                link(f(temp[:, 1, :], temp[:, 0, :], ACT.Exp, scale=-1.0))
                f(temp[:, 2, :], temp[:, 1, :], ACT.Ln, bias=c("one")).then_inc(S["temp_out"], 1)

            def pre1(s):
                copy_ft(2, s, bank[0], "a1_tr", s + 1, "a1_ft")
                act.wait_ge(S["a1_dx"], s + 1)
                f(dx0[:], bank[1][:, 0:HT], ACT.Copy).then_inc(S["a1_ft"], 1)
                f(dx1[:], bank[1][0:D1, HT:], ACT.Copy).then_inc(S["a1_ft"], 1)
                act.wait_ge(S["a1_mt"], s + 1)
                f(mt0[:], bank[2][:, 0:HT], ACT.Tanh).then_inc(S["mt_ready"], 1)
                f(mt1[:], bank[2][0:32, HT:], ACT.Tanh).then_inc(S["mt_ready"], 1)
                act.wait_ge(S["a1_t1"], s + 1)
                f(t1[0:64, :], bank[0][0:64, 0:HT], ACT.Tanh).then_inc(S["t1_ready"], 1)
                act.wait_ge(S["a1_rk"], 2 * s + 1)
                link(f(kt0[:], bank[2][:, 0:HT], ACT.Copy))
                link(f(kt1[:], bank[2][0:D1, HT:], ACT.Copy))
                f(ksq0[:], kt0[:], ACT.Square)
                f(ksq1[:], kt1[:], ACT.Square).then_inc(S["ksq_ready"], 1)
                act.wait_ge(S["a1_rk"], 2 * s + 2)
                f(rt0[:], bank[3][:, 0:HT], ACT.Copy)
                f(rt1[:], bank[3][0:D1, HT:], ACT.Copy).then_inc(S["rk_ready"], 1)
                act.wait_ge(S["a1_n2"], s + 1)
                f(kn0[:], bank[6][:, 0:HT], ACT.Sqrt)
                f(kn1[:], bank[6][0:D1, HT:], ACT.Sqrt).then_inc(S["n2_ready"], 1)
                act.wait_ge(S["a1_w"], s + 1)
                f(ew.rearrange("p i k -> p (i k)"), bank[1][:, 0:2 * D], ACT.Exp).then_inc(S["ew_ready"], 1)
                act.wait_ge(S["a1_vg"], 2 * s + 1)
                if s:
                    act.wait_ge(S["st_v"], 32 * s)
                f(vs[:].rearrange("p i k -> p (i k)"), bank[4][:, 0:2 * D], ACT.Copy).then_inc(S["v_ready"], 1)
                act.wait_ge(S["cs_ready"], s + 1)
                for kind, (d, sc) in enumerate(((0, 1.0), (1, -1.0), (0, -1.0), (1, 1.0))):
                    f(ex0[:, kind], cs0[:, :, d, :], ACT.Exp, scale=sc)
                    ins = f(ex1[:, kind], cs1[:, :, d, :], ACT.Exp, scale=sc)
                ins.then_inc(S["ex_ready"], 1)
                for i in range(2):
                    act.wait_ge(S["gram_in"], 2 * s + i + 1)
                    g = gram[:, i].rearrange("p h k -> p (h k)")
                    f(g, g, ACT.Exp).then_inc(S["gram_exp"], 1)
                for i in range(2):
                    act.wait_ge(S["a1_at"], 2 * s + i + 1)
                    f(atr[:, s, i].rearrange("p g k -> p (g k)"), bank[1 + i][:, 0:384], ACT.Copy)\
                        .then_inc(S["at_ready"], 1)
                act.wait_ge(S["g_raw"], s + 1)
                f(sg[:, s].rearrange("p i k -> p (i k)"), sg[:, s].rearrange("p i k -> p (i k)"), ACT.Silu).then_inc(S["g_ready"], 1)

            def post1(s):
                act.wait_ge(S["y_in"], s + 1)
                f(gsq[:].rearrange("p i k -> p (i k)"), pre[:, 2 * s:2 * s + 2, :].rearrange("p i k -> p (i k)"),
                  ACT.Square).then_inc(S["y_sq"], 1)
                act.wait_ge(S["a1_ytr"], s + 1)
                f(ct0[:], bank[1][:, 0:HT], ACT.Copy).then_inc(S["yt_ready"], 1)
                f(ct1[0:D1, :], bank[1][0:D1, HT:], ACT.Copy).then_inc(S["yt_ready"], 1)

            loads()
            tokens()
            temperature()
            attention0(0)
            attention0(1)
            route(0, 0)
            experts(0, 0)
            pre1(0)
            route(0, 1)
            experts(0, 1)
            post1(0)
            pre1(1)
            route(1, 0)
            experts(1, 0)
            post1(1)
            route(1, 1)
            experts(1, 1)

        @block.vector
        def _(dve):
            v = nc.vector
            chain = [0]

            def link(ins):
                chain[0] += 1
                ins.then_inc(S["dve_chain"], 1)
                dve.wait_ge(S["dve_chain"], chain[0])

            def flat(ap):
                return ap.rearrange("p a b -> p (a b)")

            def inv_sqrt(name, n):
                q = order.index(name)
                dve.wait_ge(S["rstd_ready"], q + 1)
                return rstd[:, q % 2, 0:n]

            def ask(name, src, scale, eps):
                q = order.index(name)
                n = width.get(name, 2)
                v.tensor_scalar(var_in[:, q % 2, 0:n], src, scale, eps, ALU.mult, ALU.add).then_inc(S["var_ready"], 1)

            def layer_norm(name, s, src, dst, ready=None):
                for i in range(2):
                    link(v.bn_stats(stats[:, 2 * s + i, :], src[:, 2 * s + i, :]))
                    link(v.bn_aggr(mv[:, 2 * s + i, :], stats[:, 2 * s + i, :]))
                ask(name, mv[:, 2 * s:2 * s + 2, 1], 1.0, LN_EPS)
                rs = inv_sqrt(name, 2)
                for i in range(2):
                    ins = v.tensor_scalar(dst[:, 2 * s + i, :], src[:, 2 * s + i, :], mv[:, 2 * s + i, 0:1],
                                          rs[:, i:i + 1], ALU.subtract, ALU.mult)
                    if i == 1 and ready:
                        ins.then_inc(S[ready], 1)
                        dve.wait_ge(S[ready], s + 1)
                    else:
                        link(ins)

            def tokens():
                dve.wait_ge(S["ld_tok"], 16)
                v.tensor_tensor(wtok, wtok, bc(gin, 2, D), ALU.mult).then_inc(S["wtok_scaled"], 1)
                dve.wait_ge(S["tok_ss"], 1)
                ask("tok1", bank[2][:, 0:4], 1.0 / PATCH_DIM, RMS_EPS)
                rs = inv_sqrt("tok1", 4)
                dve.wait_ge(S["ld_row"], 16)
                dve.wait_ge(S["tok_y"], 1)
                for t in range(TILES):
                    v.scalar_tensor_tensor(h0[:, t, :], bank[t // 2][:, (t % 2) * D:(t % 2 + 1) * D], rs[:, t:t + 1],
                                           r("b_proj"), ALU.mult, ALU.add).then_inc(S["y_ready"], 1)
                dve.wait_ge(S["y_sq2"], TILES)
                ask("tok2", ss[:, 1, :], 1.0 / D, RMS_EPS)
                rs = inv_sqrt("tok2", 4)
                for t in range(TILES):
                    ins = v.scalar_tensor_tensor(h0[:, t, :], h0[:, t, :], rs[:, t:t + 1], r("g_out"),
                                                 ALU.mult, ALU.mult)
                    if t % 2:
                        ins.then_inc(S["h0_ready"], 1)

            def composites():
                dve.wait_ge(S["ld_att0"], 32)
                dve.wait_ge(S["lora_mm"], 1)
                for j in range(3):
                    v.scalar_tensor_tensor(wn[:, 0, j, 0:D], bank[3 + j][:, 0:D], 0.5, wn[:, 0, j, 0:D],
                                           ALU.mult, ALU.add)
                    ins = v.scalar_tensor_tensor(wn[0:D1, 1, j, 0:D], bank[3 + j][0:D1, D:2 * D], 0.5,
                                                 wn[0:D1, 1, j, 0:D], ALU.mult, ALU.add)
                ins.then_inc(S["wn_ready"], 1)
                dve.wait_ge(S["ld_const"], 16)
                dve.wait_ge(S["ld_row"], 16)
                link(v.tensor_reduce(wgsum[:].rearrange("p c a -> p (c a)"), wg.rearrange("p c a b -> p (c a) b"),
                                     AX.X, ALU.add))
                link(v.tensor_reduce(bgs[:], r("bg").rearrange("p (a b) -> p a b", a=2), AX.X, ALU.add))
                for ch in range(2):
                    link(v.tensor_tensor(wgx[:, ch], bc(wgsum[:, ch, :], 1, HEADS),
                                         bc(c("head12")[:, ch * HEADS:(ch + 1) * HEADS], 2, 2), ALU.mult))
                link(v.tensor_scalar(temp[:, 1, :], r("lucid"), -1.0, None, ALU.mult))
                v.tensor_tensor(temp[:, 0, :], r("lucid"), temp[:, 1, :], ALU.max).then_inc(S["temp_in"], 1)
                dve.wait_ge(S["comp_mm"], 1)
                for j in range(3):
                    sc = HD ** -0.5 if j == 0 else 1.0
                    link(v.tensor_scalar(cw0[:, j, :], bank[3 + j][:, 0:D], sc, None, ALU.mult))
                    link(v.tensor_scalar(cw1[0:D1 + 1, j, :], bank[3 + j][0:D1 + 1, D:2 * D], sc, None, ALU.mult))
                    link(v.scalar_tensor_tensor(cw1[D1:D1 + 1, j, :], b64[D1:D1 + 1, j, :], sc, cw1[D1:D1 + 1, j, :],
                                                ALU.mult, ALU.add))
                dve.wait_ge(S["posb_mm"], 1)
                v.tensor_copy(posb[:], bank[6][:, 0:T * HEADS].rearrange("p (k h) -> p k h", h=HEADS))\
                    .then_inc(S["comp_ready"], 1)
                dve.wait_ge(S["comp_ready"], 1)
                dve.wait_ge(S["temp_out"], 1)
                link(v.scalar_tensor_tensor(temp[:, 0, :], r("lucid"), 0.0, temp[:, 2, :], ALU.max, ALU.add))

            def expand(n, a, d, tiles):
                xa, xb = expanded(n)
                for i in range(2):
                    yield v.tensor_tensor(xa[:, 4 * i:4 * i + 4], bc(a(i), 2, 8),
                                          bc(bc(c("head8"), 1, 4), 3, 32), ALU.mult)
                    yield v.tensor_tensor(xb[:, 4 * i:4 * i + 4], bc(d(i), 2, 4),
                                          bc(bc(c("head8", D1)[:, 0:4], 1, 4), 3, 32), ALU.mult)

            def blocks(tile_):
                return lambda i: tile_[:, 128 * i:128 * i + 128].rearrange("p (b k) -> p b k", b=4)

            def attention0(s):
                dve.wait_ge(S["a0_k"], s + 1)
                for n, ins in enumerate(expand(0, blocks(bank[2][:, 0:HT]), blocks(bank[2][0:D1, HT:]), 2)):
                    if n % 2:
                        ins.then_inc(S["kx_ready"], 1)
                dve.wait_ge(S["a0_gate"], s + 1)
                gr = gates0[:].rearrange("p i h a -> p (i h) a")
                v.tensor_tensor(gr, bank[7][:, 0:48].rearrange("p (n a) -> p n a", a=2), bc(bgs[:], 1, 24),
                                ALU.add).then_inc(S["gate_in"], 1)
                dve.wait_ge(S["a0_v"], s + 1)
                for b in range(BLK // 2):
                    v.tensor_tensor(vx[:, 2 * b:2 * b + 2].rearrange("p b g j k -> p (b g) j k"),
                                    bank[3 + b][:, 0:2 * D].rearrange("p (n j k) -> p n j k", j=4, k=HD),
                                    bc(bc(c("quad4"), 1, 6), 3, HD), ALU.mult).then_inc(S["vx_ready"], 1)
                dve.wait_ge(S["gate_exp"], s + 1)
                g = flat(gr)
                link(v.tensor_scalar(g, g, 1.0, None, ALU.add))
                link(v.reciprocal(g, g))
                ga, gb = gates0[:, :, :, 0], gates0[:, :, :, 1]
                link(v.tensor_tensor(gb, gb, bc(r("gru"), 1, 2), ALU.mult))
                link(v.scalar_tensor_tensor(gate[:], gb, -1.0, ga, ALU.add, ALU.mult))
                link(v.tensor_scalar(gate[:], gate[:], 2.0, None, ALU.add))
                for i in range(2):
                    link(v.tensor_tensor(gbias[:, i], bc(gate[:, i, :], 2, T), posb[:].rearrange("p k h -> p h k"),
                                         ALU.mult))
                for i in range(2):
                    p = prob[:, i]
                    dve.wait_ge(S["a0_s"], 2 * s + i + 1)
                    link(v.tensor_tensor(p, bank[i][:, 0:384].rearrange("p (h k) -> p h k", h=HEADS),
                                         bc(c("off_pair"), 1, HEADS), ALU.add))
                    p4 = p.rearrange("p h (b k) -> p h b k", b=2)
                    link(v.tensor_tensor(p4, p4, bc(gbias[:, i], 2, 2), ALU.add))
                    link(v.tensor_reduce(smax[:, i], p, AX.X, ALU.max))
                    v.tensor_tensor(p, p, bc(smax[:, i], 2, 32), ALU.subtract).then_inc(S["s_shift"], 1)
                for i in range(2):
                    p = prob[:, i]
                    dve.wait_ge(S["s_exp"], 2 * s + i + 1)
                    link(v.tensor_reduce(smax[:, i], p, AX.X, ALU.add))
                    link(v.reciprocal(smax[:, i], smax[:, i]))
                    v.tensor_tensor(p, p, bc(smax[:, i], 2, 32), ALU.mult).then_inc(S["p_ready"], 1)
                dve.wait_ge(S["a0_wo"], s + 1)
                a = slice(2 * s, 2 * s + 2)
                v.tensor_tensor(pre[:, a, :], bank[4][:, 0:2 * D].rearrange("p (i k) -> p i k", i=2), h0[:, a, :],
                                ALU.add).then_inc(S["wo_read"], 1)
                dve.wait_ge(S["wo_read"], s + 1)
                layer_norm(f"a0_{s}", s, pre, h1)
                layer_norm(f"f0_{s}", s, h1, xffn)
                link(v.tensor_tensor(xffn[:, a, :], xffn[:, a, :], bc(r("ln_gamma"), 1, 2), ALU.mult))
                v.tensor_tensor(xffn[:, a, :], xffn[:, a, :], bc(r("ln_beta"), 1, 2), ALU.add)\
                    .then_inc(S["x_ready"], 1)

            def route(l, s):
                n = 2 * l + s
                dve.wait_ge(S["ff_lg"], n + 1)
                src = bank[6][:, 0:2 * NEXP].rearrange("p (i k) -> p i k", i=2)
                if l == 0:
                    link(v.tensor_copy(lg[:], src))
                else:
                    link(v.tensor_tensor(lg[:], src, bc(r("gate_b"), 1, 2), ALU.add))
                for i in range(2):
                    link(v.max(top[:, i, :], lg[:, i, :]))
                    link(v.max_index(topi[:, i, :], top[:, i, :], lg[:, i, :]))
                v.tensor_tensor(topd[:, :, 0:1], top[:, :, 1:2], top[:, :, 0:1], ALU.subtract).then_inc(S["top_in"], 1)
                link(v.tensor_copy(topf[:], topi[:, :, 0:2]))
                dve.wait_ge(S["top_exp"], n + 1)
                link(v.tensor_scalar(topd[:, :, 2:3], topd[:, :, 1:2], 1.0, None, ALU.add))
                link(v.reciprocal(topd[:, :, 2:3], topd[:, :, 2:3]))
                link(v.tensor_tensor(topd[:, :, 1:2], topd[:, :, 1:2], topd[:, :, 2:3], ALU.mult))
                for k in range(2):
                    link(v.tensor_tensor(hot[:, k], bc(c("iota8"), 1, 2), topf[:, :, k:k + 1].broadcast_to([128, 2, NEXP]),
                                         ALU.is_equal))
                    link(v.tensor_tensor(hot[:, k], hot[:, k],
                                         topd[:, :, 2 - k:3 - k].broadcast_to([128, 2, NEXP]), ALU.mult))
                a = slice(2 * s, 2 * s + 2)
                v.tensor_tensor(gts[:, a, :], hot[:, 0], hot[:, 1], ALU.add).then_inc(S["gts_ready"], 1)
                if l == 0:
                    v.tensor_scalar(acc[:, a, :], h1[:, a, :], 2.0, None, ALU.mult).then_inc(S["acc_init"], 1)
                else:
                    dve.wait_ge(S["b2_mm"], s + 1)
                    v.tensor_tensor(acc[:, a, :], bank[6][:, 0:2 * D].rearrange("p (i k) -> p i k", i=2), h3[:, a, :],
                                    ALU.add).then_inc(S["acc_init"], 1)

            def pre1(s):
                fa, fb = f0[2][:, s, :], f1[2][0:D1, s, :]
                dve.wait_ge(S["ld_att1"], 16)
                dve.wait_ge(S["a1_ft"], 4 * (s + 1))
                v.scalar_tensor_tensor(xx0[:], dx0[:], maa[:, 0, 0:1], fa, ALU.mult, ALU.add)
                v.scalar_tensor_tensor(xx1[:], dx1[:], maa[0:D1, 1, 0:1], fb, ALU.mult, ALU.add)\
                    .then_inc(S["a1_xx"], 1)
                for m in range(MIX):
                    dve.wait_ge(S["a1_mm"], MIX * s + m + 1)
                    v.scalar_tensor_tensor(xc0[:, m, :], bank[3 + m][:, 0:HT], maa[:, 0, 1 + m:2 + m], dx0[:],
                                           ALU.add, ALU.mult)
                    v.scalar_tensor_tensor(xc1[:, m, :], bank[3 + m][0:D1, HT:], maa[0:D1, 1, 1 + m:2 + m], dx1[:],
                                           ALU.add, ALU.mult).then_inc(S["a1_xd"], 1)
                dve.wait_ge(S["a1_vg"], 2 * s + 2)
                v.tensor_copy(flat(sg[:, s]), bank[5][:, 0:2 * D]).then_inc(S["g_raw"], 1)
                dve.wait_ge(S["n2_ready"], s + 1)
                for kn, kt in ((kn0, kt0), (kn1, kt1)):
                    link(v.tensor_scalar(kn[:], kn[:], 1e-12, None, ALU.max))
                    link(v.reciprocal(kn[:], kn[:]))
                    link(v.tensor_tensor(kn[:], kn[:], kt[:], ALU.mult))
                for n, ins in enumerate(expand(0, blocks(kn0), blocks(kn1), 2)):
                    pass
                ins.then_inc(S["kn_ready"], 1)
                dve.wait_ge(S["a1_cs"], s + 1)
                v.tensor_scalar(cs0[:].rearrange("p i d k -> p (i d k)"), bank[7][:], -60.0, 60.0, ALU.max, ALU.min)
                v.tensor_scalar(cs1[:].rearrange("p i d k -> p (i d k)"), bank[0][0:D1, :], -60.0, 60.0,
                                ALU.max, ALU.min).then_inc(S["cs_ready"], 1)
                for i in range(2):
                    dve.wait_ge(S["a1_gram"], 2 * s + i + 1)
                    link(v.tensor_tensor(gram[:, i], bank[1 + i][:, 0:384].rearrange("p (h k) -> p h k", h=HEADS),
                                         bc(temp[:, 0, :], 2, 32), ALU.mult))
                    v.tensor_scalar(gram[:, i], gram[:, i], -20.0, 20.0, ALU.max, ALU.min).then_inc(S["gram_in"], 1)
                dve.wait_ge(S["ex_ready"], s + 1)
                dve.wait_ge(S["rk_ready"], s + 1)
                for ex, rt, kt in ((ex0, rt0, kt0), (ex1, rt1, kt1)):
                    for kind in range(4):
                        op = rt if kind < 2 else kt
                        link(v.tensor_tensor(ex[:, kind], ex[:, kind], op[:].rearrange("p (i k) -> p i k", i=2), ALU.mult))
                for m in (1, 2):
                    for ins in expand(m, lambda i: ex0[:, 1 + m, i].rearrange("p (b k) -> p b k", b=4),
                                      lambda i: ex1[:, 1 + m, i].rearrange("p (b k) -> p b k", b=4), 2):
                        pass
                ins.then_inc(S["decay_ops"], 1)
                for i in range(2):
                    dve.wait_ge(S["gram_exp"], 2 * s + i + 1)
                    if s:
                        dve.wait_ge(S["st_p"], 32 * s)
                    link(v.tensor_scalar(pmat[:, i], gram[:, i, :, 0:T], c("even"), None, ALU.mult))
                    link(v.scalar_tensor_tensor(pmat[:, i], gram[:, i, :, T:], c("odd"), pmat[:, i],
                                                ALU.mult, ALU.add))
                    v.tensor_tensor(pmat[:, i], pmat[:, i], bc(c("eye16"), 1, HEADS), ALU.add)\
                        .then_inc(S["p_mat"], 1)
                for i in range(2):
                    dve.wait_ge(S["a1_ab"], 2 * s + i + 1)
                    for mask, bk in (("lower", 3), ("upper", 5)):
                        ins = v.copy_predicated(amix[:, i], bc(c(mask), 1, HEADS).bitcast(I32),
                                                bank[bk + i][:, 0:384].rearrange("p (h k) -> p h k", h=HEADS))
                        if mask == "lower":
                            link(ins)
                    ins.then_inc(S["a_mix"], 1)

            def solve(s):
                dve.wait_ge(S["ld_g"], 16 * 32 * (s + 1))
                W = T + HD
                for k in range(T):
                    link(v.reciprocal(piv[:], sysm[:, :, k, k]))
                    link(v.tensor_tensor(sysm[:, :, k, k + 1:W], sysm[:, :, k, k + 1:W], bc(piv[:], 2, W - k - 1),
                                         ALU.mult))
                    if k == T - 1:
                        break
                    pr = prod[:, :, k + 1:T, k + 1:W]
                    link(v.tensor_tensor(pr, bc(sysm[:, :, k + 1:T, k], 3, W - k - 1),
                                         bc(sysm[:, :, k, k + 1:W], 2, T - k - 1), ALU.mult))
                    link(v.tensor_tensor(sysm[:, :, k + 1:T, k + 1:W], sysm[:, :, k + 1:T, k + 1:W], pr, ALU.subtract))
                for k in range(T - 1, 0, -1):
                    pr = prod[:, :, 0:k, T:W]
                    link(v.tensor_tensor(pr, bc(sysm[:, :, 0:k, k], 3, HD), bc(sysm[:, :, k, T:W], 2, k), ALU.mult))
                    ins = v.tensor_tensor(sysm[:, :, 0:k, T:W], sysm[:, :, 0:k, T:W], pr, ALU.subtract)
                    if k > 1:
                        link(ins)
                ins.then_inc(S["solved"], 1)

            def experts_done(name, n, s, dst, ready):
                dve.wait_ge(S["acc_add"], NEXP * (n + 1))
                layer_norm(name, s, acc, dst, ready)

            def post1(s):
                a = slice(2 * s, 2 * s + 2)
                dve.wait_ge(S["a1_y"], s + 1)
                y = bank[0][:, 0:2 * D].rearrange("p (n k) -> p n k", k=HD)
                yc = pre[:, a, :].rearrange("p i (h k) -> p (i h) k", k=HD)
                link(v.tensor_reduce(gsum[:], y, AX.X, ALU.add))
                link(v.tensor_scalar(gsum[:], gsum[:], 1.0 / HD, None, ALU.mult))
                v.tensor_tensor(yc, y, bc(gsum[:], 2, HD), ALU.subtract).then_inc(S["y_in"], 1)
                dve.wait_ge(S["y_sq"], s + 1)
                link(v.tensor_reduce(gsum[:], gsq[:].rearrange("p i (h k) -> p (i h) k", k=HD), AX.X, ALU.add))
                ask(f"gn_{s}", gsum[:], 1.0 / HD, GN_EPS)
                rs = inv_sqrt(f"gn_{s}", 24)
                link(v.tensor_tensor(yc, yc, bc(rs, 2, HD), ALU.mult))
                link(v.tensor_tensor(pre[:, a, :], pre[:, a, :], bc(r("ln_w"), 1, 2), ALU.mult))
                link(v.tensor_tensor(pre[:, a, :], pre[:, a, :], bc(r("ln_b"), 1, 2), ALU.add))
                dve.wait_ge(S["g_ready"], s + 1)
                v.tensor_tensor(gsq[:], pre[:, a, :], sg[:, s], ALU.mult).then_inc(S["gn_ready"], 1)
                dve.wait_ge(S["a1_wo"], s + 1)
                v.tensor_tensor(pre[:, a, :], bank[2][:, 0:2 * D].rearrange("p (i k) -> p i k", i=2), h2[:, a, :],
                                ALU.add).then_inc(S["wo1_read"], 1)
                dve.wait_ge(S["wo1_read"], s + 1)
                layer_norm(f"h3_{s}", s, pre, h3, "h3_ready")

            v.memset(f1[0][D1:D1 + 1, :, :], 1.0).then_inc(S["ones_set"], 1)
            v.memset(ct1[D1:D1 + 1, :], 1.0).then_inc(S["ones_set"], 1)
            tokens()
            composites()
            attention0(0)
            attention0(1)
            route(0, 0)
            experts_done("h2_0", 0, 0, h2, "h2_ready")
            dve.wait_ge(S["amix_zero"], 1)
            v.memset(t1[64:65, :], 1.0).then_inc(S["t1_ones"], 1)
            pre1(0)
            route(0, 1)
            solve(0)
            experts_done("h2_1", 1, 1, h2, "h2_ready")
            post1(0)
            pre1(1)
            route(1, 0)
            solve(1)
            experts_done("out_0", 2, 0, pre, "out_ready")
            post1(1)
            route(1, 1)
            experts_done("out_1", 3, 1, pre, "out_ready")

        @block.gpsimd
        def _(pool):
            g = nc.gpsimd

            def power(name):
                q, n = order.index(name), width.get(name, 2)
                pool.wait_ge(S["var_ready"], q + 1)
                g.tensor_tensor(rstd[:, q % 2, 0:n], var_in[:, q % 2, 0:n], c("neghalf").broadcast_to([128, n]),
                                ALU.pow).then_inc(S["rstd_ready"], 1)

            def repeat(s):
                pool.wait_ge(S["ones_set"], 1)
                pool.wait_ge(S["a0_ft"], 2 * (s + 1))
                if s:
                    pool.wait_ge(S["a0_v"], s)
                for dst, src in ((fr0, f0[0][:, s, :]), (fr1, f1[0][0:D1 + 1, s, :])):
                    ins = g.tensor_copy(dst, bc(src.rearrange("p (b k) -> p b k", b=BLK), 2, 4))
                ins.then_inc(S["fr_ready"], 1)

            def add_experts(l, s):
                a = slice(2 * s, 2 * s + 2)
                for e in range(NEXP):
                    m = (2 * l + s) * NEXP + e
                    pool.wait_ge(S["y_act"], m + 1)
                    if e == 0:
                        pool.wait_ge(S["acc_init"], 2 * l + s + 1)
                    else:
                        pool.wait_ge(S["acc_add"], m)
                    g.tensor_tensor(acc[:, a, :], acc[:, a, :], ysc[:, m % 2], ALU.add).then_inc(S["acc_add"], 1)

            def mixes(s):
                for m in range(MIX):
                    pool.wait_ge(S["a1_xd"], MIX * s + m + 1)
                    g.tensor_tensor(xc0[:, m, :], xc0[:, m, :], f0[2][:, s, :], ALU.add)
                    g.tensor_tensor(xc1[:, m, :], xc1[:, m, :], f1[2][0:D1, s, :], ALU.add).then_inc(S["xc_ready"], 1)

            g.memset(amix[:], 0.0).then_inc(S["amix_zero"], 1)
            pool.wait_ge(S["ld_const"], 16)
            power("tok1")
            power("tok2")
            repeat(0)
            power("a0_0")
            power("f0_0")
            repeat(1)
            power("a0_1")
            power("f0_1")
            pool.wait_ge(S["a0_ctx"], HALVES)
            g.memset(vx1[:], 0.0).then_inc(S["vx1_zero"], 1)
            add_experts(0, 0)
            power("h2_0")
            mixes(0)
            add_experts(0, 1)
            power("h2_1")
            power("gn_0")
            power("h3_0")
            mixes(1)
            add_experts(1, 0)
            power("out_0")
            power("gn_1")
            power("h3_1")
            add_experts(1, 1)
            power("out_1")


def _constants():
    p = np.arange(128)
    img = p // T
    same = img[:, None] == img[None, :]
    a, b = p[:, None], p[None, :]
    shift = np.where(same, 0.5 * (np.abs(a - b) == 1) - 1.0 * (a == b), 0.0)
    mid = (b // T) * T + T // 2
    cf = np.where(same, 1.0 * (a <= b) - 1.0 * (a <= mid), 0.0)
    cb = np.where(same, 1.0 * (a < b) - 1.0 * (a < mid), 0.0)
    k = np.arange(32)
    own = (p[:, None] % 32) // T == k[None, :] // T
    key, tok = k[None, :] % T, p[:, None] % T
    head24 = np.concatenate([p[:, None] // HD == np.arange(HEADS)[None, :],
                             8 + p[:, None] // HD == np.arange(HEADS)[None, :]], 1)
    anti = a == T - 1 - b % T
    parts = {
        "ident": np.eye(128), "shift": shift, "cums": -np.concatenate([cf, cb], 1), "headsum": same,
        "head8": p[:, None] // HD == np.arange(8)[None, :], "quad4": p[:, None] // 32 == np.arange(4)[None, :],
        "head12": head24, "off_pair": np.where(own, 0.0, MASKED), "even": (img % 2 == 0)[:, None],
        "odd": (img % 2 == 1)[:, None], "lower": own & (key <= tok), "upper": own & (key > tok),
        "anti16": anti, "iota8": np.tile(np.arange(8), (128, 1)), "one": np.ones((128, 1)),
        "neghalf": np.full((128, 1), -0.5), "eye16": tok == np.arange(T)[None, :]}
    return np.ascontiguousarray(np.concatenate([np.asarray(parts[n], np.float32) for n in CONST], 1))


def _chunks(a, extra=None):
    out = np.zeros((128, 2) + a.shape[1:], np.float32)
    out[:, 0] = a[:128]
    out[:D1, 1] = a[128:]
    if extra is not None:
        out[D1, 1] = extra
    return out


def _pack(table, parts):
    cols = []
    for name in table:
        a = np.asarray(parts[name], np.float32)
        a = a.reshape(a.shape[0], -1)
        cols.append(np.concatenate([a, np.zeros((128 - a.shape[0], a.shape[1]), np.float32)], 0))
    return np.ascontiguousarray(np.concatenate(cols, 1))


def _expert_weights(w1, w2):
    tail = w1[:, 128:].reshape(NEXP, D1, FCH // 2, 2, 128).transpose(0, 3, 1, 2, 4).reshape(NEXP, 128, -1)
    low = w2.reshape(NEXP, FCH, 128, D).transpose(0, 2, 1, 3).reshape(NEXP, 128, -1)
    return np.ascontiguousarray(np.concatenate([w1[:, :128], tail, low], 2))


def kernel(**inputs):
    import concourse.bacc as _bacc
    from concourse.bass_utils import run_bass_kernel_spmd as _run

    x = {k: np.asarray(a) for k, a in inputs.items()}
    a0 = {k[8:]: v for k, v in x.items() if k.startswith("L0_attn_")}
    a1 = {k[8:]: v for k, v in x.items() if k.startswith("L1_attn_")}
    xt = x["x"].reshape(BATCH, 3, 4, 16, 4, 16).transpose(3, 5, 1, 0, 2, 4).reshape(PCH, 128, TOK)
    xt = np.ascontiguousarray(xt.transpose(1, 0, 2).reshape(128, PCH * TOK))
    tokp = _pack(TOKP, {"w": x["L0_tok_W_proj"].T.reshape(PCH, 128, D).transpose(1, 0, 2),
                        "gin": x["L0_tok_g_in"].reshape(PCH, 128).T})
    rows = np.concatenate([x["L0_tok_b_proj"], x["L0_tok_g_out"], x["L0_ffn_ln_gamma"], x["L0_ffn_ln_beta"],
                           a1["ln_w"], a1["ln_b"], a0["gru_const"].reshape(-1), a1["lucid_temp"].reshape(-1),
                           x["L1_ffn_gate_b"], a0["bg"]])
    qkv = [(a0["Wq"], a0["bq"], a0["Aq"], a0["Bq"]), (a0["Wk"], a0["bk"], a0["Ak"], a0["Bk"]),
           (a0["Wv"], a0["bv"], a0["Av"], a0["Bv"])]
    bias64 = np.zeros((128, 3, D), np.float32)
    bias64[D1] = np.stack([b for _, b, _, _ in qkv])
    rel = a0["rel_embed"]
    att0 = _pack(ATT0, {
        "wn": _chunks(np.stack([np.concatenate([w, b[:, None]], 1) for w, b, _, _ in qkv], 1)),
        "wt": _chunks(np.stack([w.T for w, _, _, _ in qkv], 1)),
        "wo": _chunks(a0["Wo"].T, a0["bo"]),
        "wg": _chunks(np.tile(a0["Wg"].T, (HEADS, 1))),
        "b64": bias64,
        "rel": np.stack([np.concatenate([rel[15::-1], rel[41:56]], 0)[k:k + T] for k in range(T)], 1)})
    lora = np.stack([np.stack([b.T, a], 1) for _, _, a, b in qkv], 1).reshape(2, -1)
    maa = np.stack([a1[f"time_maa_{n}"].reshape(-1) for n in "xwkvrg"], 1)
    maa_w2 = np.zeros((128, 2, D), np.float32)
    maa_w2[:, 0] = a1["maa_w2"][:4].reshape(128, D)
    maa_w2[:32, 1] = a1["maa_w2"][4]
    att1 = _pack(ATT1, {
        "maa_w1": _chunks(a1["maa_w1"]), "maa_w2": maa_w2, "maa": _chunks(maa),
        "w4": _chunks(np.stack([a1["Wr"], a1["Wk"], a1["Wv"], a1["Wg"]], 1)),
        "dw1": _chunks(a1["decay_w1"]),
        "dw2": np.concatenate([a1["decay_w2"], a1["time_decay"].reshape(1, D)], 0),
        "wo": _chunks(a1["Wo"]), "router": _chunks(x["L0_ffn_router_w"]), "gate": _chunks(x["L1_ffn_gate_w"]),
        "b1": x["L1_ffn_b1"].reshape(NEXP * FCH, 128).T, "b2": x["L1_ffn_b2"]})
    arrays = {"consts": _constants(), "rows": np.ascontiguousarray(rows), "x_t": xt,
              "tok_pack": tokp, "att0_pack": att0, "lora_pack": np.ascontiguousarray(lora), "att1_pack": att1,
              "w_l0": _expert_weights(x["L0_ffn_w1"], x["L0_ffn_w2"]),
              "w_l1": _expert_weights(x["L1_ffn_w1"], x["L1_ffn_w2"])}

    nc = _bacc.Bacc("TRN2", target_bir_lowering=False, num_devices=1)
    args = [nc.dram_tensor(n, a.shape, F32, kind="ExternalInput").ap() for n, a in arrays.items()]
    scratch = [nc.dram_tensor("p_scratch", (TILES, 128, HEADS * T), F32, kind="Internal").ap(),
               nc.dram_tensor("v_scratch", (TILES, 128, D), F32, kind="Internal").ap(),
               nc.dram_tensor("s_scratch", (TILES, SYS, T * HD), F32, kind="Internal").ap()]
    out = nc.dram_tensor("out", (TILES, 128, D), F32, kind="ExternalOutput").ap()
    vit_tower_kernel(nc, *args, *scratch, out)
    got = _run(nc, [arrays], core_ids=[0]).results[0]["out"]
    return np.asarray(got).reshape(BATCH, T, D)
```

```python
from contextlib import ExitStack
from itertools import chain, islice

import numpy as np
import concourse.bass as bass
from concourse import mybir

F32 = mybir.dt.float32
I32 = mybir.dt.int32
U32 = mybir.dt.uint32
ALU = mybir.AluOpType
ACT = mybir.ActivationFunctionType
AX = mybir.AxisListType

BATCH, T, D, HEADS, HD = 32, 16, 192, 12, 16
TOK = BATCH * T
TILES, HALVES = TOK // 128, 2
HT = TOK // HALVES
BLK = HT // 32
PATCH_DIM, PCH = 768, 6
NEXP, DFF, FCH = 8, 768, 6
D1 = D - 128
SYS = 96
WCOLS = DFF + DFF // 2 + FCH * D
MIX = 5
MIX_ORDER = (1, 2, 0, 3, 4)
RMS_EPS, LN_EPS, GN_EPS = 1e-5, 1e-5, 64e-5
MASKED = -1e30
ARENA = 6610

def _columns(*spec):
    at, out = 0, {}
    for name, width in spec:
        out[name] = (at, width)
        at += width
    return out, at


CONST, NCONST = _columns(
    ("ident", 128), ("shift", 128), ("cums", 256), ("headsum", 128), ("head8", 8), ("quad4", 4),
    ("head12", 24), ("off_pair", 32), ("even", 1), ("odd", 1), ("lower", 32), ("upper", 32),
    ("anti16", 128), ("iota8", 8), ("one", 1), ("neghalf", 1), ("eye16", 16))
ROW, NROW = _columns(
    ("b_proj", D), ("g_out", D), ("ln_gamma", D), ("ln_beta", D), ("ln_w", D), ("ln_b", D),
    ("gru", HEADS), ("lucid", HEADS), ("gate_b", NEXP), ("bg", 8))
TOKP, NTOKP = _columns(("w", PCH * D), ("gin", PCH))
ATT0, NATT0 = _columns(("wn", 2 * 3 * (D + 1)), ("wt", 2 * 3 * D), ("wo", 2 * D), ("wg", 16),
                       ("b64", 3 * D), ("rel", T * HEADS))
ATT1, NATT1 = _columns(("maa_w1", 2 * 160), ("maa_w2", 2 * D), ("maa", 12), ("w4", 2 * 4 * D),
                       ("dw1", 2 * 64), ("dw2", D), ("wo", 2 * D), ("router", 16), ("gate", 16), ("b1", NEXP * FCH),
                       ("b2", D))


def vit_tower_kernel(nc, consts, rows, x_t, tok_pack, att0_pack, lora_pack, att1_pack, w_l0, w_l1,
                     p_dram, s_dram, out):
    ctx = ExitStack()
    with ctx:
        def sb(name, shape, dt=F32):
            return ctx.enter_context(nc.sbuf_tensor(name, shape, dt))

        def sem(name):
            return ctx.enter_context(nc.semaphore(name))

        bank = [ctx.enter_context(nc.psum_tensor(f"bank{i}", [128, 512], F32)) for i in range(8)]

        arena = sb("arena", [128, ARENA])
        used = [0, 0]

        def shared(layer, shape):
            n = int(np.prod(shape[1:]))
            at = used[layer]
            used[layer] += n
            assert used[layer] <= ARENA, (layer, used)
            names = " ".join(f"a{i}" for i in range(len(shape) - 1))
            ap = arena[0:shape[0], at:at + n]
            if len(shape) == 2:
                return ap
            return ap.rearrange(f"p ({names}) -> p {names}", **{f"a{i}": k for i, k in enumerate(shape[1:])})

        scratch = sb("scratch", [128, 3, BLK * HEADS * 32])
        xt = scratch[:, 0, :].rearrange("p (c n) -> p c n", c=PCH)
        xsq = scratch[:, 1, :].rearrange("p (c n) -> p c n", c=PCH)
        tokp = scratch[:, 2, 0:NTOKP]
        lora = scratch[0:2, 2, NTOKP:NTOKP + 3 * 2 * D]

        con = sb("con", [128, NCONST])
        row = sb("row", [128, NROW])
        att0 = shared(0, [128, NATT0])
        att1 = sb("att1", [128, NATT1])
        wexp = sb("wexp", [128, NEXP, WCOLS])

        def c(name, p=128):
            a, n = CONST[name]
            return con[0:p, a:a + n]

        def r(name):
            a, n = ROW[name]
            return row[:, a:a + n]

        def col(tile_, table, name, p=128):
            a, n = table[name]
            return tile_[0:p, a:a + n]

        wtok = col(tokp, TOKP, "w").rearrange("p (c n) -> p c n", c=PCH)
        gin = col(tokp, TOKP, "gin")
        wn = col(att0, ATT0, "wn").rearrange("p (c j n) -> p c j n", c=2, j=3)
        wt = col(att0, ATT0, "wt").rearrange("p (c j n) -> p c j n", c=2, j=3)
        wo0 = col(att0, ATT0, "wo").rearrange("p (c n) -> p c n", c=2)
        wg = col(att0, ATT0, "wg").rearrange("p (c a b) -> p c a b", c=2, a=2)
        b64 = col(att0, ATT0, "b64").rearrange("p (j n) -> p j n", j=3)
        rel = col(att0, ATT0, "rel")
        router = [col(att1, ATT1, "router").rearrange("p (c n) -> p c n", c=2),
                  col(att1, ATT1, "gate").rearrange("p (c n) -> p c n", c=2)]
        lora_w = lora[:, :].rearrange("p (j a n) -> p j a n", j=3, a=2)
        maa_w1 = col(att1, ATT1, "maa_w1").rearrange("p (c n) -> p c n", c=2)
        maa_w2 = col(att1, ATT1, "maa_w2").rearrange("p (c n) -> p c n", c=2)
        maa = col(att1, ATT1, "maa").rearrange("p (c n) -> p c n", c=2)
        w4 = col(att1, ATT1, "w4").rearrange("p (c j n) -> p c j n", c=2, j=4)
        dw1 = col(att1, ATT1, "dw1").rearrange("p (c n) -> p c n", c=2)
        dw2 = col(att1, ATT1, "dw2")
        wo1 = col(att1, ATT1, "wo").rearrange("p (c n) -> p c n", c=2)
        b1 = col(att1, ATT1, "b1")
        b2 = col(att1, ATT1, "b2", 8)

        h0 = sb("h0", [128, TILES, D])
        h1 = sb("h1", [128, TILES, D])
        h2 = sb("h2", [128, TILES, D])
        h3 = h0
        acc = sb("acc", [128, TILES, D])
        pre = sb("pre", [128, TILES, D])
        xffn = pre
        stats = sb("stats", [128, TILES, 6])
        mv = sb("mv", [128, TILES, 2])
        var_in = sb("var_in", [128, 2, 24])
        rstd = sb("rstd", [128, 2, 24])
        f0 = [sb(f"f0_{n}", [128, HALVES, HT]) for n in ("att", "ffn")] * 2
        f1 = [sb(f"f1_{n}", [128, HALVES, HT]) for n in ("att", "ffn")] * 2
        def expanded(n):
            half = scratch[:, n // 2, (n % 2) * 1536:(n % 2 + 1) * 1536]
            a = half[:, 0:1024].rearrange("p (b h k) -> p b h k", b=4, h=8)
            b = half[0:D1, 1024:1536].rearrange("p (b h k) -> p b h k", b=4, h=4)
            return a, b

        ss = sb("ss", [128, 2, 4])
        cw0 = shared(0, [128, 3, D])
        cw1 = shared(0, [128, 3, D])
        wgsum = sb("wgsum", [128, 2, 2])
        wgx = shared(0, [128, 2, HEADS, 2])
        bgs = sb("bgs", [128, 2])
        posb = shared(0, [128, T, HEADS])
        q0 = shared(0, [128, HT])
        q1 = shared(0, [D1, HT])
        vx1 = sb("vx1", [128, BLK, 3, 4, HD])
        gates0 = shared(0, [128, 2, HEADS, 2])
        gate = shared(0, [128, 2, HEADS])
        gbias = shared(0, [128, 2, HEADS, T])
        prob = shared(0, [128, 2, HEADS, 32])
        smax = sb("smax", [128, 2, HEADS])
        atr = sb("atr", [128, 2, 3, 128])
        vx, ptr = vx1, atr
        ct0 = sb("ct0", [128, HT])
        ct1 = sb("ct1", [128, HT])
        lg = sb("lg", [128, 2, NEXP])
        top = sb("top", [128, 2, 8])
        topi = sb("topi", [128, 2, 8], U32)
        topf = sb("topf", [128, 2, 2])
        topd = sb("topd", [128, 2, 3])
        hot = sb("hot", [128, 2, 2, NEXP])
        gts = sb("gts", [128, TILES, NEXP])
        gts_t = sb("gts_t", [8, 2, 128])
        hid = scratch[:, 2, :].rearrange("p (a j n) -> p a j n", a=2, j=FCH)
        ysc = sb("ysc", [128, 2, 2, D])
        PROD_AT = used[1]
        dx0 = shared(1, [128, HT])
        dx1 = shared(1, [D1, HT])
        xx0 = shared(1, [128, HT])
        xx1 = shared(1, [D1, HT])
        mt0 = shared(1, [128, HT])
        mt1 = shared(1, [32, HT])
        xc0 = shared(1, [128, MIX, HT])
        xc1 = shared(1, [D1, MIX, HT])
        t1 = shared(1, [128, HT])
        ew = shared(1, [128, 2, D])
        sysm_all = sb("sysm", [128, 2, T, T + HD])
        cs0 = scratch[:, 1, 0:2 * HT].rearrange("p (i d k) -> p i d k", i=2, d=2)
        cs1 = scratch[0:D1, 1, 2 * HT:4 * HT].rearrange("p (i d k) -> p i d k", i=2, d=2)
        xc_all = xc0.rearrange("p m n -> p (m n)")
        ex0 = xc_all[:, 0:4 * HT].rearrange("p (a i k) -> p a i k", a=4, i=2)
        ex1 = xc1.rearrange("p m n -> p (m n)")[:, 0:4 * HT].rearrange("p (a i k) -> p a i k", a=4, i=2)
        rt0 = shared(1, [128, HT])
        rt1 = shared(1, [D1, HT])
        kt0 = shared(1, [128, HT])
        kt1 = shared(1, [D1, HT])
        ksq0 = xx0
        ksq1 = xx1
        kn0 = dx0
        kn1 = dx1
        vals = sb("vals", [128, 2, D])
        sg = sb("sg", [128, 2, D])
        amix = sb("amix", [128, 2, HEADS, 32])
        gram = [[acc[:, 2 * s:2 * s + 2].rearrange("p a n -> p (a n)").rearrange("p (h k) -> p h k", h=HEADS),
                 pre[:, 2 * s:2 * s + 2].rearrange("p a n -> p (a n)").rearrange("p (h k) -> p h k", h=HEADS)]
                for s in range(HALVES)]
        pv = shared(1, [128, 2, HEADS, T + HD])
        pmat = pv[:, :, :, 0:T]
        temp = sb("temp", [128, 3, HEADS])
        sysm = sysm_all[0:SYS]
        prod = arena[0:SYS, PROD_AT:PROD_AT + 2 * T * (T + HD)].rearrange("p (i t k) -> p i t k", i=2, t=T)
        piv = sb("piv", [SYS, 2])
        gsum = sb("gsum", [128, 24])
        gsq = sb("gsq", [128, 2, D])

        names = """ld_const ld_row ld_tok ld_att0 ld_att1 st_out
            wtok_scaled xsq_ready tok_y tok_ss y_ready y_sq2 h0_ready wo_read wo1_read g_raw
            lora_mm wn_ready comp_mm posb_mm comp_ready ones_set
            a0_tr a0_ft a0_q a0_k a0_v q_ready kx_ready v_out v_placed gate_in gate_exp vx_zero
            a0_s s_shift s_exp p_ready a0_pt pt_ready a0_ctx ct_ready a0_wo
            x_ready ff_tr ff_ft ff_lg top_in top_exp gts_ready gt_tr gt_ev b2_mm acc_init
            h_mm h_act y_mm y_act acc_add
            h2_ready a1_tr a1_ft a1_dx a1_xx a1_mt mt_ready a1_mm a1_xd xc_ready
            a1_t1 t1_ready a1_w ew_ready a1_cs cs_ready ex_ready a1_k a1_r rk_ready a1_v a1_g v_ready g_ready
            ksq_ready a1_n2 n2_ready kn_ready a1_gram a1_ab dk_ready gram_in gram_exp p_mat
            a_mix a1_at at_ready st_p ld_g st_s ld_s solved x_placed
            a1_y y_in y_sq gn_ready a1_ytr yt_ready a1_wo h3_ready out_ready
            var_ready rstd_ready temp_in temp_out t1_ones amix_zero dve_chain act_chain pool_chain""".split()
        S = {n: sem(n) for n in names}
        ld_x = [sem(f"ld_x{ch}") for ch in range(PCH)]
        ld_w = [[sem(f"ld_w{l}_{e}") for e in range(NEXP)] for l in range(2)]
        order = ["tok1", "tok2", "a0_0", "f0_0", "a0_1", "f0_1", "h2_0", "h2_1", "gn_0", "h3_0",
                 "gn_1", "h3_1", "out_0", "out_1"]
        width = {"tok1": 4, "tok2": 4, "gn_0": 24, "gn_1": 24}

        bx, by, bz = bank[5], bank[6], bank[7]

        def place(copy, dst, quadrants, done):
            src = vals[:].rearrange("p i (g j k) -> p i g j k", g=3, j=4)
            for j in quadrants:
                for b in range(4):
                    copy(dst[32 * j:32 * j + 32, b::4, :, j, :], src[32 * b:32 * b + 32, :, :, j, :]).then_inc(done, 1)

        def after_banks(s):
            return (bx, by, bz) if s else (bank[0], bank[1], bank[2])

        def run(*steps):
            for _ in chain(*steps):
                pass

        def weave(order, **steps):
            for name in order:
                next(steps[name], None)
            for rest in steps.values():
                for _ in rest:
                    pass

        def wait_slots(n):
            for _ in range(n):
                yield

        block = ctx.enter_context(nc.Block())

        def units(m):
            return (3 * (m + 1) + 1) // 2

        def bc(ap, axis, n):
            a = ap.unsqueeze(axis)
            shape = list(a.shape)
            shape[axis] = n
            return a.broadcast_to(shape)

        @block.sync
        def _(sp):
            sp.dma_start(tokp[:], tok_pack).then_inc(S["ld_tok"], 16)
            for ch in range(PCH):
                sp.dma_start(xt[:, ch, :], x_t[:, ch * TOK:(ch + 1) * TOK]).then_inc(ld_x[ch], 16)
            for e in range(NEXP):
                sp.dma_start(wexp[:, e, :], w_l0[e]).then_inc(ld_w[0][e], 16)
            for s in range(HALVES):
                for i in range(2):
                    sp.wait_ge(S["v_ready"], s + 1)
                    sp.wait_ge(S["p_mat"], 2 * s + i + 1)
                    sp.dma_start(p_dram[2 * s + i].rearrange("h p k -> p h k"), pv[:, i]).then_inc(S["st_p"], 16)
                sp.wait_ge(S["st_p"], 32 * (s + 1))
                for i in range(2):
                    src = p_dram[2 * s + i].rearrange("h (b t) k -> (h b) t k", t=T)
                    sp.dma_start(sysm[:, i], src).then_inc(S["ld_g"], 16)
                sp.wait_ge(S["solved"], s + 1)
                for i in range(2):
                    dst = s_dram[2 * s + i].rearrange("h (b t) k -> (h b) t k", t=T)
                    sp.dma_start(dst, sysm[:, i, :, T:]).then_inc(S["st_s"], 16)
                sp.wait_ge(S["st_s"], 32 * (s + 1))
                for i in range(2):
                    sp.dma_start(vals[:, i].rearrange("p (h k) -> p h k", h=HEADS),
                                 s_dram[2 * s + i].rearrange("h p k -> p h k")).then_inc(S["ld_s"], 16)
            for s in range(HALVES):
                sp.wait_ge(S["out_ready"], s + 1)
                for i in range(2):
                    t = 2 * s + i
                    sp.dma_start(out[t], pre[:, t, :]).then_inc(S["st_out"], 16)
            sp.wait_ge(S["st_out"], 16 * TILES)

        @block.tensor
        def _(pe):
            mm = nc.tensor.matmul

            def tokens():
                pe.wait_ge(S["ld_const"], 16)
                pe.wait_ge(S["wtok_scaled"], 1)
                for ch in range(PCH):
                    pe.wait_ge(ld_x[ch], 16)
                    for t in range(TILES):
                        last = mm(bank[t][:, 0:D], xt[:, ch, t * 128:(t + 1) * 128], wtok[:, ch, :],
                                  start=ch == 0, stop=ch == PCH - 1)
                last.then_inc(S["tok_y"], 1)
                pe.wait_ge(S["xsq_ready"], PCH)
                for t in range(TILES):
                    for ch in range(PCH):
                        last = mm(bank[4][:, t:t + 1], xsq[:, ch, t * 128:(t + 1) * 128], c("one"),
                                  start=ch == 0, stop=ch == PCH - 1)
                last.then_inc(S["tok_ss"], 1)

            def composites():
                pe.wait_ge(S["ld_att0"], 32)
                for j in range(3):
                    mm(bank[5 + j][:, 0:D], lora_w[:, j, 0, 0:128], lora_w[:, j, 1, :], start=True, stop=True)
                    last = mm(bank[5 + j][0:D1, D:2 * D], lora_w[:, j, 0, 128:D], lora_w[:, j, 1, :],
                              start=True, stop=True)
                last.then_inc(S["lora_mm"], 1)
                pe.wait_ge(S["wn_ready"], 1)
                for j in range(3):
                    for e0, e1, o in ((0, 128, 0), (128, D + 1, D)):
                        mm(bank[5 + j][0:e1 - e0, o:o + D], wn[:, 0, j, e0:e1], wt[:, 0, j, :],
                           start=True, stop=False)
                        last = mm(bank[5 + j][0:e1 - e0, o:o + D], wn[0:D1, 1, j, e0:e1], wt[0:D1, 1, j, :],
                                  start=False, stop=True)
                    last.then_inc(S["comp_mm"], 1)
                pe.wait_ge(S["y_ready"], TILES)
                mm(bank[0][:, 0:T * HEADS], c("anti16", T), rel[0:T, :], start=True, stop=True).then_inc(S["posb_mm"], 1)

            def transpose_half(src, s, dst):
                for i in range(2):
                    t = 2 * s + i
                    nc.tensor.transpose(dst[:, i * 128:(i + 1) * 128], src[:, t, 0:128], c("ident"))
                    tail = src[:, t, 128:D]
                    last = nc.tensor.transpose(dst[0:D1, HT + i * 128:HT + (i + 1) * 128], tail, c("ident"))
                return last


            def attention0(s):
                pe.wait_ge(S["h0_ready"], s + 1)
                pe.wait_ge(S["comp_ready"], 1)
                if s:
                    pe.wait_ge(S["acc_init"], s)
                transpose_half(h0, s, bx).then_inc(S["a0_tr"], 1)
                yield
                pe.wait_ge(S["a0_ft"], 2 * (s + 1))
                pe.wait_ge(S["ones_set"], 2)
                fa, fb = f0[0][:, s, :], f1[0][0:D1 + 1, s, :]
                for j, bk in ((1, bz), (0, by)):
                    for lo, hi, o in ((0, 128, 0), (128, D, HT)):
                        mm(bk[0:hi - lo, o:o + HT], cw0[:, j, lo:hi], fa, start=True, stop=False)
                        last = mm(bk[0:hi - lo, o:o + HT], cw1[0:D1 + 1, j, lo:hi], fb, start=False, stop=True)
                    last.then_inc(S["a0_q" if j == 0 else "a0_k"], 1)
                for i in range(2):
                    t = slice(i * 128, (i + 1) * 128)
                    mm(bx[:, i * D:(i + 1) * D], fa[:, t], cw0[:, 2, :], start=True, stop=False)
                    mm(bx[:, i * D:(i + 1) * D], fb[:, t], cw1[0:D1 + 1, 2, :], start=False, stop=True)
                    o = bx[:, 2 * D + i * 24:2 * D + (i + 1) * 24]
                    mm(o, fa[:, t], wgx[:, 0, :, :].rearrange("p h a -> p (h a)"), start=True, stop=False)
                    last = mm(o, fb[0:D1, t], wgx[0:D1, 1, :, :].rearrange("p h a -> p (h a)"), start=False, stop=True)
                last.then_inc(S["a0_v"], 1)
                yield
                pe.wait_ge(S["q_ready"], 2 * (s + 1))
                for i, bk in enumerate((by, bz)):
                    pe.wait_ge(S["kx_ready"], 2 * s + 2)
                    kxa, kxb = expanded(i)
                    for b in range(4):
                        o, n = bk[32 * b:32 * b + 32, :], 4 * i + b
                        mm(o[:, 0:256], q0[:, 32 * n:32 * n + 32], kxa[:, b].rearrange("p h k -> p (h k)"),
                           start=True, stop=True)
                        last = mm(o[:, 256:384], q1[:, 32 * n:32 * n + 32], kxb[:, b].rearrange("p h k -> p (h k)"),
                                  start=True, stop=True)
                    last.then_inc(S["a0_s"], 1)
                yield
                pe.wait_ge(S["v_out"], s + 1)
                for i, bk in enumerate((bx, by)):
                    pe.wait_ge(S["p_ready"], 2 * s + i + 1)
                    p = prob[:, i].rearrange("p h k -> p (h k)")
                    for g in range(3):
                        last = nc.tensor.transpose(bk[:, g * 128:(g + 1) * 128], p[:, g * 128:(g + 1) * 128], c("ident"))
                    last.then_inc(S["a0_pt"], 1)
                    yield
                pe.wait_ge(S["v_placed"], 16 * (s + 1))
                for i in range(2):
                    pe.wait_ge(S["pt_ready"], 2 * s + i + 1)
                    for b in range(4):
                        n = 4 * i + b
                        for g in range(3):
                            o = bz[64 * (g % 2):64 * (g % 2) + 64, HT * (g // 2) + 32 * n:HT * (g // 2) + 32 * n + 32]
                            last = mm(o, vx[:, n, g].rearrange("p h k -> p (h k)"), ptr[:, i, g, 32 * b:32 * b + 32],
                                      start=True, stop=True)
                last.then_inc(S["a0_ctx"], 1)
                yield
                pe.wait_ge(S["ct_ready"], 2 * (s + 1))
                for i in range(2):
                    o = bx[:, i * D:(i + 1) * D]
                    mm(o, ct0[:, i * 128:(i + 1) * 128], wo0[:, 0, :], start=True, stop=False)
                    last = mm(o, ct1[0:D1 + 1, i * 128:(i + 1) * 128], wo0[0:D1 + 1, 1, :], start=False, stop=True)
                last.then_inc(S["a0_wo"], 1)
                yield

            def route(l, s):
                n = 2 * l + s
                pa, pb, pc = after_banks(1 if l == 0 else s)
                if l == 0:
                    pe.wait_ge(S["x_ready"], s + 1)
                else:
                    pe.wait_ge(S["h3_ready"], s + 1)
                if n == 0:
                    pe.wait_ge(S["ld_att1"], 16)
                transpose_half(xffn if l == 0 else h3, s, pb).then_inc(S["ff_tr"], 1)
                yield
                pe.wait_ge(S["ff_ft"], 3 * (n + 1))
                for i in range(2):
                    o = pc[:, i * NEXP:(i + 1) * NEXP]
                    mm(o, f0[1 + 2 * l][:, s, i * 128:(i + 1) * 128], router[l][:, 0, :], start=True, stop=False)
                    last = mm(o, f1[1 + 2 * l][0:D1, s, i * 128:(i + 1) * 128], router[l][0:D1, 1, :],
                              start=False, stop=True)
                last.then_inc(S["ff_lg"], 1)
                yield
                if l:
                    pe.wait_ge(S["gts_ready"], n + 1)
                    for i in range(2):
                        last = nc.tensor.transpose(pa[0:NEXP, i * 128:(i + 1) * 128], gts[:, 2 * s + i, :], c("ident"))
                    last.then_inc(S["gt_tr"], 1)
                    pe.wait_ge(S["gt_ev"], s + 1)
                    for i in range(2):
                        last = mm(pb[:, i * D:(i + 1) * D], gts_t[:, i, :], b2, start=True, stop=True)
                    last.then_inc(S["b2_mm"], 1)

            def up(l, s, e):
                ph = 2 * l + s
                pe.wait_ge(ld_w[l][e], 16)
                fa, fb = f0[1 + 2 * l][:, s, :], f1[1 + 2 * l][:, s, :]
                for jp in range(3):
                    n = (ph * NEXP + e) * 3 + jp
                    if n >= 4 and n % 2 == 0:
                        pe.wait_ge(S["h_act"], 2 * (n // 2 - 1))
                    outs = [bank[2 * (n // 2 % 2) + a][:, (n % 2) * HT:(n % 2 + 1) * HT] for a in range(2)]
                    for a in range(2):
                        j = 2 * jp + a
                        mm(outs[a], wexp[:, e, j * 128:(j + 1) * 128], fa, start=True, stop=False)
                    for a in range(2):
                        o = DFF + jp * 128
                        last = mm(outs[a], wexp[64 * a:64 * a + 64, e, o:o + 128], fb[64 * a:64 * a + 64, :],
                                  start=False, stop=True)
                    if n % 2:
                        last.then_inc(S["h_mm"], 1)

            def down(l, s, e):
                n = (2 * l + s) * NEXP + e
                pe.wait_ge(S["h_act"], 2 * units(n))
                if n >= 1:
                    pe.wait_ge(S["y_act"], n)
                w2 = wexp[:, e, DFF + DFF // 2:].rearrange("p (j n) -> p j n", j=FCH)
                for i in range(2):
                    for j in range(FCH):
                        last = mm(bank[4][:, i * D:(i + 1) * D], hid[:, n % 2, j, i * 128:(i + 1) * 128],
                                  w2[:, j, :], start=j == 0, stop=j == FCH - 1)
                last.then_inc(S["y_mm"], 1)

            def experts(l, s, between=()):
                pe.wait_ge(S["acc_init"], 2 * l + s + 1)
                between = iter(between)
                for e in range(NEXP):
                    up(l, s, e)
                    next(between, None)
                    if e:
                        down(l, s, e - 1)
                        next(between, None)
                down(l, s, NEXP - 1)
                for _ in between:
                    pass

            def pre1(s):
                pe.wait_ge(S["h2_ready"], s + 1)
                transpose_half(h2, s, bx).then_inc(S["a1_tr"], 1)
                for i in range(2):
                    t = 2 * s + i
                    mm(by[:, i * 128:(i + 1) * 128], h2[:, t, 0:128], c("shift"), start=True, stop=True)
                    last = mm(by[0:D1, HT + i * 128:HT + (i + 1) * 128], h2[:, t, 128:D], c("shift"),
                              start=True, stop=True)
                last.then_inc(S["a1_dx"], 1)
                yield
                pe.wait_ge(S["a1_xx"], s + 1)
                for lo, hi, o in ((0, 128, 0), (128, 160, HT)):
                    mm(bz[0:hi - lo, o:o + HT], maa_w1[:, 0, lo:hi], xx0, start=True, stop=False)
                    last = mm(bz[0:hi - lo, o:o + HT], maa_w1[0:D1, 1, lo:hi], xx1, start=False, stop=True)
                last.then_inc(S["a1_mt"], 1)
                yield
                pe.wait_ge(S["mt_ready"], 2 * (s + 1))
                for n, m in enumerate(MIX_ORDER):
                    if n >= 3:
                        pe.wait_ge(S["a1_xd"], MIX * s + n - 2)
                    p = 32 * (m % 4)
                    w = maa_w2[p:p + 32, m // 4, :]
                    x = mt0[p:p + 32, :] if m < 4 else mt1
                    bk = (bx, by, bz)[n % 3]
                    mm(bk[:, 0:HT], w[:, 0:128], x, start=True, stop=True)
                    mm(bk[0:D1, HT:], w[:, 128:D], x, start=True, stop=True).then_inc(S["a1_mm"], 1)
                    if n in (1, 4):
                        yield

                def mixed_t(bk, m, w):
                    for lo, hi, o in ((0, 128, 0), (128, D, HT)):
                        mm(bk[0:hi - lo, o:o + HT], w4[:, 0, w, lo:hi], xc0[:, m, :], start=True, stop=False)
                        last = mm(bk[0:hi - lo, o:o + HT], w4[0:D1, 1, w, lo:hi], xc1[:, m, :], start=False, stop=True)
                    return last

                def mixed(bk, m, w):
                    for i in range(2):
                        o = bk[:, i * D:(i + 1) * D]
                        mm(o, xc0[:, m, i * 128:(i + 1) * 128], w4[:, 0, w, :], start=True, stop=False)
                        last = mm(o, xc1[:, m, i * 128:(i + 1) * 128], w4[0:D1, 1, w, :], start=False, stop=True)
                    return last

                pe.wait_ge(S["xc_ready"], MIX * s + 1)
                pe.wait_ge(S["a1_xd"], MIX * s + 3)
                mixed_t(bz, 1, 1).then_inc(S["a1_k"], 1)
                yield
                pe.wait_ge(S["xc_ready"], MIX * s + 2)
                pe.wait_ge(S["a1_xd"], MIX * s + 5)
                mixed(by, 2, 2).then_inc(S["a1_v"], 1)
                pe.wait_ge(S["ksq_ready"], s + 1)
                mm(bx[:, 0:HT], c("headsum"), ksq0, start=True, stop=True)
                mm(bx[0:D1, HT:], c("headsum", D1)[:, 0:D1], ksq1, start=True, stop=True).then_inc(S["a1_n2"], 1)
                yield
                for i, bk in enumerate((bz, bx)):
                    pe.wait_ge(S["kn_ready"], 2 * s + i + 1)
                    pair_product(bk, kn0[:, 128 * i:128 * i + 128], kn1[:, 128 * i:128 * i + 128], i)\
                        .then_inc(S["a1_gram"], 1)
                yield
                pe.wait_ge(S["xc_ready"], MIX * s + 3)
                pe.wait_ge(S["v_ready"], s + 1)
                mm(by[0:64, 0:HT], dw1[:, 0, :], xc0[:, 0, :], start=True, stop=False)
                mm(by[0:64, 0:HT], dw1[0:D1, 1, :], xc1[:, 0, :], start=False, stop=True).then_inc(S["a1_t1"], 1)
                yield
                pe.wait_ge(S["xc_ready"], MIX * s + 5)
                pe.wait_ge(S["gram_in"], 2 * s + 1)
                mixed_t(bz, 3, 0).then_inc(S["a1_r"], 1)
                pe.wait_ge(S["gram_in"], 2 * s + 2)
                mixed(bx, 4, 3).then_inc(S["a1_g"], 1)
                pe.wait_ge(S["t1_ready"], s + 1)
                pe.wait_ge(S["t1_ones"], 1)
                for i in range(2):
                    last = mm(by[:, i * D:(i + 1) * D], t1[0:65, i * 128:(i + 1) * 128], dw2[0:65, :],
                              start=True, stop=True)
                last.then_inc(S["a1_w"], 1)
                yield
                pe.wait_ge(S["ew_ready"], s + 1)
                pe.wait_ge(S["rk_ready"], s + 1)
                for i in range(2):
                    mm(by[:, i * 256:(i + 1) * 256], ew[:, i, 0:128], c("cums"), start=True, stop=True)
                    last = mm(bz[0:D1, i * 256:(i + 1) * 256], ew[:, i, 128:D], c("cums"), start=True, stop=True)
                last.then_inc(S["a1_cs"], 1)
                yield
                pe.wait_ge(S["g_raw"], s + 1)
                for i, banks in enumerate(((bx, by), (bz, bx))):
                    pe.wait_ge(S["dk_ready"], 2 * s + i + 1)
                    for m in range(2):
                        if i == 1 and m == 1:
                            pe.wait_ge(S["a_mix"], 2 * s + 1)
                        last = pair_product(banks[m], ex0[:, m, i, :], ex1[:, m, i, :], (2 + 2 * i + m) % 4)
                    last.then_inc(S["a1_ab"], 1)
                    yield
                for i, bk in enumerate((by, bx)):
                    pe.wait_ge(S["a_mix"], 2 * s + i + 1)
                    a = amix[:, i].rearrange("p h k -> p (h k)")
                    for g in range(3):
                        last = nc.tensor.transpose(bk[:, g * 128:(g + 1) * 128], a[:, g * 128:(g + 1) * 128], c("ident"))
                    last.then_inc(S["a1_at"], 1)
                    yield

            def pair_product(bk, left0, left1, slot):
                xa, xb = expanded(slot)
                for b in range(4):
                    o = bk[32 * b:32 * b + 32, :]
                    mm(o[:, 0:256], left0[:, 32 * b:32 * b + 32], xa[:, b].rearrange("p h k -> p (h k)"),
                       start=True, stop=True)
                    last = mm(o[:, 256:384], left1[:, 32 * b:32 * b + 32], xb[:, b].rearrange("p h k -> p (h k)"),
                              start=True, stop=True)
                return last

            def post1(s):
                pa, pb, pc = after_banks(s)
                pe.wait_ge(S["at_ready"], 2 * (s + 1))
                pe.wait_ge(S["x_placed"], 16 * (s + 1))
                for i in range(2):
                    for b in range(4):
                        n = 4 * i + b
                        for g in range(3):
                            last = mm(pc[32 * b:32 * b + 32, i * D + g * 64:i * D + (g + 1) * 64],
                                      atr[:, i, g, 32 * b:32 * b + 32], vx1[:, n, g].rearrange("p h k -> p (h k)"),
                                      start=True, stop=True)
                last.then_inc(S["a1_y"], 1)
                yield
                pe.wait_ge(S["gn_ready"], s + 1)
                transpose_half(gsq, 0, pa).then_inc(S["a1_ytr"], 1)
                yield
                pe.wait_ge(S["yt_ready"], 2 * (s + 1))
                for i in range(2):
                    o = pc[:, i * D:(i + 1) * D]
                    mm(o, ct0[:, i * 128:(i + 1) * 128], wo1[:, 0, :], start=True, stop=False)
                    last = mm(o, ct1[0:D1, i * 128:(i + 1) * 128], wo1[0:D1, 1, :], start=False, stop=True)
                last.then_inc(S["a1_wo"], 1)
                yield

            tokens()
            composites()
            run(attention0(0), route(0, 0))
            experts(0, 0, chain(attention0(1), wait_slots(1), route(0, 1)))
            experts(0, 1, pre1(0))
            second = pre1(1)
            weave("apapapapapap", a=chain(post1(0), route(1, 0)), p=islice(second, 6))
            experts(1, 0, chain(second, wait_slots(2), post1(1), route(1, 1)))
            experts(1, 1)

        @block.scalar
        def _(act):
            count = [0]

            def link(ins):
                count[0] += 1
                ins.then_inc(S["act_chain"], 1)
                act.wait_ge(S["act_chain"], count[0])

            f = nc.scalar.activation

            def loads():
                act.dma_start(con[:], consts).then_inc(S["ld_const"], 16)
                act.dma_start(row[:], rows.partition_broadcast(128)).then_inc(S["ld_row"], 16)
                act.dma_start(att0[:], att0_pack).then_inc(S["ld_att0"], 16)
                act.dma_start(lora[:], lora_pack).then_inc(S["ld_att0"], 16)
                act.dma_start(att1[:], att1_pack).then_inc(S["ld_att1"], 16)

            def tokens():
                for ch in range(PCH):
                    act.wait_ge(ld_x[ch], 16)
                    f(xsq[:, ch, :], xt[:, ch, :], ACT.Square).then_inc(S["xsq_ready"], 1)
                for t in range(TILES):
                    act.wait_ge(S["y_ready"], t + 1)
                    f(pre[:, t, :], h0[:, t, :], ACT.Square, accum_out=ss[:, 1, t:t + 1]).then_inc(S["y_sq2"], 1)

            def copy_ft(n, s, src, ready, got, inc, full=False):
                act.wait_ge(S[ready], got)
                f(f0[n][:, s, :], src[:, 0:HT], ACT.Copy).then_inc(S[inc], 1)
                f(f1[n][0:D1, s, :], src[0:D1, HT:2 * HT], ACT.Copy).then_inc(S[inc], 1)
                if full:
                    f(f1[n][D1:128, s, :], src[0:D1, HT:2 * HT], ACT.Copy).then_inc(S[inc], 1)

            def attention0(s):
                copy_ft(0, s, bx, "a0_tr", s + 1, "a0_ft")
                yield
                act.wait_ge(S["a0_q"], s + 1)
                f(q0, by[:, 0:HT], ACT.Copy).then_inc(S["q_ready"], 1)
                f(q1, by[0:D1, HT:], ACT.Copy).then_inc(S["q_ready"], 1)
                act.wait_ge(S["gate_in"], s + 1)
                f(vals[:].rearrange("p i k -> p (i k)"), bx[:, 0:2 * D], ACT.Copy).then_inc(S["v_out"], 1)
                g = gates0[:].rearrange("p i h a -> p (i h a)")
                f(g, g, ACT.Exp, scale=-1.0).then_inc(S["gate_exp"], 1)
                yield
                act.wait_ge(S["v_out"], s + 1)
                act.wait_ge(S["vx_zero"], 1)
                place(lambda o, x: f(o, x, ACT.Copy), vx, (0, 1), S["v_placed"])
                yield
                for i, bk in enumerate((bx, by)):
                    act.wait_ge(S["s_shift"], 2 * s + i + 1)
                    p = prob[:, i].rearrange("p h k -> p (h k)")
                    f(p, p, ACT.Exp).then_inc(S["s_exp"], 1)
                    if i:
                        act.wait_ge(S["a0_pt"], 2 * s + 1)
                        f(ptr[:, 0].rearrange("p g k -> p (g k)"), bx[:, 0:384], ACT.Copy).then_inc(S["pt_ready"], 1)
                    yield
                act.wait_ge(S["a0_pt"], 2 * s + 2)
                f(ptr[:, 1].rearrange("p g k -> p (g k)"), by[:, 0:384], ACT.Copy).then_inc(S["pt_ready"], 1)
                act.wait_ge(S["a0_ctx"], s + 1)
                f(ct0[:], bz[:, 0:HT], ACT.Copy).then_inc(S["ct_ready"], 1)
                f(ct1[0:D1, :], bz[0:D1, HT:], ACT.Copy).then_inc(S["ct_ready"], 1)
                yield

            def route(l, s):
                n = 2 * l + s
                pa, pb, pc = after_banks(1 if l == 0 else s)
                copy_ft(1 + 2 * l, s, pb, "ff_tr", n + 1, "ff_ft", full=True)
                yield
                act.wait_ge(S["top_in"], n + 1)
                f(topd[:, :, 1:2], topd[:, :, 0:1], ACT.Exp).then_inc(S["top_exp"], 1)
                yield
                if l:
                    act.wait_ge(S["gt_tr"], s + 1)
                    f(gts_t[:].rearrange("p i k -> p (i k)"), pa[0:NEXP, 0:256], ACT.Copy).then_inc(S["gt_ev"], 1)

            def up(l, s, u):
                u += (2 * l + s) * 12
                m = (2 * u + 1) // 3
                if m >= 2:
                    act.wait_ge(S["y_mm"], m - 1)
                act.wait_ge(S["h_mm"], u + 1)
                chunks = hid.rearrange("p a j n -> p (a j) n")
                for a in range(2):
                    src = bank[2 * (u % 2) + a]
                    if l == 0:
                        at = 4 * (u % 3) + a
                        f(chunks[:, at:at + 3:2, :], src[:].rearrange("p (j n) -> p j n", j=2), ACT.Silu)\
                            .then_inc(S["h_act"], 1)
                    else:
                        for j in range(2):
                            ch = 4 * u + a + 2 * j
                            ins = f(chunks[:, ch % 12, :], src[:, j * HT:(j + 1) * HT], ACT.Gelu,
                                    bias=b1[:, ch % (NEXP * FCH):ch % (NEXP * FCH) + 1])
                        ins.then_inc(S["h_act"], 1)

            def down(l, s, e):
                m = (2 * l + s) * NEXP + e
                act.wait_ge(S["y_mm"], m + 1)
                if m >= 2:
                    act.wait_ge(S["acc_add"], m - 1)
                for i in range(2):
                    ins = f(ysc[:, m % 2, i, :], bank[4][:, i * D:(i + 1) * D], ACT.Copy,
                            scale=gts[:, 2 * s + i, e:e + 1])
                ins.then_inc(S["y_act"], 1)
                if l == 0 and s == 1:
                    act.dma_start(wexp[:, e, :], w_l1[e]).then_inc(ld_w[1][e], 16)

            def experts(l, s, between=()):
                act.wait_ge(S["gts_ready"], 2 * l + s + 1)
                between = iter(between)
                done = 0
                for e in range(NEXP):
                    while done < 3 * (e + 1) // 2:
                        up(l, s, done)
                        done += 1
                    next(between, None)
                    if e:
                        down(l, s, e - 1)
                        next(between, None)
                down(l, s, NEXP - 1)
                for _ in between:
                    pass

            def temperature():
                act.wait_ge(S["temp_in"], 1)
                link(f(temp[:, 1, :], temp[:, 0, :], ACT.Exp, scale=-1.0))
                f(temp[:, 2, :], temp[:, 1, :], ACT.Ln, bias=c("one")).then_inc(S["temp_out"], 1)

            def pre1(s):
                copy_ft(2, s, bx, "a1_tr", s + 1, "a1_ft")
                act.wait_ge(S["a1_dx"], s + 1)
                f(dx0[:], by[:, 0:HT], ACT.Copy).then_inc(S["a1_ft"], 1)
                f(dx1[:], by[0:D1, HT:], ACT.Copy).then_inc(S["a1_ft"], 1)
                yield
                act.wait_ge(S["a1_mt"], s + 1)
                f(mt0, bz[:, 0:HT], ACT.Tanh).then_inc(S["mt_ready"], 1)
                f(mt1, bz[0:32, HT:], ACT.Tanh).then_inc(S["mt_ready"], 1)
                yield
                yield
                yield
                act.wait_ge(S["a1_k"], s + 1)
                link(f(kt0, bz[:, 0:HT], ACT.Copy))
                link(f(kt1, bz[0:D1, HT:], ACT.Copy))
                f(ksq0, kt0, ACT.Square)
                f(ksq1, kt1, ACT.Square).then_inc(S["ksq_ready"], 1)
                yield
                act.wait_ge(S["a1_v"], s + 1)
                f(pv[:, :, :, T:], by[:, 0:2 * D].rearrange("p (i h k) -> p i h k", i=2, h=HEADS), ACT.Copy)\
                    .then_inc(S["v_ready"], 1)
                act.wait_ge(S["a1_n2"], s + 1)
                f(kn0, bx[:, 0:HT], ACT.Sqrt)
                f(kn1, bx[0:D1, HT:], ACT.Sqrt).then_inc(S["n2_ready"], 1)
                yield
                for i in range(2):
                    act.wait_ge(S["gram_in"], 2 * s + i + 1)
                    f(gram[s][i], gram[s][i], ACT.Exp).then_inc(S["gram_exp"], 1)
                yield
                act.wait_ge(S["a1_t1"], s + 1)
                f(t1[0:64, :], by[0:64, 0:HT], ACT.Tanh).then_inc(S["t1_ready"], 1)
                yield
                act.wait_ge(S["a1_w"], s + 1)
                f(ew.rearrange("p i k -> p (i k)"), by[:, 0:2 * D], ACT.Exp).then_inc(S["ew_ready"], 1)
                f(rt0, bz[:, 0:HT], ACT.Copy)
                f(rt1, bz[0:D1, HT:], ACT.Copy).then_inc(S["rk_ready"], 1)
                yield
                act.wait_ge(S["cs_ready"], s + 1)
                for kind, (d, sc) in enumerate(((0, 1.0), (1, -1.0), (0, -1.0), (1, 1.0))):
                    f(ex0[:, kind], cs0[:, :, d, :], ACT.Exp, scale=sc)
                    ins = f(ex1[:, kind], cs1[:, :, d, :], ACT.Exp, scale=sc)
                ins.then_inc(S["ex_ready"], 1)
                yield
                yield
                yield
                for i, bk in enumerate((by, bx)):
                    act.wait_ge(S["a1_at"], 2 * s + i + 1)
                    f(atr[:, i].rearrange("p g k -> p (g k)"), bk[:, 0:384], ACT.Copy).then_inc(S["at_ready"], 1)
                    yield
                act.wait_ge(S["g_raw"], s + 1)
                f(sg[:].rearrange("p i k -> p (i k)"), sg[:].rearrange("p i k -> p (i k)"), ACT.Silu)\
                    .then_inc(S["g_ready"], 1)

            def post1(s):
                pa, pb, pc = after_banks(s)
                act.wait_ge(S["ld_s"], 32 * (s + 1))
                place(lambda o, x: f(o, x, ACT.Copy), vx1, (0, 1), S["x_placed"])
                act.wait_ge(S["y_in"], s + 1)
                f(gsq[:].rearrange("p i k -> p (i k)"), pre[:, 2 * s:2 * s + 2, :].rearrange("p i k -> p (i k)"),
                  ACT.Square).then_inc(S["y_sq"], 1)
                yield
                act.wait_ge(S["a1_ytr"], s + 1)
                f(ct0[:], pa[:, 0:HT], ACT.Copy).then_inc(S["yt_ready"], 1)
                f(ct1[0:D1, :], pa[0:D1, HT:], ACT.Copy).then_inc(S["yt_ready"], 1)
                yield
                yield

            loads()
            tokens()
            temperature()
            run(attention0(0), route(0, 0))
            experts(0, 0, chain(attention0(1), wait_slots(2), route(0, 1)))
            experts(0, 1, pre1(0))
            second = pre1(1)
            weave("apapapapapap", a=chain(post1(0), route(1, 0)), p=islice(second, 6))
            experts(1, 0, chain(second, wait_slots(2), post1(1), route(1, 1)))
            experts(1, 1)

        @block.vector
        def _(dve):
            v = nc.vector
            count = [0]

            def link(ins):
                count[0] += 1
                ins.then_inc(S["dve_chain"], 1)
                dve.wait_ge(S["dve_chain"], count[0])

            def flat(ap):
                return ap.rearrange("p a b -> p (a b)")

            def inv_sqrt(name, n):
                q = order.index(name)
                dve.wait_ge(S["rstd_ready"], q + 1)
                return rstd[:, q % 2, 0:n]

            def ask(name, src, scale, eps):
                q = order.index(name)
                n = width.get(name, 2)
                v.tensor_scalar(var_in[:, q % 2, 0:n], src, scale, eps, ALU.mult, ALU.add).then_inc(S["var_ready"], 1)

            def layer_norm(name, s, src, dst, ready=None):
                for i in range(2):
                    link(v.bn_stats(stats[:, 2 * s + i, :], src[:, 2 * s + i, :]))
                    link(v.bn_aggr(mv[:, 2 * s + i, :], stats[:, 2 * s + i, :]))
                ask(name, mv[:, 2 * s:2 * s + 2, 1], 1.0, LN_EPS)
                rs = inv_sqrt(name, 2)
                for i in range(2):
                    ins = v.tensor_scalar(dst[:, 2 * s + i, :], src[:, 2 * s + i, :], mv[:, 2 * s + i, 0:1],
                                          rs[:, i:i + 1], ALU.subtract, ALU.mult)
                    if i == 1 and ready:
                        ins.then_inc(S[ready], 1)
                        dve.wait_ge(S[ready], s + 1)
                    else:
                        link(ins)

            def tokens():
                dve.wait_ge(S["ld_tok"], 16)
                v.tensor_tensor(wtok, wtok, bc(gin, 2, D), ALU.mult).then_inc(S["wtok_scaled"], 1)
                dve.wait_ge(S["tok_ss"], 1)
                ask("tok1", bank[4][:, 0:4], 1.0 / PATCH_DIM, RMS_EPS)
                rs = inv_sqrt("tok1", 4)
                dve.wait_ge(S["ld_row"], 16)
                dve.wait_ge(S["tok_y"], 1)
                for t in range(TILES):
                    v.scalar_tensor_tensor(h0[:, t, :], bank[t][:, 0:D], rs[:, t:t + 1],
                                           r("b_proj"), ALU.mult, ALU.add).then_inc(S["y_ready"], 1)
                dve.wait_ge(S["y_sq2"], TILES)
                ask("tok2", ss[:, 1, :], 1.0 / D, RMS_EPS)
                rs = inv_sqrt("tok2", 4)
                for t in range(TILES):
                    ins = v.scalar_tensor_tensor(h0[:, t, :], h0[:, t, :], rs[:, t:t + 1], r("g_out"),
                                                 ALU.mult, ALU.mult)
                    if t % 2:
                        ins.then_inc(S["h0_ready"], 1)

            def composites():
                dve.wait_ge(S["ld_att0"], 32)
                dve.wait_ge(S["lora_mm"], 1)
                for j in range(3):
                    v.scalar_tensor_tensor(wn[:, 0, j, 0:D], bank[5 + j][:, 0:D], 0.5, wn[:, 0, j, 0:D],
                                           ALU.mult, ALU.add)
                    ins = v.scalar_tensor_tensor(wn[0:D1, 1, j, 0:D], bank[5 + j][0:D1, D:2 * D], 0.5,
                                                 wn[0:D1, 1, j, 0:D], ALU.mult, ALU.add)
                ins.then_inc(S["wn_ready"], 1)
                dve.wait_ge(S["ld_const"], 16)
                dve.wait_ge(S["ld_row"], 16)
                link(v.tensor_reduce(wgsum[:].rearrange("p c a -> p (c a)"), wg.rearrange("p c a b -> p (c a) b"),
                                     AX.X, ALU.add))
                link(v.tensor_reduce(bgs[:], r("bg").rearrange("p (a b) -> p a b", a=2), AX.X, ALU.add))
                for ch in range(2):
                    link(v.tensor_tensor(wgx[:, ch], bc(wgsum[:, ch, :], 1, HEADS),
                                         bc(c("head12")[:, ch * HEADS:(ch + 1) * HEADS], 2, 2), ALU.mult))
                link(v.tensor_scalar(temp[:, 1, :], r("lucid"), -1.0, None, ALU.mult))
                v.tensor_tensor(temp[:, 0, :], r("lucid"), temp[:, 1, :], ALU.max).then_inc(S["temp_in"], 1)
                for j in range(3):
                    dve.wait_ge(S["comp_mm"], j + 1)
                    sc = HD ** -0.5 if j == 0 else 1.0
                    link(v.tensor_scalar(cw0[:, j, :], bank[5 + j][:, 0:D], sc, None, ALU.mult))
                    link(v.tensor_scalar(cw1[0:D1 + 1, j, :], bank[5 + j][0:D1 + 1, D:2 * D], sc, None, ALU.mult))
                    link(v.scalar_tensor_tensor(cw1[D1:D1 + 1, j, :], b64[D1:D1 + 1, j, :], sc, cw1[D1:D1 + 1, j, :],
                                                ALU.mult, ALU.add))
                dve.wait_ge(S["posb_mm"], 1)
                v.tensor_copy(posb[:], bank[0][:, 0:T * HEADS].rearrange("p (k h) -> p k h", h=HEADS))\
                    .then_inc(S["comp_ready"], 1)
                dve.wait_ge(S["comp_ready"], 1)
                dve.wait_ge(S["temp_out"], 1)
                link(v.scalar_tensor_tensor(temp[:, 0, :], r("lucid"), 0.0, temp[:, 2, :], ALU.max, ALU.add))

            def expand(slot, a, d):
                xa, xb = expanded(slot)
                v.tensor_tensor(xa, bc(a, 2, 8), bc(bc(c("head8"), 1, 4), 3, 32), ALU.mult)
                return v.tensor_tensor(xb, bc(d, 2, 4), bc(bc(c("head8", D1)[:, 0:4], 1, 4), 3, 32), ALU.mult)

            def blocks(tile_, i):
                return tile_[:, 128 * i:128 * i + 128].rearrange("p (b k) -> p b k", b=4)

            def attention0(s):
                dve.wait_ge(S["a0_k"], s + 1)
                for i in range(2):
                    expand(i, blocks(bz[:, 0:HT], i), blocks(bz[0:D1, HT:], i)).then_inc(S["kx_ready"], 1)
                dve.wait_ge(S["a0_v"], s + 1)
                gr = gates0.rearrange("p i h a -> p (i h) a")
                v.tensor_tensor(gr, bx[:, 2 * D:2 * D + 48].rearrange("p (n a) -> p n a", a=2), bc(bgs[:], 1, 24),
                                ALU.add).then_inc(S["gate_in"], 1)
                dve.wait_ge(S["v_out"], s + 1)
                dve.wait_ge(S["vx_zero"], 1)
                place(v.tensor_copy, vx, (2, 3), S["v_placed"])
                dve.wait_ge(S["gate_exp"], s + 1)
                g = flat(gr)
                link(v.tensor_scalar(g, g, 1.0, None, ALU.add))
                link(v.reciprocal(g, g))
                ga, gb = gates0[:, :, :, 0], gates0[:, :, :, 1]
                link(v.tensor_tensor(gb, gb, bc(r("gru"), 1, 2), ALU.mult))
                link(v.scalar_tensor_tensor(gate[:], gb, -1.0, ga, ALU.add, ALU.mult))
                link(v.tensor_scalar(gate[:], gate[:], 2.0, None, ALU.add))
                for i in range(2):
                    link(v.tensor_tensor(gbias[:, i], bc(gate[:, i, :], 2, T), posb[:].rearrange("p k h -> p h k"),
                                         ALU.mult))
                for i in range(2):
                    p = prob[:, i]
                    dve.wait_ge(S["a0_s"], 2 * s + i + 1)
                    link(v.tensor_tensor(p, (by, bz)[i][:, 0:384].rearrange("p (h k) -> p h k", h=HEADS),
                                         bc(c("off_pair"), 1, HEADS), ALU.add))
                    p4 = p.rearrange("p h (b k) -> p h b k", b=2)
                    link(v.tensor_tensor(p4, p4, bc(gbias[:, i], 2, 2), ALU.add))
                    link(v.tensor_reduce(smax[:, i], p, AX.X, ALU.max))
                    v.tensor_tensor(p, p, bc(smax[:, i], 2, 32), ALU.subtract).then_inc(S["s_shift"], 1)
                for i in range(2):
                    p = prob[:, i]
                    dve.wait_ge(S["s_exp"], 2 * s + i + 1)
                    link(v.tensor_reduce(smax[:, i], p, AX.X, ALU.add))
                    link(v.reciprocal(smax[:, i], smax[:, i]))
                    v.tensor_tensor(p, p, bc(smax[:, i], 2, 32), ALU.mult).then_inc(S["p_ready"], 1)
                dve.wait_ge(S["a0_wo"], s + 1)
                a = slice(2 * s, 2 * s + 2)
                v.tensor_tensor(pre[:, a, :], bx[:, 0:2 * D].rearrange("p (i k) -> p i k", i=2), h0[:, a, :],
                                ALU.add).then_inc(S["wo_read"], 1)
                dve.wait_ge(S["wo_read"], s + 1)
                layer_norm(f"a0_{s}", s, pre, h1)
                layer_norm(f"f0_{s}", s, h1, xffn)
                link(v.tensor_tensor(xffn[:, a, :], xffn[:, a, :], bc(r("ln_gamma"), 1, 2), ALU.mult))
                v.tensor_tensor(xffn[:, a, :], xffn[:, a, :], bc(r("ln_beta"), 1, 2), ALU.add)\
                    .then_inc(S["x_ready"], 1)

            def route(l, s):
                n = 2 * l + s
                pa, pb, pc = after_banks(1 if l == 0 else s)
                dve.wait_ge(S["ff_lg"], n + 1)
                src = pc[:, 0:2 * NEXP].rearrange("p (i k) -> p i k", i=2)
                if l == 0:
                    link(v.tensor_copy(lg[:], src))
                else:
                    link(v.tensor_tensor(lg[:], src, bc(r("gate_b"), 1, 2), ALU.add))
                for i in range(2):
                    link(v.max(top[:, i, :], lg[:, i, :]))
                    link(v.max_index(topi[:, i, :], top[:, i, :], lg[:, i, :]))
                v.tensor_tensor(topd[:, :, 0:1], top[:, :, 1:2], top[:, :, 0:1], ALU.subtract).then_inc(S["top_in"], 1)
                yield
                link(v.tensor_copy(topf[:], topi[:, :, 0:2]))
                dve.wait_ge(S["top_exp"], n + 1)
                link(v.tensor_scalar(topd[:, :, 2:3], topd[:, :, 1:2], 1.0, None, ALU.add))
                link(v.reciprocal(topd[:, :, 2:3], topd[:, :, 2:3]))
                link(v.tensor_tensor(topd[:, :, 1:2], topd[:, :, 1:2], topd[:, :, 2:3], ALU.mult))
                for k in range(2):
                    link(v.tensor_tensor(hot[:, k], bc(c("iota8"), 1, 2), topf[:, :, k:k + 1].broadcast_to([128, 2, NEXP]),
                                         ALU.is_equal))
                    link(v.tensor_tensor(hot[:, k], hot[:, k],
                                         topd[:, :, 2 - k:3 - k].broadcast_to([128, 2, NEXP]), ALU.mult))
                a = slice(2 * s, 2 * s + 2)
                v.tensor_tensor(gts[:, a, :], hot[:, 0], hot[:, 1], ALU.add).then_inc(S["gts_ready"], 1)
                if l == 0:
                    v.tensor_scalar(acc[:, a, :], h1[:, a, :], 2.0, None, ALU.mult).then_inc(S["acc_init"], 1)
                else:
                    yield
                    dve.wait_ge(S["b2_mm"], s + 1)
                    v.tensor_tensor(acc[:, a, :], pb[:, 0:2 * D].rearrange("p (i k) -> p i k", i=2), h3[:, a, :],
                                    ALU.add).then_inc(S["acc_init"], 1)

            def pre1(s):
                fa, fb = f0[2][:, s, :], f1[2][0:D1, s, :]
                dve.wait_ge(S["ld_att1"], 16)
                dve.wait_ge(S["a1_ft"], 4 * (s + 1))
                v.scalar_tensor_tensor(xx0[:], dx0[:], maa[:, 0, 0:1], fa, ALU.mult, ALU.add)
                v.scalar_tensor_tensor(xx1[:], dx1[:], maa[0:D1, 1, 0:1], fb, ALU.mult, ALU.add)\
                    .then_inc(S["a1_xx"], 1)
                yield
                for n, m in enumerate(MIX_ORDER):
                    dve.wait_ge(S["a1_mm"], MIX * s + n + 1)
                    bk = (bx, by, bz)[n % 3]
                    v.scalar_tensor_tensor(xc0[:, m, :], bk[:, 0:HT], maa[:, 0, 1 + m:2 + m], dx0, ALU.add, ALU.mult)
                    v.scalar_tensor_tensor(xc1[:, m, :], bk[0:D1, HT:], maa[0:D1, 1, 1 + m:2 + m], dx1,
                                           ALU.add, ALU.mult).then_inc(S["a1_xd"], 1)
                    if n in (1, 4):
                        yield
                dve.wait_ge(S["n2_ready"], s + 1)
                for kn, kt in ((kn0, kt0), (kn1, kt1)):
                    link(v.tensor_scalar(kn, kn, 1e-12, None, ALU.max))
                    link(v.reciprocal(kn, kn))
                    link(v.tensor_tensor(kn, kn, kt, ALU.mult))
                for i in range(2):
                    expand(i, blocks(kn0, i), blocks(kn1, i)).then_inc(S["kn_ready"], 1)
                yield
                for i, bk in enumerate((bz, bx)):
                    dve.wait_ge(S["a1_gram"], 2 * s + i + 1)
                    link(v.tensor_tensor(gram[s][i], bk[:, 0:384].rearrange("p (h k) -> p h k", h=HEADS),
                                         bc(temp[:, 0, :], 2, 32), ALU.mult))
                    v.tensor_scalar(gram[s][i], gram[s][i], -20.0, 20.0, ALU.max, ALU.min).then_inc(S["gram_in"], 1)
                yield
                for i in range(2):
                    dve.wait_ge(S["gram_exp"], 2 * s + i + 1)
                    link(v.tensor_scalar(pmat[:, i], gram[s][i][:, :, 0:T], c("even"), None, ALU.mult))
                    link(v.scalar_tensor_tensor(pmat[:, i], gram[s][i][:, :, T:], c("odd"), pmat[:, i],
                                                ALU.mult, ALU.add))
                    v.tensor_tensor(pmat[:, i], pmat[:, i], bc(c("eye16"), 1, HEADS), ALU.add)\
                        .then_inc(S["p_mat"], 1)
                yield
                dve.wait_ge(S["a1_g"], s + 1)
                v.tensor_copy(flat(sg), bx[:, 0:2 * D]).then_inc(S["g_raw"], 1)
                yield
                dve.wait_ge(S["a1_cs"], s + 1)
                v.tensor_scalar(cs0.rearrange("p i d k -> p (i d k)"), by[:], -60.0, 60.0, ALU.max, ALU.min)
                v.tensor_scalar(cs1.rearrange("p i d k -> p (i d k)"), bz[0:D1, :], -60.0, 60.0,
                                ALU.max, ALU.min).then_inc(S["cs_ready"], 1)
                yield
                dve.wait_ge(S["ex_ready"], s + 1)
                dve.wait_ge(S["rk_ready"], s + 1)
                for ex, rt, kt in ((ex0, rt0, kt0), (ex1, rt1, kt1)):
                    for kind in range(4):
                        op = rt if kind < 2 else kt
                        link(v.tensor_tensor(ex[:, kind], ex[:, kind], op.rearrange("p (i k) -> p i k", i=2), ALU.mult))
                for i in range(2):
                    for m in range(2):
                        ins = expand((2 + 2 * i + m) % 4, ex0[:, 2 + m, i].rearrange("p (b k) -> p b k", b=4),
                                     ex1[:, 2 + m, i].rearrange("p (b k) -> p b k", b=4))
                    ins.then_inc(S["dk_ready"], 1)
                    yield
                for i, banks in enumerate(((bx, by), (bz, bx))):
                    dve.wait_ge(S["a1_ab"], 2 * s + i + 1)
                    for mask, bk in zip(("lower", "upper"), banks):
                        ins = v.copy_predicated(amix[:, i], bc(c(mask), 1, HEADS).bitcast(I32),
                                                bk[:, 0:384].rearrange("p (h k) -> p h k", h=HEADS))
                        if mask == "lower":
                            link(ins)
                    ins.then_inc(S["a_mix"], 1)
                    yield

            def solve(s):
                dve.wait_ge(S["ld_g"], 32 * (s + 1))
                W = T + HD
                for k in range(T):
                    link(v.reciprocal(piv[:], sysm[:, :, k, k]))
                    link(v.tensor_tensor(sysm[:, :, k, k + 1:W], sysm[:, :, k, k + 1:W], bc(piv[:], 2, W - k - 1),
                                         ALU.mult))
                    if k == T - 1:
                        break
                    pr = prod[:, :, k + 1:T, k + 1:W]
                    link(v.tensor_tensor(pr, bc(sysm[:, :, k + 1:T, k], 3, W - k - 1),
                                         bc(sysm[:, :, k, k + 1:W], 2, T - k - 1), ALU.mult))
                    link(v.tensor_tensor(sysm[:, :, k + 1:T, k + 1:W], sysm[:, :, k + 1:T, k + 1:W], pr, ALU.subtract))
                    yield
                for k in range(T - 1, 0, -1):
                    pr = prod[:, :, 0:k, T:W]
                    link(v.tensor_tensor(pr, bc(sysm[:, :, 0:k, k], 3, HD), bc(sysm[:, :, k, T:W], 2, k), ALU.mult))
                    ins = v.tensor_tensor(sysm[:, :, 0:k, T:W], sysm[:, :, 0:k, T:W], pr, ALU.subtract)
                    if k > 1:
                        link(ins)
                        yield
                ins.then_inc(S["solved"], 1)

            def experts_done(name, n, s, dst, ready):
                dve.wait_ge(S["acc_add"], NEXP * (n + 1))
                layer_norm(name, s, acc, dst, ready)

            def post1(s):
                a = slice(2 * s, 2 * s + 2)
                pa, pb, pc = after_banks(s)
                dve.wait_ge(S["ld_s"], 32 * (s + 1))
                place(v.tensor_copy, vx1, (2, 3), S["x_placed"])
                dve.wait_ge(S["a1_y"], s + 1)
                y = pc[:, 0:2 * D].rearrange("p (n k) -> p n k", k=HD)
                yc = pre[:, a, :].rearrange("p i (h k) -> p (i h) k", k=HD)
                link(v.tensor_reduce(gsum[:], y, AX.X, ALU.add))
                link(v.tensor_scalar(gsum[:], gsum[:], 1.0 / HD, None, ALU.mult))
                v.tensor_tensor(yc, y, bc(gsum[:], 2, HD), ALU.subtract).then_inc(S["y_in"], 1)
                yield
                dve.wait_ge(S["y_sq"], s + 1)
                link(v.tensor_reduce(gsum[:], gsq[:].rearrange("p i (h k) -> p (i h) k", k=HD), AX.X, ALU.add))
                ask(f"gn_{s}", gsum[:], 1.0 / HD, GN_EPS)
                rs = inv_sqrt(f"gn_{s}", 24)
                link(v.tensor_tensor(yc, yc, bc(rs, 2, HD), ALU.mult))
                link(v.tensor_tensor(pre[:, a, :], pre[:, a, :], bc(r("ln_w"), 1, 2), ALU.mult))
                link(v.tensor_tensor(pre[:, a, :], pre[:, a, :], bc(r("ln_b"), 1, 2), ALU.add))
                dve.wait_ge(S["g_ready"], s + 1)
                v.tensor_tensor(gsq[:], pre[:, a, :], sg[:], ALU.mult).then_inc(S["gn_ready"], 1)
                yield
                dve.wait_ge(S["a1_wo"], s + 1)
                v.tensor_tensor(pre[:, a, :], pc[:, 0:2 * D].rearrange("p (i k) -> p i k", i=2), h2[:, a, :],
                                ALU.add).then_inc(S["wo1_read"], 1)
                dve.wait_ge(S["wo1_read"], s + 1)
                layer_norm(f"h3_{s}", s, pre, h3, "h3_ready")

            v.memset(f1[0][D1:D1 + 1, :, :], 1.0).then_inc(S["ones_set"], 1)
            v.memset(ct1[D1:D1 + 1, :], 1.0).then_inc(S["ones_set"], 1)
            tokens()
            composites()
            attention0(0)
            run(route(0, 0))
            attention0(1)
            run(route(0, 1))
            experts_done("h2_0", 0, 0, h2, "h2_ready")
            dve.wait_ge(S["amix_zero"], 1)
            v.memset(t1[64:65, :], 1.0).then_inc(S["t1_ones"], 1)
            weave("pppppp" + "ssss" + "p" + "ss" + "p" + "ss" + "pp" + "sss" + "p" + "sss" + "p", p=pre1(0), s=solve(0))
            experts_done("h2_1", 1, 1, h2, "h2_ready")
            second, solution = pre1(1), solve(1)
            weave("apapapaaa", a=chain(post1(0), route(1, 0)), p=islice(second, 6))
            weave("ssss" + "p" + "ss" + "p" + "ss" + "pp" + "sss" + "p" + "sss" + "p", p=second, s=solution)
            run(post1(1), route(1, 1))
            experts_done("out_0", 2, 0, pre, "out_ready")
            experts_done("out_1", 3, 1, pre, "out_ready")

        @block.gpsimd
        def _(pool):
            g = nc.gpsimd

            def power(name):
                q, n = order.index(name), width.get(name, 2)
                pool.wait_ge(S["var_ready"], q + 1)
                g.tensor_tensor(rstd[:, q % 2, 0:n], var_in[:, q % 2, 0:n], c("neghalf").broadcast_to([128, n]),
                                ALU.pow).then_inc(S["rstd_ready"], 1)

            def add_experts(l, s, first=0, end=NEXP):
                a = slice(2 * s, 2 * s + 2)
                for e in range(first, end):
                    m = (2 * l + s) * NEXP + e
                    pool.wait_ge(S["y_act"], m + 1)
                    if e == 0:
                        pool.wait_ge(S["acc_init"], 2 * l + s + 1)
                    else:
                        pool.wait_ge(S["acc_add"], m)
                    g.tensor_tensor(acc[:, a, :], acc[:, a, :], ysc[:, m % 2], ALU.add).then_inc(S["acc_add"], 1)

            def mixes(s, first=0, end=MIX):
                for n, m in list(enumerate(MIX_ORDER))[first:end]:
                    pool.wait_ge(S["a1_xd"], MIX * s + n + 1)
                    g.tensor_tensor(xc0[:, m, :], xc0[:, m, :], f0[2][:, s, :], ALU.add)
                    g.tensor_tensor(xc1[:, m, :], xc1[:, m, :], f1[2][0:D1, s, :], ALU.add).then_inc(S["xc_ready"], 1)

            g.memset(amix[:], 0.0).then_inc(S["amix_zero"], 1)
            g.memset(vx1[:], 0.0).then_inc(S["vx_zero"], 1)
            pool.wait_ge(S["ld_const"], 16)
            power("tok1")
            power("tok2")
            power("a0_0")
            power("f0_0")
            add_experts(0, 0, end=3)
            power("a0_1")
            power("f0_1")
            add_experts(0, 0, first=3)
            power("h2_0")
            add_experts(0, 1, end=1)
            mixes(0)
            add_experts(0, 1, first=1)
            power("h2_1")
            power("gn_0")
            mixes(1, end=2)
            power("h3_0")
            mixes(1, first=2)
            add_experts(1, 0, end=4)
            power("gn_1")
            power("h3_1")
            add_experts(1, 0, first=4)
            power("out_0")
            add_experts(1, 1)
            power("out_1")


def _constants():
    p = np.arange(128)
    img = p // T
    same = img[:, None] == img[None, :]
    a, b = p[:, None], p[None, :]
    shift = np.where(same, 0.5 * (np.abs(a - b) == 1) - 1.0 * (a == b), 0.0)
    mid = (b // T) * T + T // 2
    cf = np.where(same, 1.0 * (a <= b) - 1.0 * (a <= mid), 0.0)
    cb = np.where(same, 1.0 * (a < b) - 1.0 * (a < mid), 0.0)
    k = np.arange(32)
    own = (p[:, None] % 32) // T == k[None, :] // T
    key, tok = k[None, :] % T, p[:, None] % T
    head24 = np.concatenate([p[:, None] // HD == np.arange(HEADS)[None, :],
                             8 + p[:, None] // HD == np.arange(HEADS)[None, :]], 1)
    anti = a == T - 1 - b % T
    parts = {
        "ident": np.eye(128), "shift": shift, "cums": -np.concatenate([cf, cb], 1), "headsum": same,
        "head8": p[:, None] // HD == np.arange(8)[None, :], "quad4": p[:, None] // 32 == np.arange(4)[None, :],
        "head12": head24, "off_pair": np.where(own, 0.0, MASKED), "even": (img % 2 == 0)[:, None],
        "odd": (img % 2 == 1)[:, None], "lower": own & (key <= tok), "upper": own & (key > tok),
        "anti16": anti, "iota8": np.tile(np.arange(8), (128, 1)), "one": np.ones((128, 1)),
        "neghalf": np.full((128, 1), -0.5), "eye16": tok == np.arange(T)[None, :]}
    return np.ascontiguousarray(np.concatenate([np.asarray(parts[n], np.float32) for n in CONST], 1))


def _chunks(a, extra=None):
    out = np.zeros((128, 2) + a.shape[1:], np.float32)
    out[:, 0] = a[:128]
    out[:D1, 1] = a[128:]
    if extra is not None:
        out[D1, 1] = extra
    return out


def _pack(table, parts):
    cols = []
    for name in table:
        a = np.asarray(parts[name], np.float32)
        a = a.reshape(a.shape[0], -1)
        cols.append(np.concatenate([a, np.zeros((128 - a.shape[0], a.shape[1]), np.float32)], 0))
    return np.ascontiguousarray(np.concatenate(cols, 1))


def _expert_weights(w1, w2):
    tail = w1[:, 128:].reshape(NEXP, D1, FCH // 2, 2, 128).transpose(0, 3, 1, 2, 4).reshape(NEXP, 128, -1)
    low = w2.reshape(NEXP, FCH, 128, D).transpose(0, 2, 1, 3).reshape(NEXP, 128, -1)
    return np.ascontiguousarray(np.concatenate([w1[:, :128], tail, low], 2))


def kernel(**inputs):
    import concourse.bacc as _bacc
    from concourse.bass_utils import run_bass_kernel_spmd as _run

    x = {k: np.asarray(a) for k, a in inputs.items()}
    a0 = {k[8:]: v for k, v in x.items() if k.startswith("L0_attn_")}
    a1 = {k[8:]: v for k, v in x.items() if k.startswith("L1_attn_")}
    xt = x["x"].reshape(BATCH, 3, 4, 16, 4, 16).transpose(3, 5, 1, 0, 2, 4).reshape(PCH, 128, TOK)
    xt = np.ascontiguousarray(xt.transpose(1, 0, 2).reshape(128, PCH * TOK))
    tokp = _pack(TOKP, {"w": x["L0_tok_W_proj"].T.reshape(PCH, 128, D).transpose(1, 0, 2),
                        "gin": x["L0_tok_g_in"].reshape(PCH, 128).T})
    rows = np.concatenate([x["L0_tok_b_proj"], x["L0_tok_g_out"], x["L0_ffn_ln_gamma"], x["L0_ffn_ln_beta"],
                           a1["ln_w"], a1["ln_b"], a0["gru_const"].reshape(-1), a1["lucid_temp"].reshape(-1),
                           x["L1_ffn_gate_b"], a0["bg"]])
    qkv = [(a0["Wq"], a0["bq"], a0["Aq"], a0["Bq"]), (a0["Wk"], a0["bk"], a0["Ak"], a0["Bk"]),
           (a0["Wv"], a0["bv"], a0["Av"], a0["Bv"])]
    bias64 = np.zeros((128, 3, D), np.float32)
    bias64[D1] = np.stack([b for _, b, _, _ in qkv])
    rel = a0["rel_embed"]
    att0 = _pack(ATT0, {
        "wn": _chunks(np.stack([np.concatenate([w, b[:, None]], 1) for w, b, _, _ in qkv], 1)),
        "wt": _chunks(np.stack([w.T for w, _, _, _ in qkv], 1)),
        "wo": _chunks(a0["Wo"].T, a0["bo"]),
        "wg": _chunks(np.tile(a0["Wg"].T, (HEADS, 1))),
        "b64": bias64,
        "rel": np.stack([np.concatenate([rel[15::-1], rel[41:56]], 0)[k:k + T] for k in range(T)], 1)})
    lora = np.stack([np.stack([b.T, a], 1) for _, _, a, b in qkv], 1).reshape(2, -1)
    maa = np.stack([a1[f"time_maa_{n}"].reshape(-1) for n in "xwkvrg"], 1)
    maa_w2 = np.zeros((128, 2, D), np.float32)
    maa_w2[:, 0] = a1["maa_w2"][:4].reshape(128, D)
    maa_w2[:32, 1] = a1["maa_w2"][4]
    att1 = _pack(ATT1, {
        "maa_w1": _chunks(a1["maa_w1"]), "maa_w2": maa_w2, "maa": _chunks(maa),
        "w4": _chunks(np.stack([a1["Wr"], a1["Wk"], a1["Wv"], a1["Wg"]], 1)),
        "dw1": _chunks(a1["decay_w1"]),
        "dw2": np.concatenate([a1["decay_w2"], a1["time_decay"].reshape(1, D)], 0),
        "wo": _chunks(a1["Wo"]), "router": _chunks(x["L0_ffn_router_w"]), "gate": _chunks(x["L1_ffn_gate_w"]),
        "b1": x["L1_ffn_b1"].reshape(NEXP * FCH, 128).T, "b2": x["L1_ffn_b2"]})
    arrays = {"consts": _constants(), "rows": np.ascontiguousarray(rows), "x_t": xt,
              "tok_pack": tokp, "att0_pack": att0, "lora_pack": np.ascontiguousarray(lora), "att1_pack": att1,
              "w_l0": _expert_weights(x["L0_ffn_w1"], x["L0_ffn_w2"]),
              "w_l1": _expert_weights(x["L1_ffn_w1"], x["L1_ffn_w2"])}

    nc = _bacc.Bacc("TRN2", target_bir_lowering=False, num_devices=1)
    args = [nc.dram_tensor(n, a.shape, F32, kind="ExternalInput").ap() for n, a in arrays.items()]
    scratch = [nc.dram_tensor("p_scratch", (TILES, HEADS, 128, T + HD), F32, kind="Internal").ap(),
               nc.dram_tensor("s_scratch", (TILES, HEADS, 128, HD), F32, kind="Internal").ap()]
    out = nc.dram_tensor("out", (TILES, 128, D), F32, kind="ExternalOutput").ap()
    vit_tower_kernel(nc, *args, *scratch, out)
    got = _run(nc, [arrays], core_ids=[0]).results[0]["out"]
    return np.asarray(got).reshape(BATCH, T, D)
```

```python
from contextlib import ExitStack
from itertools import chain, islice

import numpy as np
import concourse.bass as bass
from concourse import mybir

F32 = mybir.dt.float32
F32R = mybir.dt.float32r
I32 = mybir.dt.int32
U32 = mybir.dt.uint32
ALU = mybir.AluOpType
ACT = mybir.ActivationFunctionType
AX = mybir.AxisListType

BATCH, T, D, HEADS, HD = 32, 16, 192, 12, 16
TOK = BATCH * T
TILES, HALVES = TOK // 128, 2
HT = TOK // HALVES
BLK = HT // 32
PATCH_DIM, PCH = 768, 6
NEXP, DFF, FCH = 8, 768, 6
D1 = D - 128
SYS = 96
W1COLS, W2COLS = 2 * DFF, FCH * D
RING = 2
MIX = 5
MIX_ORDER = (1, 2, 0, 3, 4)
RMS_EPS, LN_EPS, GN_EPS = 1e-5, 1e-5, 64e-5
MASKED = -1e30
ARENA = 6146

def _columns(*spec):
    at, out = 0, {}
    for name, width in spec:
        out[name] = (at, width)
        at += width
    return out, at


CONST, NCONST = _columns(
    ("ident", 128), ("shift", 128), ("cums", 256), ("headsum", 128), ("head8", 8), 
    ("head12", 24), ("off_pair", 32), ("even", 1), ("odd", 1), ("lower", 32), ("upper", 32),
    ("anti16", 128), ("iota8", 8), ("one", 1), ("neghalf", 1), ("eye16", 16))
ROW, NROW = _columns(
    ("b_proj", D), ("g_out", D), ("ln_gamma", D), ("ln_beta", D), ("ln_w", D), ("ln_b", D),
    ("gru", HEADS), ("lucid", HEADS), ("gate_b", NEXP), ("bg", 8))
TOKP, NTOKP = _columns(("w", PCH * D), ("gin", PCH))
ATT0, NATT0 = _columns(("wn", 2 * 3 * (D + 1)), ("wt", 2 * 3 * D), ("wo", 2 * D), ("wg", 16),
                       ("rel", T * HEADS))
ATT1, NATT1 = _columns(("maa_w1", 2 * 160), ("maa_w2", 2 * D), ("maa", 12), ("w4", 2 * 4 * D),
                       ("dw1", 2 * 64), ("dw2", D), ("wo", 2 * D), ("router", 16), ("gate", 16), ("b1", NEXP * FCH),
                       ("b2", D))


def vit_tower_kernel(nc, consts, rows, x_t, tok_pack, att0_pack, lora_pack, bias_pack, att1_pack, w1_l0, w2_l0, w1_l1, w2_l1,
                     p_dram, s_dram, out):
    ctx = ExitStack()
    with ctx:
        def sb(name, shape, dt=F32):
            return ctx.enter_context(nc.sbuf_tensor(name, shape, dt))

        def sem(name):
            return ctx.enter_context(nc.semaphore(name))

        bank = [ctx.enter_context(nc.psum_tensor(f"bank{i}", [128, 512], F32)) for i in range(8)]

        arena = sb("arena", [128, ARENA])
        used = [0, 0]

        def shared(layer, shape):
            n = int(np.prod(shape[1:]))
            at = used[layer]
            used[layer] += n
            assert used[layer] <= ARENA, (layer, used)
            names = " ".join(f"a{i}" for i in range(len(shape) - 1))
            ap = arena[0:shape[0], at:at + n]
            if len(shape) == 2:
                return ap
            return ap.rearrange(f"p ({names}) -> p {names}", **{f"a{i}": k for i, k in enumerate(shape[1:])})

        scratch = sb("scratch", [128, 3, BLK * HEADS * 32])
        xt = scratch[:, 0, :].rearrange("p (c n) -> p c n", c=PCH)
        xsq = scratch[:, 1, :].rearrange("p (c n) -> p c n", c=PCH)
        tokp = scratch[:, 2, 0:NTOKP]
        lora = scratch[0:2, 2, NTOKP:NTOKP + 3 * 2 * D]

        con = sb("con", [128, NCONST])
        row = sb("row", [128, NROW])
        att0 = shared(0, [128, NATT0])
        att1 = sb("att1", [128, NATT1])
        w1 = sb("w1", [128, RING, W1COLS])
        w1_hi = sb("w1_hi", [128, RING, W1COLS], F32R)
        w1_lo = sb("w1_lo", [128, RING, W1COLS], F32R)
        w2 = sb("w2", [128, NEXP, W2COLS])

        def c(name, p=128):
            a, n = CONST[name]
            return con[0:p, a:a + n]

        def r(name):
            a, n = ROW[name]
            return row[:, a:a + n]

        def col(tile_, table, name, p=128):
            a, n = table[name]
            return tile_[0:p, a:a + n]

        wtok = col(tokp, TOKP, "w").rearrange("p (c n) -> p c n", c=PCH)
        gin = col(tokp, TOKP, "gin")
        wn = col(att0, ATT0, "wn").rearrange("p (c j n) -> p c j n", c=2, j=3)
        wt = col(att0, ATT0, "wt").rearrange("p (c j n) -> p c j n", c=2, j=3)
        wo0 = col(att0, ATT0, "wo").rearrange("p (c n) -> p c n", c=2)
        wg = col(att0, ATT0, "wg").rearrange("p (c a b) -> p c a b", c=2, a=2)
        b64 = scratch[:, 2, NTOKP + 6 * D:NTOKP + 9 * D].rearrange("p (j n) -> p j n", j=3)
        rel = col(att0, ATT0, "rel")
        router = [col(att1, ATT1, "router").rearrange("p (c n) -> p c n", c=2),
                  col(att1, ATT1, "gate").rearrange("p (c n) -> p c n", c=2)]
        lora_w = lora[:, :].rearrange("p (j a n) -> p j a n", j=3, a=2)
        maa_w1 = col(att1, ATT1, "maa_w1").rearrange("p (c n) -> p c n", c=2)
        maa_w2 = col(att1, ATT1, "maa_w2").rearrange("p (c n) -> p c n", c=2)
        maa = col(att1, ATT1, "maa").rearrange("p (c n) -> p c n", c=2)
        w4 = col(att1, ATT1, "w4").rearrange("p (c j n) -> p c j n", c=2, j=4)
        dw1 = col(att1, ATT1, "dw1").rearrange("p (c n) -> p c n", c=2)
        dw2 = col(att1, ATT1, "dw2")
        wo1 = col(att1, ATT1, "wo").rearrange("p (c n) -> p c n", c=2)
        b1 = col(att1, ATT1, "b1")
        b2 = col(att1, ATT1, "b2", 8)

        h0 = sb("h0", [128, TILES, D])
        h1 = sb("h1", [128, TILES, D])
        h2 = h1
        h3 = h0
        acc = sb("acc", [128, TILES, D])
        pre = sb("pre", [128, TILES, D])
        xffn = pre
        stats = sb("stats", [128, TILES, 6])
        mv = sb("mv", [128, TILES, 2])
        var_in = sb("var_in", [128, 2, 4])
        rstd = sb("rstd", [128, 2, 4])
        f0 = [sb(f"f0_{n}", [128, HALVES, HT]) for n in ("att", "ffn")] * 2
        f1 = [sb(f"f1_{n}", [128, HALVES, HT]) for n in ("att", "ffn")] * 2
        def expanded(n):
            half = scratch[:, n // 2, (n % 2) * 1536:(n % 2 + 1) * 1536]
            a = half[:, 0:1024].rearrange("p (b h k) -> p b h k", b=4, h=8)
            b = half[0:D1, 1024:1536].rearrange("p (b h k) -> p b h k", b=4, h=4)
            return a, b

        x_hi = sb("x_hi", [128, HALVES, HT], F32R)
        x_lo = sb("x_lo", [128, HALVES, HT], F32R)
        x_tail = sb("x_tail", [128, HALVES, HT], F32R)
        ss = sb("ss", [128, 2, 4])
        cw0 = shared(0, [128, 3, D])
        cw1 = shared(0, [128, 3, D])
        wgsum = sb("wgsum", [128, 2, 2])
        wgx = shared(0, [128, 2, HEADS, 2])
        bgs = sb("bgs", [128, 2])
        posb = shared(0, [128, T, HEADS])
        q0 = shared(0, [128, HT])
        q1 = shared(0, [D1, HT])
        vx1 = sb("vx1", [128, BLK, 3, 4, HD])
        gates0 = shared(0, [128, 2, HEADS, 2])
        gate = shared(0, [128, 2, HEADS])
        gbias = shared(0, [128, 2, HEADS, T])
        prob = shared(0, [128, 2, HEADS, 32])
        smax = sb("smax", [128, 2, HEADS])
        atr = sb("atr", [128, 2, 3, 128])
        vx, ptr = vx1, atr
        ct0 = sb("ct0", [128, HT])
        ct1 = sb("ct1", [128, HT])
        lg = sb("lg", [128, 2, NEXP])
        top = sb("top", [128, 2, 8])
        topi = sb("topi", [128, 2, 8], U32)
        topf = sb("topf", [128, 2, 2])
        topd = sb("topd", [128, 2, 3])
        hot = sb("hot", [128, 2, 2, NEXP])
        gts = sb("gts", [128, TILES, NEXP])
        gts_t = sb("gts_t", [8, 2, 128])
        hid = scratch[:, 2, :].rearrange("p (a j n) -> p a j n", a=2, j=FCH)
        ysc = sb("ysc", [128, 2, 2, D])
        PROD_AT = used[1]
        dx0 = shared(1, [128, HT])
        dx1 = shared(1, [D1, HT])
        xx0 = shared(1, [128, HT])
        xx1 = shared(1, [D1, HT])
        ew = arena[:, used[1] - 2 * HT:used[1] - 2 * HT + 2 * D].rearrange("p (a n) -> p a n", a=2)
        mt0 = shared(1, [128, HT])
        mt1 = shared(1, [32, HT])
        xc0 = shared(1, [128, MIX, HT])
        xc1 = shared(1, [D1, MIX, HT])
        t1 = shared(1, [128, HT])
        sysm_all = sb("sysm", [128, 2, T, T + HD])
        cs0 = scratch[:, 1, 0:2 * HT].rearrange("p (i d k) -> p i d k", i=2, d=2)
        cs1 = scratch[0:D1, 1, 2 * HT:4 * HT].rearrange("p (i d k) -> p i d k", i=2, d=2)
        xc_all = xc0.rearrange("p m n -> p (m n)")
        ex0 = xc_all[:, 0:4 * HT].rearrange("p (a i k) -> p a i k", a=4, i=2)
        ex1 = xc1.rearrange("p m n -> p (m n)")[:, 0:4 * HT].rearrange("p (a i k) -> p a i k", a=4, i=2)
        rt0 = shared(1, [128, HT])
        rt1 = shared(1, [D1, HT])
        kt0 = shared(1, [128, HT])
        kt1 = shared(1, [D1, HT])
        ksq0 = xx0
        ksq1 = xx1
        kn0 = dx0
        kn1 = dx1
        vals = sb("vals", [128, 2, D])
        sg = sb("sg", [128, 2, D])
        amix = sb("amix", [128, 2, HEADS, 32])
        gram = [[acc[:, 2 * s:2 * s + 2].rearrange("p a n -> p (a n)").rearrange("p (h k) -> p h k", h=HEADS),
                 pre[:, 2 * s:2 * s + 2].rearrange("p a n -> p (a n)").rearrange("p (h k) -> p h k", h=HEADS)]
                for s in range(HALVES)]
        pv = shared(1, [128, 2, HEADS, T + HD])
        pmat = pv[:, :, :, 0:T]
        temp = sb("temp", [128, 3, HEADS])
        sysm = sysm_all[0:SYS]
        prod = arena[0:SYS, PROD_AT:PROD_AT + 2 * T * (T + HD)].rearrange("p (i t k) -> p i t k", i=2, t=T)
        piv = sb("piv", [SYS, 2])
        gsum = sb("gsum", [128, 24])
        unused = sb("unused", [128, 24])
        gsq = scratch[:, 1, 0:2 * D].rearrange("p (a n) -> p a n", a=2)

        names = """ld_const ld_row ld_tok ld_att0 ld_att1 st_out
            wtok_scaled xsq_ready xsum_ready tok_y tok_ss y_ready y_sq2 h0_ready wo_read wo1_read g_raw
            lora_mm wn_ready comp_mm posb_mm comp_ready ones_set
            a0_tr a0_ft a0_gate a0_q a0_k a0_v q_ready kx_ready v_out v_placed gate_in gate_exp vx_zero
            a0_s s_shift s_exp p_ready a0_pt pt_ready a0_ctx ct_ready a0_wo
            x_ready ff_tr ff_ft x_hi_ready x_lo_ready w1_hi_ready w1_lo_ready
            ff_lg top_in top_exp gts_ready gt_tr gt_ev b2_mm acc_init
            h_mm h_act y_mm y_act acc_add
            h2_ready a1_tr a1_ft a1_dx a1_xx a1_mt mt_ready a1_mm a1_xd xc_ready
            a1_t1 t1_ready a1_w ew_ready a1_cs cs_ready ex_ready a1_k a1_r rk_ready a1_v a1_g v_ready g_ready
            ksq_ready a1_n2 n2_ready kn_in kn_ready kn1_ready a1_gram gram_in gram_exp p_mat
            dk_in dk_ready dk1_ready a1_ab gn_var gn_std
            a_mix a1_at at_ready st_p ld_g st_s ld_s solved x_placed
            a1_y y_in y_sq gn_ready a1_ytr yt_ready a1_wo h3_ready out_ready
            var_ready rstd_ready temp_in temp_out t1_ones amix_zero dve_chain act_chain""".split()
        S = {n: sem(n) for n in names}
        ld_x = [sem(f"ld_x{ch}") for ch in range(PCH)]
        ld_w1 = [sem(f"ld_w1_{slot}") for slot in range(RING)]
        ld_w2 = [[sem(f"ld_w2_{l}_{e}") for e in range(NEXP)] for l in range(2)]
        uses = [(l, s, e) for l in range(2) for s in range(HALVES) for e in range(NEXP)]
        order = ["tok1", "tok2", "a0_0", "f0_0", "a0_1", "f0_1", "h2_0", "h2_1", "h3_0",
                 "h3_1", "out_0", "out_1"]
        width = {"tok1": 4, "tok2": 4}

        HB = 3
        br = bank[3]
        bx, by, bz = bank[5], bank[6], bank[7]

        def place(copy, dst, quadrants, done):
            src = vals[:].rearrange("p i (g j k) -> p i g j k", g=3, j=4)
            for j in quadrants:
                for b in range(4):
                    copy(dst[32 * j:32 * j + 32, b::4, :, j, :], src[32 * b:32 * b + 32, :, :, j, :]).then_inc(done, 1)

        def after_banks(s):
            return (bx, by, bz) if s else (bank[0], bank[1], bank[2])

        def expand_on(engine, slot, a, d):
            xa, xb = expanded(slot)
            engine.tensor_tensor(xa, bc(a, 2, 8), bc(bc(c("head8"), 1, 4), 3, 32), ALU.mult)
            return engine.tensor_tensor(xb, bc(d, 2, 4), bc(bc(c("head8", D1)[:, 0:4], 1, 4), 3, 32), ALU.mult)

        def blocks(tile_, i):
            return tile_[:, 128 * i:128 * i + 128].rearrange("p (b k) -> p b k", b=4)

        def run(*steps):
            for _ in chain(*steps):
                pass

        def weave(order, **steps):
            for name in order:
                next(steps[name], None)
            for rest in steps.values():
                for _ in rest:
                    pass

        block = ctx.enter_context(nc.Block())

        def rounds_before(order, step):
            at = [i for i, name in enumerate(order) if name == "p"][step - 1]
            return (order[:at].count("x") + 2) // 5

        order_00 = "aapxxpxxxxxpxpxxxxpxpxxxpxpxxxxxpxxpxp"
        order_01 = "xpxpxpxppxxxpxxppxxxxxppxxxxxxxxpxxxxppxxxpx"
        late_head = "apaapap"
        order_10 = "aapaxxxxpxxxpxppxxpxxpxxxxxxxpxxxpxpxxpxxxxxxpxxpxxpxxxpx"
        order_11 = "xaxxaxxax"
        vector_0 = "pppppppppssssspssssssp"
        vector_1 = "aapapaaapappppppsssssssspsssp"

        def bc(ap, axis, n):
            a = ap.unsqueeze(axis)
            shape = list(a.shape)
            shape[axis] = n
            return a.broadcast_to(shape)

        @block.sync
        def _(sp):
            sp.dma_start(tokp[:], tok_pack).then_inc(S["ld_tok"], 16)
            for ch in range(PCH):
                sp.dma_start(xt[:, ch, :], x_t[:, ch * TOK:(ch + 1) * TOK]).then_inc(ld_x[ch], 16)
            sp.dma_start(lora[:], lora_pack).then_inc(S["ld_att0"], 16)
            sp.dma_start(b64[D1:D1 + 1], bias_pack).then_inc(S["ld_att0"], 16)
            sp.dma_start(att0[:], att0_pack).then_inc(S["ld_att0"], 16)
            for m in range(RING):
                sp.dma_start(w1[:, m, :], w1_l0[m]).then_inc(ld_w1[m], 16)
            sp.dma_start(att1[:], att1_pack).then_inc(S["ld_att1"], 16)
            for e in range(NEXP):
                sp.dma_start(w2[:, e, :], w2_l0[e]).then_inc(ld_w2[0][e], 16)
            for s in range(HALVES):
                for i in range(2):
                    sp.wait_ge(S["v_ready"], s + 1)
                    sp.wait_ge(S["p_mat"], 2 * s + i + 1)
                    sp.dma_start(p_dram[2 * s + i].rearrange("h p k -> p h k"), pv[:, i]).then_inc(S["st_p"], 16)
                sp.wait_ge(S["st_p"], 32 * (s + 1))
                for i in range(2):
                    src = p_dram[2 * s + i].rearrange("h (b t) k -> (h b) t k", t=T)
                    sp.dma_start(sysm[:, i], src).then_inc(S["ld_g"], 16)
                sp.wait_ge(S["solved"], s + 1)
                for i in range(2):
                    dst = s_dram[2 * s + i].rearrange("h (b t) k -> (h b) t k", t=T)
                    sp.dma_start(dst, sysm[:, i, :, T:]).then_inc(S["st_s"], 16)
                sp.wait_ge(S["st_s"], 32 * (s + 1))
                for i in range(2):
                    sp.dma_start(vals[:, i].rearrange("p (h k) -> p h k", h=HEADS),
                                 s_dram[2 * s + i].rearrange("h p k -> p h k")).then_inc(S["ld_s"], 16)
            for s in range(HALVES):
                sp.wait_ge(S["out_ready"], s + 1)
                for i in range(2):
                    t = 2 * s + i
                    sp.dma_start(out[t], pre[:, t, :]).then_inc(S["st_out"], 16)
            sp.wait_ge(S["st_out"], 16 * TILES)

        @block.tensor
        def _(pe):
            mm = nc.tensor.matmul

            def tokens():
                pe.wait_ge(S["ld_const"], 16)
                pe.wait_ge(S["wtok_scaled"], 1)
                for ch in range(PCH):
                    pe.wait_ge(ld_x[ch], 16)
                    for t in range(TILES):
                        last = mm(bank[t][:, 0:D], xt[:, ch, t * 128:(t + 1) * 128], wtok[:, ch, :],
                                  start=ch == 0, stop=ch == PCH - 1)
                last.then_inc(S["tok_y"], 1)
                pe.wait_ge(S["xsum_ready"], PCH - 1)
                for t in range(TILES):
                    last = mm(bank[4][:, t:t + 1], xsq[:, 0, t * 128:(t + 1) * 128], c("one"), start=True, stop=True)
                last.then_inc(S["tok_ss"], 1)

            def composites():
                pe.wait_ge(S["ld_att0"], 48)
                for j in range(3):
                    mm(bank[5 + j][:, 0:D], lora_w[:, j, 0, 0:128], lora_w[:, j, 1, :], start=True, stop=True)
                    last = mm(bank[5 + j][0:D1, D:2 * D], lora_w[:, j, 0, 128:D], lora_w[:, j, 1, :],
                              start=True, stop=True)
                last.then_inc(S["lora_mm"], 1)
                pe.wait_ge(S["wn_ready"], 1)
                for j in range(3):
                    for e0, e1, o in ((0, 128, 0), (128, D + 1, D)):
                        mm(bank[5 + j][0:e1 - e0, o:o + D], wn[:, 0, j, e0:e1], wt[:, 0, j, :],
                           start=True, stop=False)
                        last = mm(bank[5 + j][0:e1 - e0, o:o + D], wn[0:D1, 1, j, e0:e1], wt[0:D1, 1, j, :],
                                  start=False, stop=True)
                    last.then_inc(S["comp_mm"], 1)
                pe.wait_ge(S["y_ready"], TILES)
                mm(bank[0][:, 0:T * HEADS], c("anti16", T), rel[0:T, :], start=True, stop=True).then_inc(S["posb_mm"], 1)

            def transpose_half(src, s, dst):
                for i in range(2):
                    t = 2 * s + i
                    nc.tensor.transpose(dst[:, i * 128:(i + 1) * 128], src[:, t, 0:128], c("ident"))
                    tail = src[:, t, 128:D]
                    last = nc.tensor.transpose(dst[0:D1, HT + i * 128:HT + (i + 1) * 128], tail, c("ident"))
                return last


            def attention0(s):
                pe.wait_ge(S["h0_ready"], s + 1)
                pe.wait_ge(S["comp_ready"], 1)
                if s:
                    pe.wait_ge(S["wo_read"], s)
                transpose_half(h0, s, bx).then_inc(S["a0_tr"], 1)
                yield
                pe.wait_ge(S["a0_ft"], 2 * (s + 1))
                pe.wait_ge(S["ones_set"], 2)
                fa, fb = f0[0][:, s, :], f1[0][0:D1 + 1, s, :]
                if s:
                    pe.wait_ge(S["acc_init"], s)
                for i in range(2):
                    t = slice(i * 128, (i + 1) * 128)
                    o = br[:, i * 24:(i + 1) * 24]
                    mm(o, fa[:, t], wgx[:, 0, :, :].rearrange("p h a -> p (h a)"), start=True, stop=False)
                    last = mm(o, fb[0:D1, t], wgx[0:D1, 1, :, :].rearrange("p h a -> p (h a)"), start=False, stop=True)
                last.then_inc(S["a0_gate"], 1)
                for j, bk in ((1, bz), (0, by)):
                    for lo, hi, o in ((0, 128, 0), (128, D, HT)):
                        mm(bk[0:hi - lo, o:o + HT], cw0[:, j, lo:hi], fa, start=True, stop=False)
                        last = mm(bk[0:hi - lo, o:o + HT], cw1[0:D1 + 1, j, lo:hi], fb, start=False, stop=True)
                    last.then_inc(S["a0_q" if j == 0 else "a0_k"], 1)
                for i in range(2):
                    t = slice(i * 128, (i + 1) * 128)
                    mm(bx[:, i * D:(i + 1) * D], fa[:, t], cw0[:, 2, :], start=True, stop=False)
                    last = mm(bx[:, i * D:(i + 1) * D], fb[:, t], cw1[0:D1 + 1, 2, :], start=False, stop=True)
                last.then_inc(S["a0_v"], 1)
                yield
                pe.wait_ge(S["q_ready"], 2 * (s + 1))
                for i, bk in enumerate((by, bz)):
                    pe.wait_ge(S["kx_ready"], 2 * s + 2)
                    kxa, kxb = expanded(i)
                    for b in range(4):
                        o, n = bk[32 * b:32 * b + 32, :], 4 * i + b
                        mm(o[:, 0:256], q0[:, 32 * n:32 * n + 32], kxa[:, b].rearrange("p h k -> p (h k)"),
                           start=True, stop=True)
                        last = mm(o[:, 256:384], q1[:, 32 * n:32 * n + 32], kxb[:, b].rearrange("p h k -> p (h k)"),
                                  start=True, stop=True)
                    last.then_inc(S["a0_s"], 1)
                yield
                yield
                pe.wait_ge(S["v_out"], s + 1)
                for i, bk in enumerate((bx, by)):
                    pe.wait_ge(S["p_ready"], 2 * s + i + 1)
                    p = prob[:, i].rearrange("p h k -> p (h k)")
                    for g in range(3):
                        last = nc.tensor.transpose(bk[:, g * 128:(g + 1) * 128], p[:, g * 128:(g + 1) * 128], c("ident"))
                    last.then_inc(S["a0_pt"], 1)
                    yield
                pe.wait_ge(S["v_placed"], 16 * (s + 1))
                for i in range(2):
                    pe.wait_ge(S["pt_ready"], 2 * s + i + 1)
                    for b in range(4):
                        n = 4 * i + b
                        for g in range(3):
                            o = bz[64 * (g % 2):64 * (g % 2) + 64, HT * (g // 2) + 32 * n:HT * (g // 2) + 32 * n + 32]
                            last = mm(o, vx[:, n, g].rearrange("p h k -> p (h k)"), ptr[:, i, g, 32 * b:32 * b + 32],
                                      start=True, stop=True)
                last.then_inc(S["a0_ctx"], 1)
                yield
                pe.wait_ge(S["ct_ready"], 2 * (s + 1))
                for i in range(2):
                    o = bx[:, i * D:(i + 1) * D]
                    mm(o, ct0[:, i * 128:(i + 1) * 128], wo0[:, 0, :], start=True, stop=False)
                    last = mm(o, ct1[0:D1 + 1, i * 128:(i + 1) * 128], wo0[0:D1 + 1, 1, :], start=False, stop=True)
                last.then_inc(S["a0_wo"], 1)
                yield

            def route(l, s):
                n = 2 * l + s
                if l == 0:
                    pe.wait_ge(S["x_ready"], s + 1)
                else:
                    pe.wait_ge(S["h3_ready"], s + 1)
                if n:
                    pe.wait_ge(S["acc_init"], n)
                if n == 0:
                    pe.wait_ge(S["ld_att1"], 16)
                transpose_half(xffn if l == 0 else h3, s, br).then_inc(S["ff_tr"], 1)
                yield
                pe.wait_ge(S["x_hi_ready"], n + 1)
                for i in range(2):
                    o = br[:, i * NEXP:(i + 1) * NEXP]
                    mm(o, f0[1 + 2 * l][:, s, i * 128:(i + 1) * 128], router[l][:, 0, :], start=True, stop=False)
                    last = mm(o, f1[1 + 2 * l][0:D1, s, i * 128:(i + 1) * 128], router[l][0:D1, 1, :],
                              start=False, stop=True)
                last.then_inc(S["ff_lg"], 1)
                yield
                yield
                if l:
                    pe.wait_ge(S["gts_ready"], n + 1)
                    for i in range(2):
                        last = nc.tensor.transpose(br[0:NEXP, i * 128:(i + 1) * 128], gts[:, 2 * s + i, :], c("ident"))
                    last.then_inc(S["gt_tr"], 1)
                    pe.wait_ge(S["gt_ev"], s + 1)
                    for i in range(2):
                        last = mm(br[:, i * D:(i + 1) * D], gts_t[:, i, :], b2, start=True, stop=True)
                    last.then_inc(S["b2_mm"], 1)
                    yield

            def up(l, s, e, jp):
                m = (2 * l + s) * NEXP + e
                n = m * 3 + jp
                pe.wait_ge(S["w1_lo_ready"], m + 1)
                if n >= HB:
                    pe.wait_ge(S["h_act"], n - HB + 1)
                hi, lo = w1_hi[:, m % RING, :], w1_lo[:, m % RING, :]
                for a in range(2):
                    o = bank[n % HB][:, a * HT:(a + 1) * HT]
                    j = (2 * jp + a) * 128
                    mm(o, hi[:, j:j + 128], x_hi[:, s, :], start=True, stop=False)
                    mm(o, lo[:, j:j + 128], x_hi[:, s, :], start=False, stop=False)
                    mm(o, hi[:, j:j + 128], x_lo[:, s, :], start=False, stop=False)
                    j += DFF
                    mm(o, hi[:, j:j + 128], x_tail[:, s, :], start=False, stop=False)
                    last = mm(o, lo[0:D1, j:j + 128], x_tail[0:D1, s, :], start=False, stop=True)
                last.then_inc(S["h_mm"], 1)

            def down(l, s, e, i):
                n = (2 * l + s) * NEXP + e
                pe.wait_ge(ld_w2[l][e], 16)
                pe.wait_ge(S["h_act"], 3 * (n + 1))
                if n >= 1:
                    pe.wait_ge(S["y_act"], n)
                w = w2[:, e, :].rearrange("p (j n) -> p j n", j=FCH)
                for j in range(FCH):
                    last = mm(bank[4][:, i * D:(i + 1) * D], hid[:, n % 2, j, i * 128:(i + 1) * 128],
                              w[:, j, :], start=j == 0, stop=j == FCH - 1)
                if i:
                    last.then_inc(S["y_mm"], 1)

            def experts(l, s):
                pe.wait_ge(S["x_lo_ready"], 2 * l + s + 1)
                for e in range(NEXP + 1):
                    if e < NEXP:
                        for jp in range(3):
                            up(l, s, e, jp)
                            yield
                    if e:
                        for i in range(2):
                            down(l, s, e - 1, i)
                            yield

            def pre1(s):
                pe.wait_ge(S["h2_ready"], s + 1)
                transpose_half(h2, s, bx).then_inc(S["a1_tr"], 1)
                for i in range(2):
                    t = 2 * s + i
                    mm(by[:, i * 128:(i + 1) * 128], h2[:, t, 0:128], c("shift"), start=True, stop=True)
                    last = mm(by[0:D1, HT + i * 128:HT + (i + 1) * 128], h2[:, t, 128:D], c("shift"),
                              start=True, stop=True)
                last.then_inc(S["a1_dx"], 1)
                yield
                pe.wait_ge(S["a1_xx"], s + 1)
                for lo, hi, o in ((0, 128, 0), (128, 160, HT)):
                    mm(bz[0:hi - lo, o:o + HT], maa_w1[:, 0, lo:hi], xx0, start=True, stop=False)
                    last = mm(bz[0:hi - lo, o:o + HT], maa_w1[0:D1, 1, lo:hi], xx1, start=False, stop=True)
                last.then_inc(S["a1_mt"], 1)
                yield
                pe.wait_ge(S["mt_ready"], 2 * (s + 1))
                for n, m in enumerate(MIX_ORDER):
                    if n >= 3:
                        pe.wait_ge(S["a1_xd"], MIX * s + n - 2)
                    p = 32 * (m % 4)
                    w = maa_w2[p:p + 32, m // 4, :]
                    x = mt0[p:p + 32, :] if m < 4 else mt1
                    bk = (bx, by, bz)[n % 3]
                    mm(bk[:, 0:HT], w[:, 0:128], x, start=True, stop=True)
                    mm(bk[0:D1, HT:], w[:, 128:D], x, start=True, stop=True).then_inc(S["a1_mm"], 1)
                    if n in (1, 4):
                        yield

                def mixed_t(bk, m, w):
                    for lo, hi, o in ((0, 128, 0), (128, D, HT)):
                        mm(bk[0:hi - lo, o:o + HT], w4[:, 0, w, lo:hi], xc0[:, m, :], start=True, stop=False)
                        last = mm(bk[0:hi - lo, o:o + HT], w4[0:D1, 1, w, lo:hi], xc1[:, m, :], start=False, stop=True)
                    return last

                def mixed(bk, m, w):
                    for i in range(2):
                        o = bk[:, i * D:(i + 1) * D]
                        mm(o, xc0[:, m, i * 128:(i + 1) * 128], w4[:, 0, w, :], start=True, stop=False)
                        last = mm(o, xc1[:, m, i * 128:(i + 1) * 128], w4[0:D1, 1, w, :], start=False, stop=True)
                    return last

                pe.wait_ge(S["xc_ready"], MIX * s + 1)
                pe.wait_ge(S["a1_xd"], MIX * s + 3)
                mixed_t(bz, 1, 1).then_inc(S["a1_k"], 1)
                yield
                pe.wait_ge(S["xc_ready"], MIX * s + 2)
                pe.wait_ge(S["a1_xd"], MIX * s + 5)
                mixed(by, 2, 2).then_inc(S["a1_v"], 1)
                pe.wait_ge(S["ksq_ready"], s + 1)
                mm(bx[:, 0:HT], c("headsum"), ksq0, start=True, stop=True)
                mm(bx[0:D1, HT:], c("headsum", D1)[:, 0:D1], ksq1, start=True, stop=True).then_inc(S["a1_n2"], 1)
                yield
                pe.wait_ge(S["xc_ready"], MIX * s + 3)
                pe.wait_ge(S["v_ready"], s + 1)
                mm(by[0:64, 0:HT], dw1[:, 0, :], xc0[:, 0, :], start=True, stop=False)
                mm(by[0:64, 0:HT], dw1[0:D1, 1, :], xc1[:, 0, :], start=False, stop=True).then_inc(S["a1_t1"], 1)
                yield
                pe.wait_ge(S["xc_ready"], MIX * s + 5)
                mixed_t(bz, 3, 0).then_inc(S["a1_r"], 1)
                pe.wait_ge(S["n2_ready"], s + 1)
                mixed(bx, 4, 3).then_inc(S["a1_g"], 1)
                pe.wait_ge(S["t1_ready"], s + 1)
                pe.wait_ge(S["t1_ones"], 1)
                for i in range(2):
                    last = mm(by[:, i * D:(i + 1) * D], t1[0:65, i * 128:(i + 1) * 128], dw2[0:65, :],
                              start=True, stop=True)
                last.then_inc(S["a1_w"], 1)
                yield
                pe.wait_ge(S["rk_ready"], s + 1)
                pe.wait_ge(S["g_raw"], s + 1)
                for i, bk in enumerate((bz, bx)):
                    pe.wait_ge(S["kn1_ready" if i else "kn_ready"], s + 1)
                    pair_product(bk, kn0[:, 128 * i:128 * i + 128], kn1[:, 128 * i:128 * i + 128], i)\
                        .then_inc(S["a1_gram"], 1)
                yield
                pe.wait_ge(S["ew_ready"], s + 1)
                pe.wait_ge(S["gram_in"], 2 * s + 1)
                for i in range(2):
                    mm(by[:, i * 256:(i + 1) * 256], ew[:, i, 0:128], c("cums"), start=True, stop=True)
                    last = mm(bz[0:D1, i * 256:(i + 1) * 256], ew[:, i, 128:D], c("cums"), start=True, stop=True)
                last.then_inc(S["a1_cs"], 1)
                yield
                pe.wait_ge(S["gram_in"], 2 * s + 2)
                pe.wait_ge(S["cs_ready"], s + 1)
                for i, banks in enumerate(((bx, by), (bz, bx))):
                    pe.wait_ge(S["dk1_ready" if i else "dk_ready"], s + 1)
                    for m in range(2):
                        if i == 1 and m == 1:
                            pe.wait_ge(S["a_mix"], 2 * s + 1)
                        last = pair_product(banks[m], ex0[:, m, i, :], ex1[:, m, i, :], (2 + 2 * i + m) % 4)
                    last.then_inc(S["a1_ab"], 1)
                    yield
                for i, bk in enumerate((by, bx)):
                    pe.wait_ge(S["a_mix"], 2 * s + i + 1)
                    a = amix[:, i].rearrange("p h k -> p (h k)")
                    for g in range(3):
                        last = nc.tensor.transpose(bk[:, g * 128:(g + 1) * 128], a[:, g * 128:(g + 1) * 128], c("ident"))
                    last.then_inc(S["a1_at"], 1)
                    yield

            def pair_product(bk, left0, left1, slot):
                xa, xb = expanded(slot)
                for b in range(4):
                    o = bk[32 * b:32 * b + 32, :]
                    mm(o[:, 0:256], left0[:, 32 * b:32 * b + 32], xa[:, b].rearrange("p h k -> p (h k)"),
                       start=True, stop=True)
                    last = mm(o[:, 256:384], left1[:, 32 * b:32 * b + 32], xb[:, b].rearrange("p h k -> p (h k)"),
                              start=True, stop=True)
                return last

            def post1(s):
                pa, pb, pc = after_banks(s)
                pe.wait_ge(S["at_ready"], 2 * (s + 1))
                pe.wait_ge(S["x_placed"], 16 * (s + 1))
                for i in range(2):
                    for b in range(4):
                        n = 4 * i + b
                        for g in range(3):
                            last = mm(pc[32 * b:32 * b + 32, i * D + g * 64:i * D + (g + 1) * 64],
                                      atr[:, i, g, 32 * b:32 * b + 32], vx1[:, n, g].rearrange("p h k -> p (h k)"),
                                      start=True, stop=True)
                last.then_inc(S["a1_y"], 1)
                yield
                pe.wait_ge(S["gn_ready"], s + 1)
                transpose_half(gsq, 0, pa).then_inc(S["a1_ytr"], 1)
                yield
                pe.wait_ge(S["yt_ready"], 2 * (s + 1))
                for i in range(2):
                    o = pc[:, i * D:(i + 1) * D]
                    mm(o, ct0[:, i * 128:(i + 1) * 128], wo1[:, 0, :], start=True, stop=False)
                    last = mm(o, ct1[0:D1, i * 128:(i + 1) * 128], wo1[0:D1, 1, :], start=False, stop=True)
                last.then_inc(S["a1_wo"], 1)
                yield

            tokens()
            composites()
            first = route(0, 0)
            run(attention0(0), islice(first, 1))
            weave(order_00, a=first, x=experts(0, 0), p=chain(attention0(1), route(0, 1)))
            weave(order_01, x=experts(0, 1), p=pre1(0))
            second = pre1(1)
            first = route(1, 0)
            weave(late_head, a=chain(post1(0), islice(first, 1)), p=islice(second, 3))
            last = route(1, 1)
            weave(order_10, a=first, x=experts(1, 0), p=chain(second, post1(1), islice(last, 1)))
            weave(order_11, a=last, x=experts(1, 1))

        @block.scalar
        def _(act):
            count = [0]

            def link(ins):
                count[0] += 1
                ins.then_inc(S["act_chain"], 1)
                act.wait_ge(S["act_chain"], count[0])

            f = nc.scalar.activation

            def loads():
                act.dma_start(con[:], consts).then_inc(S["ld_const"], 16)
                act.dma_start(row[:], rows.partition_broadcast(128)).then_inc(S["ld_row"], 16)

            def tokens():
                for ch in range(PCH):
                    act.wait_ge(ld_x[ch], 16)
                    f(xsq[:, ch, :], xt[:, ch, :], ACT.Square).then_inc(S["xsq_ready"], 1)
                for t in range(TILES):
                    act.wait_ge(S["y_ready"], t + 1)
                    f(pre[:, t, :], h0[:, t, :], ACT.Square, accum_out=ss[:, 1, t:t + 1]).then_inc(S["y_sq2"], 1)

            loaded = [0]

            def preload(func):
                f(unused[:, loaded[0]:loaded[0] + 1], c("one"), func)
                loaded[0] += 1

            def copy_ft(n, s, src, ready, got, inc, full=False):
                act.wait_ge(S[ready], got)
                f(f0[n][:, s, :], src[:, 0:HT], ACT.Copy).then_inc(S[inc], 1)
                f(f1[n][0:D1, s, :], src[0:D1, HT:2 * HT], ACT.Copy).then_inc(S[inc], 1)
                if full:
                    f(f1[n][D1:128, s, :], src[0:D1, HT:2 * HT], ACT.Copy).then_inc(S[inc], 1)

            def attention0(s):
                copy_ft(0, s, bx, "a0_tr", s + 1, "a0_ft")
                yield
                preload(ACT.Exp)
                act.wait_ge(S["gate_in"], s + 1)
                g = gates0[:].rearrange("p i h a -> p (i h a)")
                f(g, g, ACT.Exp, scale=-1.0).then_inc(S["gate_exp"], 1)
                act.wait_ge(S["a0_q"], s + 1)
                f(q0, by[:, 0:HT], ACT.Copy).then_inc(S["q_ready"], 1)
                f(q1, by[0:D1, HT:], ACT.Copy).then_inc(S["q_ready"], 1)
                act.wait_ge(S["a0_v"], s + 1)
                f(vals[:].rearrange("p i k -> p (i k)"), bx[:, 0:2 * D], ACT.Copy).then_inc(S["v_out"], 1)
                yield
                act.wait_ge(S["v_out"], s + 1)
                act.wait_ge(S["vx_zero"], 1)
                place(lambda o, x: f(o, x, ACT.Copy), vx, (0, 1), S["v_placed"])
                yield
                for i in range(2):
                    act.wait_ge(S["s_shift"], 2 * s + i + 1)
                    p = prob[:, i].rearrange("p h k -> p (h k)")
                    f(p, p, ACT.Exp).then_inc(S["s_exp"], 1)
                yield
                for i, bk in enumerate((bx, by)):
                    act.wait_ge(S["a0_pt"], 2 * s + i + 1)
                    f(ptr[:, i].rearrange("p g k -> p (g k)"), bk[:, 0:384], ACT.Copy).then_inc(S["pt_ready"], 1)
                    yield
                act.wait_ge(S["a0_ctx"], s + 1)
                f(ct0[:], bz[:, 0:HT], ACT.Copy).then_inc(S["ct_ready"], 1)
                f(ct1[0:D1, :], bz[0:D1, HT:], ACT.Copy).then_inc(S["ct_ready"], 1)
                yield
                yield

            def route(l, s):
                n = 2 * l + s
                copy_ft(1 + 2 * l, s, br, "ff_tr", n + 1, "ff_ft", full=True)
                f(x_hi[:, s, :], br[:, 0:HT], ACT.Copy)
                f(x_tail[0:D1, s, :], br[0:D1, HT:], ACT.Copy)
                f(x_tail[D1:128, s, :], br[0:D1, HT:], ACT.Copy).then_inc(S["x_hi_ready"], 1)
                yield
                yield
                preload(ACT.Exp)
                act.wait_ge(S["top_in"], n + 1)
                f(topd[:, :, 1:2], topd[:, :, 0:1], ACT.Exp).then_inc(S["top_exp"], 1)
                yield
                if l:
                    act.wait_ge(S["gt_tr"], s + 1)
                    f(gts_t[:].rearrange("p i k -> p (i k)"), br[0:NEXP, 0:256], ACT.Copy).then_inc(S["gt_ev"], 1)
                    yield

            def up(l, s, e, jp):
                m = (2 * l + s) * NEXP + e
                n = m * 3 + jp
                if m >= 2:
                    act.wait_ge(S["y_mm"], m - 1)
                act.wait_ge(S["h_mm"], n + 1)
                src = bank[n % HB]
                if l == 0:
                    f(hid[:, m % 2, 2 * jp:2 * jp + 2, :].rearrange("p j n -> p (j n)"), src[:], ACT.Silu)\
                        .then_inc(S["h_act"], 1)
                else:
                    for a in range(2):
                        j = 2 * jp + a
                        ins = f(hid[:, m % 2, j, :], src[:, a * HT:(a + 1) * HT], ACT.Gelu,
                                bias=b1[:, e * FCH + j:e * FCH + j + 1])
                    ins.then_inc(S["h_act"], 1)

            def fetch_w1(m):
                if m < len(uses):
                    l, _, e = uses[m]
                    act.wait_ge(S["w1_lo_ready"], m - RING + 1)
                    act.dma_start(w1[:, m % RING, :], (w1_l0, w1_l1)[l][e]).then_inc(ld_w1[m % RING], 16)

            def split_w1(m):
                if m < len(uses):
                    act.wait_ge(ld_w1[m % RING], 16 * (m // RING + 1))
                    if m >= RING:
                        act.wait_ge(S["h_mm"], 3 * (m - RING + 1))
                    f(w1_hi[:, m % RING, :], w1[:, m % RING, :], ACT.Copy).then_inc(S["w1_hi_ready"], 1)

            def down(l, s, e):
                m = (2 * l + s) * NEXP + e
                if e == 0:
                    act.wait_ge(S["gts_ready"], 2 * l + s + 1)
                act.wait_ge(S["y_mm"], m + 1)
                if m >= 2:
                    act.wait_ge(S["acc_add"], m - 1)
                for i in range(2):
                    ins = f(ysc[:, m % 2, i, :], bank[4][:, i * D:(i + 1) * D], ACT.Copy,
                            scale=gts[:, 2 * s + i, e:e + 1])
                ins.then_inc(S["y_act"], 1)
                if l == 0 and s == 1:
                    act.dma_start(w2[:, e, :], w2_l1[e]).then_inc(ld_w2[1][e], 16)

            def experts(l, s):
                for e in range(NEXP + 1):
                    if e < NEXP:
                        m = (2 * l + s) * NEXP + e
                        for jp in range(3):
                            up(l, s, e, jp)
                            if jp == 2:
                                split_w1(m + RING)
                                fetch_w1(m + RING + 1)
                            yield
                    if e:
                        yield
                        down(l, s, e - 1)
                        yield

            def temperature():
                act.wait_ge(S["temp_in"], 1)
                link(f(temp[:, 1, :], temp[:, 0, :], ACT.Exp, scale=-1.0))
                f(temp[:, 2, :], temp[:, 1, :], ACT.Ln, bias=c("one")).then_inc(S["temp_out"], 1)

            def pre1(s):
                copy_ft(2, s, bx, "a1_tr", s + 1, "a1_ft")
                act.wait_ge(S["a1_dx"], s + 1)
                f(dx0[:], by[:, 0:HT], ACT.Copy).then_inc(S["a1_ft"], 1)
                f(dx1[:], by[0:D1, HT:], ACT.Copy).then_inc(S["a1_ft"], 1)
                yield
                preload(ACT.Tanh)
                act.wait_ge(S["a1_mt"], s + 1)
                f(mt0, bz[:, 0:HT], ACT.Tanh).then_inc(S["mt_ready"], 1)
                f(mt1, bz[0:32, HT:], ACT.Tanh).then_inc(S["mt_ready"], 1)
                yield
                yield
                yield
                act.wait_ge(S["a1_k"], s + 1)
                link(f(kt0, bz[:, 0:HT], ACT.Copy))
                link(f(kt1, bz[0:D1, HT:], ACT.Copy))
                f(ksq0, kt0, ACT.Square)
                f(ksq1, kt1, ACT.Square).then_inc(S["ksq_ready"], 1)
                yield
                preload(ACT.Sqrt)
                act.wait_ge(S["a1_v"], s + 1)
                f(pv[:, :, :, T:], by[:, 0:2 * D].rearrange("p (i h k) -> p i h k", i=2, h=HEADS), ACT.Copy)\
                    .then_inc(S["v_ready"], 1)
                act.wait_ge(S["a1_n2"], s + 1)
                f(kn0, bx[:, 0:HT], ACT.Sqrt)
                f(kn1, bx[0:D1, HT:], ACT.Sqrt).then_inc(S["n2_ready"], 1)
                yield
                preload(ACT.Tanh)
                act.wait_ge(S["a1_t1"], s + 1)
                f(t1[0:64, :], by[0:64, 0:HT], ACT.Tanh).then_inc(S["t1_ready"], 1)
                yield
                preload(ACT.Exp)
                act.wait_ge(S["a1_w"], s + 1)
                f(ew.rearrange("p i k -> p (i k)"), by[:, 0:2 * D], ACT.Exp).then_inc(S["ew_ready"], 1)
                f(rt0, bz[:, 0:HT], ACT.Copy)
                f(rt1, bz[0:D1, HT:], ACT.Copy).then_inc(S["rk_ready"], 1)
                yield
                preload(ACT.Exp)
                for i in range(2):
                    act.wait_ge(S["gram_in"], 2 * s + i + 1)
                    f(gram[s][i], gram[s][i], ACT.Exp).then_inc(S["gram_exp"], 1)
                yield
                preload(ACT.Exp)
                act.wait_ge(S["cs_ready"], s + 1)
                for kind, (d, sc) in enumerate(((0, 1.0), (1, -1.0), (0, -1.0), (1, 1.0))):
                    f(ex0[:, kind], cs0[:, :, d, :], ACT.Exp, scale=sc)
                    ins = f(ex1[:, kind], cs1[:, :, d, :], ACT.Exp, scale=sc)
                ins.then_inc(S["ex_ready"], 1)
                yield
                yield
                yield
                for i, bk in enumerate((by, bx)):
                    act.wait_ge(S["a1_at"], 2 * s + i + 1)
                    f(atr[:, i].rearrange("p g k -> p (g k)"), bk[:, 0:384], ACT.Copy).then_inc(S["at_ready"], 1)
                    yield
                act.wait_ge(S["g_raw"], s + 1)
                f(sg[:].rearrange("p i k -> p (i k)"), sg[:].rearrange("p i k -> p (i k)"), ACT.Silu)\
                    .then_inc(S["g_ready"], 1)

            def post1(s):
                pa, pb, pc = after_banks(s)
                preload(ACT.Sqrt)
                act.wait_ge(S["ld_s"], 32 * (s + 1))
                place(lambda o, x: f(o, x, ACT.Copy), vx1, (0, 1), S["x_placed"])
                act.wait_ge(S["y_in"], s + 1)
                f(gsq[:].rearrange("p i k -> p (i k)"), pre[:, 2 * s:2 * s + 2, :].rearrange("p i k -> p (i k)"),
                  ACT.Square).then_inc(S["y_sq"], 1)
                act.wait_ge(S["gn_var"], s + 1)
                f(gsum[:], gsum[:], ACT.Sqrt).then_inc(S["gn_std"], 1)
                yield
                act.wait_ge(S["a1_ytr"], s + 1)
                f(ct0[:], pa[:, 0:HT], ACT.Copy).then_inc(S["yt_ready"], 1)
                f(ct1[0:D1, :], pa[0:D1, HT:], ACT.Copy).then_inc(S["yt_ready"], 1)
                yield
                yield

            loads()
            tokens()
            temperature()
            split_w1(0)
            split_w1(1)
            fetch_w1(2)
            first = route(0, 0)
            run(attention0(0), islice(first, 1))
            weave(order_00, a=first, x=experts(0, 0), p=chain(attention0(1), route(0, 1)))
            weave(order_01, x=experts(0, 1), p=pre1(0))
            second = pre1(1)
            first = route(1, 0)
            weave(late_head, a=chain(post1(0), islice(first, 1)), p=islice(second, 3))
            last = route(1, 1)
            weave(order_10, a=first, x=experts(1, 0), p=chain(second, post1(1), islice(last, 1)))
            weave(order_11, a=last, x=experts(1, 1))

        @block.vector
        def _(dve):
            v = nc.vector
            count = [0]

            def link(ins):
                count[0] += 1
                ins.then_inc(S["dve_chain"], 1)
                dve.wait_ge(S["dve_chain"], count[0])

            def flat(ap):
                return ap.rearrange("p a b -> p (a b)")

            def inv_sqrt(name, n):
                q = order.index(name)
                dve.wait_ge(S["rstd_ready"], q + 1)
                return rstd[:, q % 2, 0:n]

            def ask(name, src, scale, eps):
                q = order.index(name)
                n = width.get(name, 2)
                v.tensor_scalar(var_in[:, q % 2, 0:n], src, scale, eps, ALU.mult, ALU.add).then_inc(S["var_ready"], 1)

            def layer_norm(name, s, src, dst, ready=None):
                moments(s, src)
                ask(name, mv[:, 2 * s:2 * s + 2, 1], 1.0, LN_EPS)
                rs = inv_sqrt(name, 2)
                ins = normalize(s, src, dst, rs)
                if ready:
                    ins.then_inc(S[ready], 1)
                    dve.wait_ge(S[ready], s + 1)
                else:
                    link(ins)

            def moments(s, src):
                v.bn_stats(stats[:, 2 * s, :], src[:, 2 * s, :])
                link(v.bn_stats(stats[:, 2 * s + 1, :], src[:, 2 * s + 1, :]))
                v.bn_aggr(mv[:, 2 * s, :], stats[:, 2 * s, :])
                link(v.bn_aggr(mv[:, 2 * s + 1, :], stats[:, 2 * s + 1, :]))

            def normalize(s, src, dst, rs):
                for i in range(2):
                    ins = v.tensor_scalar(dst[:, 2 * s + i, :], src[:, 2 * s + i, :], mv[:, 2 * s + i, 0:1],
                                          rs[:, i:i + 1], ALU.subtract, ALU.mult)
                return ins

            def tokens():
                dve.wait_ge(S["ld_tok"], 16)
                v.tensor_tensor(wtok, wtok, bc(gin, 2, D), ALU.mult).then_inc(S["wtok_scaled"], 1)
                for ch in range(1, PCH):
                    dve.wait_ge(S["xsq_ready"], ch + 1)
                    v.tensor_tensor(xsq[:, 0, :], xsq[:, 0, :], xsq[:, ch, :], ALU.add).then_inc(S["xsum_ready"], 1)
                    dve.wait_ge(S["xsum_ready"], ch)
                dve.wait_ge(S["tok_ss"], 1)
                ask("tok1", bank[4][:, 0:4], 1.0 / PATCH_DIM, RMS_EPS)
                rs = inv_sqrt("tok1", 4)
                dve.wait_ge(S["ld_row"], 16)
                dve.wait_ge(S["tok_y"], 1)
                for t in range(TILES):
                    v.scalar_tensor_tensor(h0[:, t, :], bank[t][:, 0:D], rs[:, t:t + 1],
                                           r("b_proj"), ALU.mult, ALU.add).then_inc(S["y_ready"], 1)
                dve.wait_ge(S["ld_att0"], 48)
                dve.wait_ge(S["lora_mm"], 1)
                for j in range(3):
                    v.scalar_tensor_tensor(wn[:, 0, j, 0:D], bank[5 + j][:, 0:D], 0.5, wn[:, 0, j, 0:D],
                                           ALU.mult, ALU.add)
                    ins = v.scalar_tensor_tensor(wn[0:D1, 1, j, 0:D], bank[5 + j][0:D1, D:2 * D], 0.5,
                                                 wn[0:D1, 1, j, 0:D], ALU.mult, ALU.add)
                ins.then_inc(S["wn_ready"], 1)
                dve.wait_ge(S["y_sq2"], TILES)
                ask("tok2", ss[:, 1, :], 1.0 / D, RMS_EPS)
                rs = inv_sqrt("tok2", 4)
                for t in range(TILES):
                    ins = v.scalar_tensor_tensor(h0[:, t, :], h0[:, t, :], rs[:, t:t + 1], r("g_out"),
                                                 ALU.mult, ALU.mult)
                    if t % 2:
                        ins.then_inc(S["h0_ready"], 1)

            def composites():
                dve.wait_ge(S["ld_const"], 16)
                dve.wait_ge(S["ld_row"], 16)
                link(v.tensor_reduce(wgsum[:].rearrange("p c a -> p (c a)"), wg.rearrange("p c a b -> p (c a) b"),
                                     AX.X, ALU.add))
                link(v.tensor_reduce(bgs[:], r("bg").rearrange("p (a b) -> p a b", a=2), AX.X, ALU.add))
                for ch in range(2):
                    link(v.tensor_tensor(wgx[:, ch], bc(wgsum[:, ch, :], 1, HEADS),
                                         bc(c("head12")[:, ch * HEADS:(ch + 1) * HEADS], 2, 2), ALU.mult))
                link(v.tensor_scalar(temp[:, 1, :], r("lucid"), -1.0, None, ALU.mult))
                v.tensor_tensor(temp[:, 0, :], r("lucid"), temp[:, 1, :], ALU.max).then_inc(S["temp_in"], 1)
                for j in range(3):
                    dve.wait_ge(S["comp_mm"], j + 1)
                    sc = HD ** -0.5 if j == 0 else 1.0
                    link(v.tensor_scalar(cw0[:, j, :], bank[5 + j][:, 0:D], sc, None, ALU.mult))
                    link(v.tensor_scalar(cw1[0:D1 + 1, j, :], bank[5 + j][0:D1 + 1, D:2 * D], sc, None, ALU.mult))
                    link(v.scalar_tensor_tensor(cw1[D1:D1 + 1, j, :], b64[D1:D1 + 1, j, :], sc, cw1[D1:D1 + 1, j, :],
                                                ALU.mult, ALU.add))
                dve.wait_ge(S["posb_mm"], 1)
                v.tensor_copy(posb[:], bank[0][:, 0:T * HEADS].rearrange("p (k h) -> p k h", h=HEADS))\
                    .then_inc(S["comp_ready"], 1)
                dve.wait_ge(S["comp_ready"], 1)
                dve.wait_ge(S["temp_out"], 1)
                link(v.scalar_tensor_tensor(temp[:, 0, :], r("lucid"), 0.0, temp[:, 2, :], ALU.max, ALU.add))

            def attention0(s):
                dve.wait_ge(S["a0_gate"], s + 1)
                gr = gates0.rearrange("p i h a -> p (i h) a")
                v.tensor_tensor(gr, br[:, 0:48].rearrange("p (n a) -> p n a", a=2), bc(bgs[:], 1, 24),
                                ALU.add).then_inc(S["gate_in"], 1)
                dve.wait_ge(S["a0_k"], s + 1)
                for i in range(2):
                    expand_on(v, i, blocks(bz[:, 0:HT], i), blocks(bz[0:D1, HT:], i)).then_inc(S["kx_ready"], 1)
                dve.wait_ge(S["gate_exp"], s + 1)
                g = flat(gr)
                link(v.tensor_scalar(g, g, 1.0, None, ALU.add))
                link(v.reciprocal(g, g))
                ga, gb = gates0[:, :, :, 0], gates0[:, :, :, 1]
                link(v.tensor_tensor(gb, gb, bc(r("gru"), 1, 2), ALU.mult))
                link(v.scalar_tensor_tensor(gate[:], gb, -1.0, ga, ALU.add, ALU.mult))
                link(v.tensor_scalar(gate[:], gate[:], 2.0, None, ALU.add))
                for i in range(2):
                    link(v.tensor_tensor(gbias[:, i], bc(gate[:, i, :], 2, T), posb[:].rearrange("p k h -> p h k"),
                                         ALU.mult))
                    link(v.tensor_tensor(prob[:, i].rearrange("p h (b k) -> p h b k", b=2), bc(gbias[:, i], 2, 2),
                                         bc(c("off_pair").rearrange("p (b k) -> p b k", b=2), 1, HEADS), ALU.add))
                for i in range(2):
                    p = prob[:, i]
                    dve.wait_ge(S["a0_s"], 2 * s + i + 1)
                    link(v.tensor_tensor(p, (by, bz)[i][:, 0:384].rearrange("p (h k) -> p h k", h=HEADS), p, ALU.add))
                    link(v.tensor_reduce(smax[:, i], p, AX.X, ALU.max))
                    v.tensor_tensor(p, p, bc(smax[:, i], 2, 32), ALU.subtract).then_inc(S["s_shift"], 1)
                dve.wait_ge(S["v_out"], s + 1)
                dve.wait_ge(S["vx_zero"], 1)
                place(v.tensor_copy, vx, (2, 3), S["v_placed"])
                for i in range(2):
                    p = prob[:, i]
                    dve.wait_ge(S["s_exp"], 2 * s + i + 1)
                    link(v.tensor_reduce(smax[:, i], p, AX.X, ALU.add))
                    link(v.reciprocal(smax[:, i], smax[:, i]))
                    v.tensor_tensor(p, p, bc(smax[:, i], 2, 32), ALU.mult).then_inc(S["p_ready"], 1)
                dve.wait_ge(S["a0_wo"], s + 1)
                a = slice(2 * s, 2 * s + 2)
                v.tensor_tensor(pre[:, a, :], bx[:, 0:2 * D].rearrange("p (i k) -> p i k", i=2), h0[:, a, :],
                                ALU.add).then_inc(S["wo_read"], 1)
                dve.wait_ge(S["wo_read"], s + 1)
                moments(s, pre)
                var = mv[:, a, 1]
                ask(f"a0_{s}", var, 1.0, LN_EPS)
                rs = inv_sqrt(f"a0_{s}", 2)
                link(v.tensor_tensor(var, var, rs, ALU.mult))
                link(v.tensor_tensor(var, var, rs, ALU.mult))
                ask(f"f0_{s}", var, 1.0, LN_EPS)
                link(normalize(s, pre, h1, rs))
                rs = inv_sqrt(f"f0_{s}", 2)
                for i in range(2):
                    ins = v.scalar_tensor_tensor(xffn[:, 2 * s + i, :], h1[:, 2 * s + i, :], rs[:, i:i + 1],
                                                 r("ln_gamma"), ALU.mult, ALU.mult)
                link(ins)
                v.tensor_tensor(xffn[:, a, :], xffn[:, a, :], bc(r("ln_beta"), 1, 2), ALU.add)\
                    .then_inc(S["x_ready"], 1)

            def route(l, s):
                n = 2 * l + s
                dve.wait_ge(S["x_hi_ready"], n + 1)
                v.tensor_tensor(x_lo[:, s, :], f0[1][:, s, :], x_hi[:, s, :].bitcast(F32), ALU.subtract)
                v.tensor_tensor(x_tail[D1:128, s, :], f1[1][D1:128, s, :], x_tail[D1:128, s, :].bitcast(F32),
                                ALU.subtract).then_inc(S["x_lo_ready"], 1)
                yield
                dve.wait_ge(S["ff_lg"], n + 1)
                src = br[:, 0:2 * NEXP].rearrange("p (i k) -> p i k", i=2)
                if l == 0:
                    link(v.tensor_copy(lg[:], src))
                else:
                    link(v.tensor_tensor(lg[:], src, bc(r("gate_b"), 1, 2), ALU.add))
                for i in range(2):
                    link(v.max(top[:, i, :], lg[:, i, :]))
                    link(v.max_index(topi[:, i, :], top[:, i, :], lg[:, i, :]))
                v.tensor_tensor(topd[:, :, 0:1], top[:, :, 1:2], top[:, :, 0:1], ALU.subtract).then_inc(S["top_in"], 1)
                yield
                link(v.tensor_copy(topf[:], topi[:, :, 0:2]))
                dve.wait_ge(S["top_exp"], n + 1)
                link(v.tensor_scalar(topd[:, :, 2:3], topd[:, :, 1:2], 1.0, None, ALU.add))
                link(v.reciprocal(topd[:, :, 2:3], topd[:, :, 2:3]))
                link(v.tensor_tensor(topd[:, :, 1:2], topd[:, :, 1:2], topd[:, :, 2:3], ALU.mult))
                for k in range(2):
                    link(v.tensor_tensor(hot[:, k], bc(c("iota8"), 1, 2), topf[:, :, k:k + 1].broadcast_to([128, 2, NEXP]),
                                         ALU.is_equal))
                    link(v.tensor_tensor(hot[:, k], hot[:, k],
                                         topd[:, :, 2 - k:3 - k].broadcast_to([128, 2, NEXP]), ALU.mult))
                a = slice(2 * s, 2 * s + 2)
                v.tensor_tensor(gts[:, a, :], hot[:, 0], hot[:, 1], ALU.add).then_inc(S["gts_ready"], 1)
                if l == 0:
                    v.tensor_scalar(acc[:, a, :], h1[:, a, :], 2.0, None, ALU.mult).then_inc(S["acc_init"], 1)
                else:
                    yield
                    dve.wait_ge(S["b2_mm"], s + 1)
                    v.tensor_tensor(acc[:, a, :], br[:, 0:2 * D].rearrange("p (i k) -> p i k", i=2), h3[:, a, :],
                                    ALU.add).then_inc(S["acc_init"], 1)

            def pre1(s):
                fa, fb = f0[2][:, s, :], f1[2][0:D1, s, :]
                dve.wait_ge(S["ld_att1"], 16)
                dve.wait_ge(S["a1_ft"], 4 * (s + 1))
                v.scalar_tensor_tensor(xx0[:], dx0[:], maa[:, 0, 0:1], fa, ALU.mult, ALU.add)
                v.scalar_tensor_tensor(xx1[:], dx1[:], maa[0:D1, 1, 0:1], fb, ALU.mult, ALU.add)\
                    .then_inc(S["a1_xx"], 1)
                yield
                for n, m in enumerate(MIX_ORDER):
                    dve.wait_ge(S["a1_mm"], MIX * s + n + 1)
                    bk = (bx, by, bz)[n % 3]
                    v.scalar_tensor_tensor(xc0[:, m, :], bk[:, 0:HT], maa[:, 0, 1 + m:2 + m], dx0, ALU.add, ALU.mult)
                    v.scalar_tensor_tensor(xc1[:, m, :], bk[0:D1, HT:], maa[0:D1, 1, 1 + m:2 + m], dx1,
                                           ALU.add, ALU.mult).then_inc(S["a1_xd"], 1)
                    if n == 0:
                        dve.wait_ge(S["a1_xd"], MIX * s + 1)
                        v.tensor_tensor(xc0[:, m, :], xc0[:, m, :], fa, ALU.add)
                        v.tensor_tensor(xc1[:, m, :], xc1[:, m, :], fb, ALU.add).then_inc(S["xc_ready"], 1)
                    if n in (1, 4):
                        yield
                dve.wait_ge(S["n2_ready"], s + 1)
                for kn, kt in ((kn0, kt0), (kn1, kt1)):
                    link(v.tensor_scalar(kn, kn, 1e-12, None, ALU.max))
                    link(v.reciprocal(kn, kn))
                    ins = v.tensor_tensor(kn, kn, kt, ALU.mult)
                    if kn is kn0:
                        link(ins)
                ins.then_inc(S["kn_in"], 1)
                dve.wait_ge(S["kn_in"], s + 1)
                expand_on(v, 0, blocks(kn0, 0), blocks(kn1, 0)).then_inc(S["kn_ready"], 1)
                yield
                dve.wait_ge(S["a1_g"], s + 1)
                v.tensor_copy(flat(sg), bx[:, 0:2 * D]).then_inc(S["g_raw"], 1)
                yield
                for i, bk in enumerate((bz, bx)):
                    dve.wait_ge(S["a1_gram"], 2 * s + i + 1)
                    link(v.tensor_tensor(gram[s][i], bk[:, 0:384].rearrange("p (h k) -> p h k", h=HEADS),
                                         bc(temp[:, 0, :], 2, 32), ALU.mult))
                    v.tensor_scalar(gram[s][i], gram[s][i], -20.0, 20.0, ALU.max, ALU.min).then_inc(S["gram_in"], 1)
                yield
                for i in range(2):
                    dve.wait_ge(S["gram_exp"], 2 * s + i + 1)
                    link(v.scalar_tensor_tensor(pmat[:, i], gram[s][i][:, :, 0:T], c("even"),
                                                bc(c("eye16"), 1, HEADS), ALU.mult, ALU.add))
                    v.scalar_tensor_tensor(pmat[:, i], gram[s][i][:, :, T:], c("odd"), pmat[:, i],
                                           ALU.mult, ALU.add).then_inc(S["p_mat"], 1)
                yield
                dve.wait_ge(S["a1_cs"], s + 1)
                v.tensor_scalar(cs0.rearrange("p i d k -> p (i d k)"), by[:], -60.0, 60.0, ALU.max, ALU.min)
                v.tensor_scalar(cs1.rearrange("p i d k -> p (i d k)"), bz[0:D1, :], -60.0, 60.0,
                                ALU.max, ALU.min).then_inc(S["cs_ready"], 1)
                yield
                dve.wait_ge(S["ex_ready"], s + 1)
                dve.wait_ge(S["rk_ready"], s + 1)
                for ex, rt, kt in ((ex0, rt0, kt0), (ex1, rt1, kt1)):
                    for m, op in enumerate((rt, kt)):
                        kinds = ex[:, 2 * m:2 * m + 2].rearrange("p a i k -> p a (i k)")
                        ins = v.tensor_tensor(kinds, kinds, bc(op, 1, 2), ALU.mult)
                ins.then_inc(S["dk_in"], 1)
                dve.wait_ge(S["dk_in"], s + 1)
                yield
                for i, banks in enumerate(((bx, by), (bz, bx))):
                    dve.wait_ge(S["a1_ab"], 2 * s + i + 1)
                    for mask, bk in zip(("lower", "upper"), banks):
                        ins = v.copy_predicated(amix[:, i], bc(c(mask), 1, HEADS).bitcast(I32),
                                                bk[:, 0:384].rearrange("p (h k) -> p h k", h=HEADS))
                        if mask == "lower":
                            link(ins)
                    ins.then_inc(S["a_mix"], 1)
                    yield

            def solve(s):
                dve.wait_ge(S["ld_g"], 32 * (s + 1))
                W = T + HD
                for k in range(T):
                    link(v.reciprocal(piv[:], sysm[:, :, k, k]))
                    link(v.tensor_tensor(sysm[:, :, k, k + 1:W], sysm[:, :, k, k + 1:W], bc(piv[:], 2, W - k - 1),
                                         ALU.mult))
                    if k == T - 1:
                        break
                    pr = prod[:, :, k + 1:T, k + 1:W]
                    link(v.tensor_tensor(pr, bc(sysm[:, :, k + 1:T, k], 3, W - k - 1),
                                         bc(sysm[:, :, k, k + 1:W], 2, T - k - 1), ALU.mult))
                    link(v.tensor_tensor(sysm[:, :, k + 1:T, k + 1:W], sysm[:, :, k + 1:T, k + 1:W], pr, ALU.subtract))
                    yield
                for k in range(T - 1, 0, -1):
                    pr = prod[:, :, 0:k, T:W]
                    link(v.tensor_tensor(pr, bc(sysm[:, :, 0:k, k], 3, HD), bc(sysm[:, :, k, T:W], 2, k), ALU.mult))
                    ins = v.tensor_tensor(sysm[:, :, 0:k, T:W], sysm[:, :, 0:k, T:W], pr, ALU.subtract)
                    if k > 1:
                        link(ins)
                        yield
                ins.then_inc(S["solved"], 1)

            def experts_done(name, n, s, dst, ready):
                dve.wait_ge(S["acc_add"], NEXP * (n + 1))
                layer_norm(name, s, acc, dst, ready)

            def post1(s):
                a = slice(2 * s, 2 * s + 2)
                pa, pb, pc = after_banks(s)
                dve.wait_ge(S["ld_s"], 32 * (s + 1))
                place(v.tensor_copy, vx1, (2, 3), S["x_placed"])
                dve.wait_ge(S["a1_y"], s + 1)
                y = pc[:, 0:2 * D].rearrange("p (n k) -> p n k", k=HD)
                yc = pre[:, a, :].rearrange("p i (h k) -> p (i h) k", k=HD)
                link(v.tensor_reduce(gsum[:], y, AX.X, ALU.add))
                v.scalar_tensor_tensor(yc, bc(gsum[:], 2, HD), -1.0 / HD, y, ALU.mult, ALU.add).then_inc(S["y_in"], 1)
                yield
                dve.wait_ge(S["y_sq"], s + 1)
                link(v.tensor_reduce(gsum[:], gsq[:].rearrange("p i (h k) -> p (i h) k", k=HD), AX.X, ALU.add))
                v.tensor_scalar(gsum[:], gsum[:], 1.0 / HD, GN_EPS, ALU.mult, ALU.add).then_inc(S["gn_var"], 1)
                dve.wait_ge(S["gn_std"], s + 1)
                link(v.reciprocal(gsum[:], gsum[:]))
                link(v.tensor_tensor(yc, yc, bc(gsum[:], 2, HD), ALU.mult))
                link(v.tensor_tensor(pre[:, a, :], pre[:, a, :], bc(r("ln_w"), 1, 2), ALU.mult))
                link(v.tensor_tensor(pre[:, a, :], pre[:, a, :], bc(r("ln_b"), 1, 2), ALU.add))
                dve.wait_ge(S["g_ready"], s + 1)
                v.tensor_tensor(gsq[:], pre[:, a, :], sg[:], ALU.mult).then_inc(S["gn_ready"], 1)
                yield
                dve.wait_ge(S["a1_wo"], s + 1)
                v.tensor_tensor(pre[:, a, :], pc[:, 0:2 * D].rearrange("p (i k) -> p i k", i=2), h2[:, a, :],
                                ALU.add).then_inc(S["wo1_read"], 1)
                dve.wait_ge(S["wo1_read"], s + 1)
                layer_norm(f"h3_{s}", s, pre, h3, "h3_ready")
                yield

            v.memset(f1[0][D1:D1 + 1, :, :], 1.0).then_inc(S["ones_set"], 1)
            v.memset(ct1[D1:D1 + 1, :], 1.0).then_inc(S["ones_set"], 1)
            tokens()
            composites()
            attention0(0)
            run(route(0, 0))
            attention0(1)
            run(route(0, 1))
            experts_done("h2_0", 0, 0, h2, "h2_ready")
            dve.wait_ge(S["amix_zero"], 1)
            v.memset(t1[64:65, :], 1.0).then_inc(S["t1_ones"], 1)
            weave(vector_0, p=pre1(0), s=solve(0))
            experts_done("h2_1", 1, 1, h2, "h2_ready")
            weave(vector_1, a=chain(post1(0), route(1, 0)), p=pre1(1), s=solve(1))
            last = route(1, 1)
            run(post1(1), islice(last, 1))
            experts_done("out_0", 2, 0, pre, "out_ready")
            run(last)
            experts_done("out_1", 3, 1, pre, "out_ready")

        @block.gpsimd
        def _(pool):
            g = nc.gpsimd

            def power(name):
                q, n = order.index(name), width.get(name, 2)
                pool.wait_ge(S["var_ready"], q + 1)
                g.tensor_tensor(rstd[:, q % 2, 0:n], var_in[:, q % 2, 0:n], c("neghalf").broadcast_to([128, n]),
                                ALU.pow).then_inc(S["rstd_ready"], 1)

            def low_w1(m):
                if m < len(uses):
                    pool.wait_ge(S["w1_hi_ready"], m + 1)
                    w = w1[:, m % RING, :]
                    g.tensor_tensor(w1_lo[:, m % RING, :], w, w1_hi[:, m % RING, :].bitcast(F32), ALU.subtract)\
                        .then_inc(S["w1_lo_ready"], 1)

            def add_experts(l, s, first=0, end=NEXP + 1):
                a = slice(2 * s, 2 * s + 2)
                for e in range(first, end):
                    m = (2 * l + s) * NEXP + e
                    if e < NEXP:
                        low_w1(m + RING)
                    if e == 0:
                        continue
                    pool.wait_ge(S["y_act"], m)
                    if e == 1:
                        pool.wait_ge(S["acc_init"], 2 * l + s + 1)
                    else:
                        pool.wait_ge(S["acc_add"], m - 1)
                    g.tensor_tensor(acc[:, a, :], acc[:, a, :], ysc[:, (m - 1) % 2], ALU.add).then_inc(S["acc_add"], 1)

            def expand_keys(s):
                pool.wait_ge(S["kn_in"], s + 1)
                expand_on(g, 1, blocks(kn0, 1), blocks(kn1, 1)).then_inc(S["kn1_ready"], 1)

            def expand_decayed(s, i):
                pool.wait_ge(S["dk_in"], s + 1)
                if i:
                    pool.wait_ge(S["a1_gram"], 2 * s + 2)
                for m in range(2):
                    ins = expand_on(g, (2 + 2 * i + m) % 4, ex0[:, 2 + m, i].rearrange("p (b k) -> p b k", b=4),
                                    ex1[:, 2 + m, i].rearrange("p (b k) -> p b k", b=4))
                ins.then_inc(S["dk1_ready" if i else "dk_ready"], 1)

            def mixes(s, first=1, end=MIX):
                for n, m in list(enumerate(MIX_ORDER))[first:end]:
                    pool.wait_ge(S["a1_xd"], MIX * s + n + 1)
                    g.tensor_tensor(xc0[:, m, :], xc0[:, m, :], f0[2][:, s, :], ALU.add)
                    g.tensor_tensor(xc1[:, m, :], xc1[:, m, :], f1[2][0:D1, s, :], ALU.add).then_inc(S["xc_ready"], 1)

            g.memset(amix[:], 0.0).then_inc(S["amix_zero"], 1)
            g.memset(vx1[:], 0.0).then_inc(S["vx_zero"], 1)
            pool.wait_ge(S["ld_const"], 16)
            power("tok1")
            power("tok2")
            low_w1(0)
            low_w1(1)
            power("a0_0")
            power("f0_0")
            n = rounds_before(order_00, 9)
            add_experts(0, 0, end=n)
            power("a0_1")
            power("f0_1")
            add_experts(0, 0, first=n)
            power("h2_0")
            mixes(0)
            n = [0, rounds_before(order_01, 8), rounds_before(order_01, 9), rounds_before(order_01, 9)]
            add_experts(0, 1, end=n[1])
            expand_keys(0)
            add_experts(0, 1, first=n[1], end=n[2])
            expand_decayed(0, 0)
            add_experts(0, 1, first=n[2], end=n[3])
            expand_decayed(0, 1)
            add_experts(0, 1, first=n[3])
            power("h2_1")
            power("h3_0")
            mixes(1)
            n = [0, rounds_before(order_10, 4), rounds_before(order_10, 8), rounds_before(order_10, 8)]
            add_experts(1, 0, end=n[1])
            expand_keys(1)
            add_experts(1, 0, first=n[1], end=n[2])
            expand_decayed(1, 0)
            add_experts(1, 0, first=n[2], end=n[3])
            expand_decayed(1, 1)
            ahead = rounds_before(order_10, 13)
            add_experts(1, 0, first=n[3], end=ahead)
            power("h3_1")
            add_experts(1, 0, first=ahead)
            power("out_0")
            add_experts(1, 1)
            power("out_1")


def _constants():
    p = np.arange(128)
    img = p // T
    same = img[:, None] == img[None, :]
    a, b = p[:, None], p[None, :]
    shift = np.where(same, 0.5 * (np.abs(a - b) == 1) - 1.0 * (a == b), 0.0)
    mid = (b // T) * T + T // 2
    cf = np.where(same, 1.0 * (a <= b) - 1.0 * (a <= mid), 0.0)
    cb = np.where(same, 1.0 * (a < b) - 1.0 * (a < mid), 0.0)
    k = np.arange(32)
    own = (p[:, None] % 32) // T == k[None, :] // T
    key, tok = k[None, :] % T, p[:, None] % T
    head24 = np.concatenate([p[:, None] // HD == np.arange(HEADS)[None, :],
                             8 + p[:, None] // HD == np.arange(HEADS)[None, :]], 1)
    anti = a == T - 1 - b % T
    parts = {
        "ident": np.eye(128), "shift": shift, "cums": -np.concatenate([cf, cb], 1), "headsum": same,
        "head8": p[:, None] // HD == np.arange(8)[None, :], 
        "head12": head24, "off_pair": np.where(own, 0.0, MASKED), "even": (img % 2 == 0)[:, None],
        "odd": (img % 2 == 1)[:, None], "lower": own & (key <= tok), "upper": own & (key > tok),
        "anti16": anti, "iota8": np.tile(np.arange(8), (128, 1)), "one": np.ones((128, 1)),
        "neghalf": np.full((128, 1), -0.5), "eye16": tok == np.arange(T)[None, :]}
    return np.ascontiguousarray(np.concatenate([np.asarray(parts[n], np.float32) for n in CONST], 1))


def _chunks(a, extra=None):
    out = np.zeros((128, 2) + a.shape[1:], np.float32)
    out[:, 0] = a[:128]
    out[:D1, 1] = a[128:]
    if extra is not None:
        out[D1, 1] = extra
    return out


def _pack(table, parts):
    cols = []
    for name in table:
        a = np.asarray(parts[name], np.float32)
        a = a.reshape(a.shape[0], -1)
        cols.append(np.concatenate([a, np.zeros((128 - a.shape[0], a.shape[1]), np.float32)], 0))
    return np.ascontiguousarray(np.concatenate(cols, 1))


def _first_weights(w1):
    return np.ascontiguousarray(np.concatenate([w1[:, :128], np.concatenate([w1[:, 128:]] * 2, 1)], 2))


def _second_weights(w2):
    return np.ascontiguousarray(w2.reshape(NEXP, FCH, 128, D).transpose(0, 2, 1, 3).reshape(NEXP, 128, -1))



def kernel(**inputs):
    import concourse.bacc as _bacc
    from concourse.bass_utils import run_bass_kernel_spmd as _run

    x = {k: np.asarray(a) for k, a in inputs.items()}
    a0 = {k[8:]: v for k, v in x.items() if k.startswith("L0_attn_")}
    a1 = {k[8:]: v for k, v in x.items() if k.startswith("L1_attn_")}
    xt = x["x"].reshape(BATCH, 3, 4, 16, 4, 16).transpose(3, 5, 1, 0, 2, 4).reshape(PCH, 128, TOK)
    xt = np.ascontiguousarray(xt.transpose(1, 0, 2).reshape(128, PCH * TOK))
    tokp = _pack(TOKP, {"w": x["L0_tok_W_proj"].T.reshape(PCH, 128, D).transpose(1, 0, 2),
                        "gin": x["L0_tok_g_in"].reshape(PCH, 128).T})
    rows = np.concatenate([x["L0_tok_b_proj"], x["L0_tok_g_out"], x["L0_ffn_ln_gamma"], x["L0_ffn_ln_beta"],
                           a1["ln_w"], a1["ln_b"], a0["gru_const"].reshape(-1), a1["lucid_temp"].reshape(-1),
                           x["L1_ffn_gate_b"], a0["bg"]])
    qkv = [(a0["Wq"], a0["bq"], a0["Aq"], a0["Bq"]), (a0["Wk"], a0["bk"], a0["Ak"], a0["Bk"]),
           (a0["Wv"], a0["bv"], a0["Av"], a0["Bv"])]
    rel = a0["rel_embed"]
    att0 = _pack(ATT0, {
        "wn": _chunks(np.stack([np.concatenate([w, b[:, None]], 1) for w, b, _, _ in qkv], 1)),
        "wt": _chunks(np.stack([w.T for w, _, _, _ in qkv], 1)),
        "wo": _chunks(a0["Wo"].T, a0["bo"]),
        "wg": _chunks(np.tile(a0["Wg"].T, (HEADS, 1))),
        "rel": np.stack([np.concatenate([rel[15::-1], rel[41:56]], 0)[k:k + T] for k in range(T)], 1)})
    lora = np.stack([np.stack([b.T, a], 1) for _, _, a, b in qkv], 1).reshape(2, -1)
    maa = np.stack([a1[f"time_maa_{n}"].reshape(-1) for n in "xwkvrg"], 1)
    maa_w2 = np.zeros((128, 2, D), np.float32)
    maa_w2[:, 0] = a1["maa_w2"][:4].reshape(128, D)
    maa_w2[:32, 1] = a1["maa_w2"][4]
    att1 = _pack(ATT1, {
        "maa_w1": _chunks(a1["maa_w1"]), "maa_w2": maa_w2, "maa": _chunks(maa),
        "w4": _chunks(np.stack([a1["Wr"], a1["Wk"], a1["Wv"], a1["Wg"]], 1)),
        "dw1": _chunks(a1["decay_w1"]),
        "dw2": np.concatenate([a1["decay_w2"], a1["time_decay"].reshape(1, D)], 0),
        "wo": _chunks(a1["Wo"]), "router": _chunks(x["L0_ffn_router_w"]), "gate": _chunks(x["L1_ffn_gate_w"]),
        "b1": x["L1_ffn_b1"].reshape(NEXP * FCH, 128).T, "b2": x["L1_ffn_b2"]})
    arrays = {"consts": _constants(), "rows": np.ascontiguousarray(rows), "x_t": xt,
              "tok_pack": tokp, "att0_pack": att0, "lora_pack": np.ascontiguousarray(lora),
              "bias_pack": np.stack([b for _, b, _, _ in qkv])[None], "att1_pack": att1,
              "w1_l0": _first_weights(x["L0_ffn_w1"]), "w2_l0": _second_weights(x["L0_ffn_w2"]),
              "w1_l1": _first_weights(x["L1_ffn_w1"]), "w2_l1": _second_weights(x["L1_ffn_w2"])}

    nc = _bacc.Bacc("TRN2", target_bir_lowering=False, num_devices=1)
    args = [nc.dram_tensor(n, a.shape, F32, kind="ExternalInput").ap() for n, a in arrays.items()]
    scratch = [nc.dram_tensor("p_scratch", (TILES, HEADS, 128, T + HD), F32, kind="Internal").ap(),
               nc.dram_tensor("s_scratch", (TILES, HEADS, 128, HD), F32, kind="Internal").ap()]
    out = nc.dram_tensor("out", (TILES, 128, D), F32, kind="ExternalOutput").ap()
    vit_tower_kernel(nc, *args, *scratch, out)
    got = _run(nc, [arrays], core_ids=[0]).results[0]["out"]
    return np.asarray(got).reshape(BATCH, T, D)
```
